# Optimizing a Trainium2 kernel written in Bass

```python
import numpy as np
import jax
import jax.numpy as jnp

def _softmax(x, axis=-1):
    return jax.nn.softmax(x, axis=axis)

def _gelu(x):
    return jax.nn.gelu(x, approximate=True)

def _silu(x):
    return jax.nn.silu(x)

def _sigmoid(x):
    return jax.nn.sigmoid(x)

def _layernorm(x, axis=-1, eps=1e-05):
    m = jnp.mean(x, axis=axis, keepdims=True)
    v = jnp.var(x, axis=axis, keepdims=True)
    return (x - m) / jnp.sqrt(v + eps)

def _scatter_add(tgt, idx, src, axis=0):
    return tgt.at[idx].add(src)

def _segment_sum(src, seg, n):
    return jax.ops.segment_sum(src, seg, n)
kernel_name = 'mk_flamingo_gated_d2_seqx_r4_e8c735'

def setup_inputs(seed: int=0):
    np.random.seed(seed)
    _w = jnp.asarray

    def _rec_inputs():
        import jax
        import jax.numpy as jnp
        _rk = jax.random.key(seed)
        x = 7.22e-05 + 1 * jax.random.normal(jax.random.fold_in(_rk, 1), (8, 256, 256), jnp.float32)
        _lenS = 256 - jax.random.randint(jax.random.fold_in(_rk, 7), (8,), 0, max(1, 256 // 4) + 1, jnp.int32)
        _lenS2 = 256 - jax.random.randint(jax.random.fold_in(_rk, 8), (8,), 0, max(1, 256 // 4) + 1, jnp.int32)
        _ctx_1024P = jax.random.normal(jax.random.fold_in(_rk, 11), (8, 16, 256), jnp.float32)
        _ctx_1024c = jax.random.dirichlet(jax.random.fold_in(_rk, 511), 0.3 * jnp.ones((16,), jnp.float32), (8, 256))
        _ctx_1024t = jnp.einsum('bsk,bkd->bsd', _ctx_1024c, _ctx_1024P)
        _ctx_1024t = _ctx_1024t * jax.lax.rsqrt(jnp.mean(jnp.square(_ctx_1024t)) + 1e-12) * 0.953939
        ctx_1024 = 4.13588e-05 + 0.999923 * (_ctx_1024t + 0.3 * jax.random.normal(jax.random.fold_in(_rk, 611), (8, 256, 256), jnp.float32))
        _g = jax.random.normal(jax.random.fold_in(_rk, 9001), (2, 2), jnp.float32)
        _g = jnp.sign(_g) * jnp.maximum(jnp.abs(_g), 1.0) + (_g == 0) * 1.0
        g_xattn = _g[0]
        g_ffn = _g[1]
        return (x, ctx_1024, g_xattn, g_ffn)
    x, ctx_1024, g_xattn, g_ffn = _rec_inputs()

    def _L0_xattn_setup():
        import jax, jax.numpy as jnp
        import numpy as np
        H = 16
        D_MODEL = 256
        D_K = D_MODEL // H
        key = jax.random.key(seed)
        ks = jax.random.split(key, 12)
        B, S = (4, 512)
        scale = 1.0 / np.sqrt(D_MODEL)
        inp = {'query': jax.random.normal(ks[0], (B, S, D_MODEL), dtype=jnp.float32), 'key': jax.random.normal(ks[1], (B, S, D_MODEL), dtype=jnp.float32), 'value': jax.random.normal(ks[2], (B, S, D_MODEL), dtype=jnp.float32), 'Wq': jax.random.normal(ks[3], (D_MODEL, D_MODEL), dtype=jnp.float32) * scale, 'bq': jnp.zeros((D_MODEL,), dtype=jnp.float32), 'Wk': jax.random.normal(ks[4], (D_MODEL, D_MODEL), dtype=jnp.float32) * scale, 'bk': jnp.zeros((D_MODEL,), dtype=jnp.float32), 'Wv': jax.random.normal(ks[5], (D_MODEL, D_MODEL), dtype=jnp.float32) * scale, 'bv': jnp.zeros((D_MODEL,), dtype=jnp.float32), 'Wo': jax.random.normal(ks[6], (D_MODEL, D_MODEL), dtype=jnp.float32) * scale, 'bo': jnp.zeros((D_MODEL,), dtype=jnp.float32)}
        return inp
    _L0_xattn_all = _L0_xattn_setup()
    _L0_xattn_in = {k: v for k, v in _L0_xattn_all.items() if k in ('Wq', 'bq', 'Wk', 'bk', 'Wv', 'bv', 'Wo', 'bo')}
    del _L0_xattn_all

    def _L0_ffn_setup():
        import jax, jax.numpy as jnp
        import numpy as np
        from jax import lax
        T, B, I, M, O = (64, 64, 256, 256, 256)

        def _xavier(key, shape):
            fan_out, fan_in = shape
            limit = float(np.sqrt(6.0 / (fan_in + fan_out)))
            return jax.random.uniform(key, shape, jnp.float32, -limit, limit)
        key = jax.random.key(seed)
        ks = jax.random.split(key, 9)
        x = jax.random.normal(ks[0], (T, B, I), jnp.float32)
        return {'x': x, 'wf': _xavier(ks[1], (M, I)), 'uf': _xavier(ks[2], (M, M)), 'bf': jnp.zeros((M,), jnp.float32), 'wi': _xavier(ks[3], (M, I)), 'ui': _xavier(ks[4], (M, M)), 'bi': jnp.zeros((M,), jnp.float32), 'wc': _xavier(ks[5], (M, I)), 'uc': _xavier(ks[6], (M, M)), 'bc': jnp.zeros((M,), jnp.float32), 'wo': _xavier(ks[7], (O, I)), 'uo': _xavier(ks[8], (O, M)), 'bo': jnp.zeros((O,), jnp.float32), 'in_c': jnp.zeros((M,), jnp.float32)}
    _L0_ffn_all = _L0_ffn_setup()
    _L0_ffn_in = {k: v for k, v in _L0_ffn_all.items() if k in ('wf', 'uf', 'bf', 'wi', 'ui', 'bi', 'wc', 'uc', 'bc', 'wo', 'uo', 'bo', 'in_c')}
    del _L0_ffn_all

    def _L1_xattn_setup():
        import jax, jax.numpy as jnp
        import numpy as np
        HEADS = 16
        D_MODEL = 256
        D_HEAD = D_MODEL // HEADS

        def _split_heads(x):
            B, S, _ = x.shape
            return x.reshape(B, S, HEADS, D_HEAD).transpose(0, 2, 1, 3)
        key = jax.random.key(seed)
        ks = jax.random.split(key, 11)
        B, S = (2, 512)
        scale = 1.0 / np.sqrt(D_MODEL)
        inp = {'key': jax.random.normal(ks[0], (B, S, D_MODEL), jnp.float32), 'value': jax.random.normal(ks[1], (B, S, D_MODEL), jnp.float32), 'query': jax.random.normal(ks[2], (B, S, D_MODEL), jnp.float32), 'Wk': jax.random.normal(ks[3], (D_MODEL, D_MODEL), jnp.float32) * scale, 'bk': jnp.zeros((D_MODEL,), jnp.float32), 'Wv': jax.random.normal(ks[4], (D_MODEL, D_MODEL), jnp.float32) * scale, 'bv': jnp.zeros((D_MODEL,), jnp.float32), 'Wq': jax.random.normal(ks[5], (D_MODEL, D_MODEL), jnp.float32) * scale, 'bq': jnp.zeros((D_MODEL,), jnp.float32), 'Wo': jax.random.normal(ks[6], (D_MODEL, D_MODEL), jnp.float32) * scale, 'bo': jnp.zeros((D_MODEL,), jnp.float32)}
        return inp
    _L1_xattn_all = _L1_xattn_setup()
    _L1_xattn_in = {k: v for k, v in _L1_xattn_all.items() if k in ('Wk', 'bk', 'Wv', 'bv', 'Wq', 'bq', 'Wo', 'bo')}
    del _L1_xattn_all

    def _L1_ffn_setup():
        import jax, jax.numpy as jnp
        import numpy as np
        D_MODEL = 256
        N_HEADS = 16
        HEAD_DIM = D_MODEL // N_HEADS
        FFN_DIM = 1024
        N_EXPERTS = 8
        CAP_FRAC = 0.25
        MOE_TOKEN_DROPOUT = 0.2
        LN_EPS = 1e-05
        B, S = (4, 128)

        def _layer_norm(x, g, b):
            mu = x.mean(-1, keepdims=True)
            var = ((x - mu) ** 2).mean(-1, keepdims=True)
            return (x - mu) * jax.lax.rsqrt(var + LN_EPS) * g + b

        def _self_attention(x, wq, bq, wk, bk, wv, bv, wo, bo):
            b, s, d = x.shape
            q = ((x @ wq + bq) * HEAD_DIM ** (-0.5)).reshape(b, s, N_HEADS, HEAD_DIM)
            k = (x @ wk + bk).reshape(b, s, N_HEADS, HEAD_DIM)
            v = (x @ wv + bv).reshape(b, s, N_HEADS, HEAD_DIM)
            scores = jnp.einsum('bqhd,bkhd->bhqk', q, k)
            p = jax.nn.softmax(scores, axis=-1)
            o = jnp.einsum('bhqk,bkhd->bqhd', p, v).reshape(b, s, d)
            return o @ wo + bo

        def _moe_ffn(x, wr, w1, b1, w2, b2):
            T, D = x.shape
            C = int(np.ceil(CAP_FRAC * T))
            logits = x @ wr
            probs = jax.nn.softmax(logits, axis=-1)
            top1 = jnp.argmax(probs, axis=-1)
            m1 = jax.nn.one_hot(top1, N_EXPERTS, dtype=x.dtype)
            top2 = jnp.argmax(jnp.where(m1 > 0, -jnp.inf, logits), axis=-1)
            m2 = jax.nn.one_hot(top2, N_EXPERTS, dtype=x.dtype)
            loc1 = jnp.cumsum(m1, axis=0) - 1.0
            loc2 = jnp.cumsum(m2, axis=0) - 1.0 + m1.sum(0, keepdims=True)
            m1 = m1 * (loc1 < C)
            m2 = m2 * (loc2 < C)
            t1 = (probs * m1).sum(-1)
            t2 = (probs * m2).sum(-1)
            denom = jnp.maximum(t1 + t2, jnp.finfo(x.dtype).eps)
            t1, t2 = (t1 / denom, t2 / denom)
            tok = jnp.arange(T)
            s1 = loc1[tok, top1].astype(jnp.int32)
            s2 = loc2[tok, top2].astype(jnp.int32)
            v1 = m1[tok, top1] > 0
            v2 = m2[tok, top2] > 0
            s1 = jnp.where(v1, s1, C)
            s2 = jnp.where(v2, s2, C)
            buf = jnp.zeros((N_EXPERTS, C, D), x.dtype)
            buf = buf.at[top1, s1].set(x, mode='drop')
            buf = buf.at[top2, s2].set(x, mode='drop')
            h = jax.nn.relu(jnp.einsum('ecd,edf->ecf', buf, w1) + b1[:, None, :])
            y = (jnp.einsum('ecf,efd->ecd', h, w2) + b2[:, None, :]) * (1.0 - MOE_TOKEN_DROPOUT)
            y1 = y[top1, jnp.minimum(s1, C - 1)]
            y2 = y[top2, jnp.minimum(s2, C - 1)]
            g1 = t1 * v1
            g2 = t2 * v2
            return g1[:, None] * y1 + g2[:, None] * y2
        key = jax.random.key(seed)
        ks = jax.random.split(key, 20)

        def w(k, shape, scale=0.02):
            return jax.random.normal(k, shape, jnp.float32) * scale
        return {'x': jax.random.normal(ks[0], (B, S, D_MODEL), jnp.float32), 'wq': w(ks[1], (D_MODEL, D_MODEL)), 'bq': w(ks[2], (D_MODEL,)), 'wk': w(ks[3], (D_MODEL, D_MODEL)), 'bk': w(ks[4], (D_MODEL,)), 'wv': w(ks[5], (D_MODEL, D_MODEL)), 'bv': w(ks[6], (D_MODEL,)), 'wo': w(ks[7], (D_MODEL, D_MODEL)), 'bo': w(ks[8], (D_MODEL,)), 'ln1_g': 1.0 + w(ks[9], (D_MODEL,)), 'ln1_b': w(ks[10], (D_MODEL,)), 'ln2_g': 1.0 + w(ks[11], (D_MODEL,)), 'ln2_b': w(ks[12], (D_MODEL,)), 'wr': w(ks[13], (D_MODEL, N_EXPERTS)), 'w1': w(ks[14], (N_EXPERTS, D_MODEL, FFN_DIM)), 'b1': w(ks[15], (N_EXPERTS, FFN_DIM)), 'w2': w(ks[16], (N_EXPERTS, FFN_DIM, D_MODEL)), 'b2': w(ks[17], (N_EXPERTS, D_MODEL))}
    _L1_ffn_all = _L1_ffn_setup()
    _L1_ffn_in = {k: v for k, v in _L1_ffn_all.items() if k in ('wq', 'bq', 'wk', 'bk', 'wv', 'bv', 'wo', 'bo', 'ln1_g', 'ln1_b', 'ln2_g', 'ln2_b', 'wr', 'w1', 'b1', 'w2', 'b2')}
    del _L1_ffn_all
    return {'x': x, 'ctx_1024': ctx_1024, 'g_xattn': g_xattn, 'g_ffn': g_ffn, 'L0_xattn_Wq': _L0_xattn_in['Wq'], 'L0_xattn_bq': _L0_xattn_in['bq'], 'L0_xattn_Wk': _L0_xattn_in['Wk'], 'L0_xattn_bk': _L0_xattn_in['bk'], 'L0_xattn_Wv': _L0_xattn_in['Wv'], 'L0_xattn_bv': _L0_xattn_in['bv'], 'L0_xattn_Wo': _L0_xattn_in['Wo'], 'L0_xattn_bo': _L0_xattn_in['bo'], 'L0_ffn_wf': _L0_ffn_in['wf'], 'L0_ffn_uf': _L0_ffn_in['uf'], 'L0_ffn_bf': _L0_ffn_in['bf'], 'L0_ffn_wi': _L0_ffn_in['wi'], 'L0_ffn_ui': _L0_ffn_in['ui'], 'L0_ffn_bi': _L0_ffn_in['bi'], 'L0_ffn_wc': _L0_ffn_in['wc'], 'L0_ffn_uc': _L0_ffn_in['uc'], 'L0_ffn_bc': _L0_ffn_in['bc'], 'L0_ffn_wo': _L0_ffn_in['wo'], 'L0_ffn_uo': _L0_ffn_in['uo'], 'L0_ffn_bo': _L0_ffn_in['bo'], 'L0_ffn_in_c': _L0_ffn_in['in_c'], 'L1_xattn_Wk': _L1_xattn_in['Wk'], 'L1_xattn_bk': _L1_xattn_in['bk'], 'L1_xattn_Wv': _L1_xattn_in['Wv'], 'L1_xattn_bv': _L1_xattn_in['bv'], 'L1_xattn_Wq': _L1_xattn_in['Wq'], 'L1_xattn_bq': _L1_xattn_in['bq'], 'L1_xattn_Wo': _L1_xattn_in['Wo'], 'L1_xattn_bo': _L1_xattn_in['bo'], 'L1_ffn_wq': _L1_ffn_in['wq'], 'L1_ffn_bq': _L1_ffn_in['bq'], 'L1_ffn_wk': _L1_ffn_in['wk'], 'L1_ffn_bk': _L1_ffn_in['bk'], 'L1_ffn_wv': _L1_ffn_in['wv'], 'L1_ffn_bv': _L1_ffn_in['bv'], 'L1_ffn_wo': _L1_ffn_in['wo'], 'L1_ffn_bo': _L1_ffn_in['bo'], 'L1_ffn_ln1_g': _L1_ffn_in['ln1_g'], 'L1_ffn_ln1_b': _L1_ffn_in['ln1_b'], 'L1_ffn_ln2_g': _L1_ffn_in['ln2_g'], 'L1_ffn_ln2_b': _L1_ffn_in['ln2_b'], 'L1_ffn_wr': _L1_ffn_in['wr'], 'L1_ffn_w1': _L1_ffn_in['w1'], 'L1_ffn_b1': _L1_ffn_in['b1'], 'L1_ffn_w2': _L1_ffn_in['w2'], 'L1_ffn_b2': _L1_ffn_in['b2']}

def reference(x, ctx_1024, g_xattn, g_ffn, L0_xattn_Wq, L0_xattn_bq, L0_xattn_Wk, L0_xattn_bk, L0_xattn_Wv, L0_xattn_bv, L0_xattn_Wo, L0_xattn_bo, L0_ffn_wf, L0_ffn_uf, L0_ffn_bf, L0_ffn_wi, L0_ffn_ui, L0_ffn_bi, L0_ffn_wc, L0_ffn_uc, L0_ffn_bc, L0_ffn_wo, L0_ffn_uo, L0_ffn_bo, L0_ffn_in_c, L1_xattn_Wk, L1_xattn_bk, L1_xattn_Wv, L1_xattn_bv, L1_xattn_Wq, L1_xattn_bq, L1_xattn_Wo, L1_xattn_bo, L1_ffn_wq, L1_ffn_bq, L1_ffn_wk, L1_ffn_bk, L1_ffn_wv, L1_ffn_bv, L1_ffn_wo, L1_ffn_bo, L1_ffn_ln1_g, L1_ffn_ln1_b, L1_ffn_ln2_g, L1_ffn_ln2_b, L1_ffn_wr, L1_ffn_w1, L1_ffn_b1, L1_ffn_w2, L1_ffn_b2):
    import jax
    import jax.numpy as jnp

    def _L0_xattn_ref(query, key, value, Wq, bq, Wk, bk, Wv, bv, Wo, bo):
        import jax, jax.numpy as jnp
        import numpy as np
        H = 16
        D_MODEL = 256
        D_K = D_MODEL // H
        B, S, _ = query.shape

        def proj(x, W, b):
            y = x @ W.T + b
            return y.reshape(B, S, H, D_K).transpose(0, 2, 1, 3)
        q = proj(query, Wq, bq)
        k = proj(key, Wk, bk)
        v = proj(value, Wv, bv)
        scores = jnp.einsum('bhqd,bhkd->bhqk', q, k) / jnp.sqrt(jnp.float32(D_K))
        attn = jax.nn.softmax(scores, axis=-1)
        x = jnp.einsum('bhqk,bhkd->bhqd', attn, v)
        x = x.transpose(0, 2, 1, 3).reshape(B, S, H * D_K)
        return x @ Wo.T + bo

    def _L0_ffn_ref(x, wf, uf, bf, wi, ui, bi, wc, uc, bc, wo, uo, bo, in_c):
        import jax, jax.numpy as jnp
        import numpy as np
        from jax import lax
        T, B, I, M, O = (64, 64, 256, 256, 256)

        def _xavier(key, shape):
            fan_out, fan_in = shape
            limit = float(np.sqrt(6.0 / (fan_in + fan_out)))
            return jax.random.uniform(key, shape, jnp.float32, -limit, limit)
        batch = x.shape[1]
        c0 = jnp.broadcast_to(in_c, (batch, in_c.shape[0]))

        def step(c, xt):
            ft = jax.nn.sigmoid(xt @ wf.T + c @ uf.T + bf)
            it = jax.nn.sigmoid(xt @ wi.T + c @ ui.T + bi)
            gt = jnp.tanh(xt @ wc.T + c @ uc.T + bc)
            c = ft * c + it * gt
            return (c, None)
        c_final, _ = lax.scan(step, c0, x)
        h = jnp.tanh(jnp.einsum('tbi,oi->tbo', x, wo) + c_final @ uo.T + bo)
        return h

    def _L1_xattn_ref(key, value, query, Wk, bk, Wv, bv, Wq, bq, Wo, bo):
        import jax, jax.numpy as jnp
        import numpy as np
        HEADS = 16
        D_MODEL = 256
        D_HEAD = D_MODEL // HEADS

        def _split_heads(x):
            B, S, _ = x.shape
            return x.reshape(B, S, HEADS, D_HEAD).transpose(0, 2, 1, 3)
        B, S, _ = query.shape
        k = _split_heads(key @ Wk + bk)
        v = _split_heads(value @ Wv + bv)
        q = _split_heads(query @ Wq + bq)
        scores = jnp.einsum('bhqd,bhkd->bhqk', q, k) / jnp.sqrt(jnp.float32(D_HEAD))
        attn = jax.nn.softmax(scores, axis=-1)
        x = jnp.einsum('bhqk,bhkd->bhqd', attn, v)
        x = x.transpose(0, 2, 1, 3).reshape(B, S, D_MODEL)
        return x @ Wo + bo

    def _L1_ffn_ref(x, wq, bq, wk, bk, wv, bv, wo, bo, ln1_g, ln1_b, ln2_g, ln2_b, wr, w1, b1, w2, b2):
        import jax, jax.numpy as jnp
        import numpy as np
        D_MODEL = 256
        N_HEADS = 16
        HEAD_DIM = D_MODEL // N_HEADS
        FFN_DIM = 1024
        N_EXPERTS = 8
        CAP_FRAC = 0.25
        MOE_TOKEN_DROPOUT = 0.2
        LN_EPS = 1e-05
        B, S = (4, 128)

        def _layer_norm(x, g, b):
            mu = x.mean(-1, keepdims=True)
            var = ((x - mu) ** 2).mean(-1, keepdims=True)
            return (x - mu) * jax.lax.rsqrt(var + LN_EPS) * g + b

        def _self_attention(x, wq, bq, wk, bk, wv, bv, wo, bo):
            b, s, d = x.shape
            q = ((x @ wq + bq) * HEAD_DIM ** (-0.5)).reshape(b, s, N_HEADS, HEAD_DIM)
            k = (x @ wk + bk).reshape(b, s, N_HEADS, HEAD_DIM)
            v = (x @ wv + bv).reshape(b, s, N_HEADS, HEAD_DIM)
            scores = jnp.einsum('bqhd,bkhd->bhqk', q, k)
            p = jax.nn.softmax(scores, axis=-1)
            o = jnp.einsum('bhqk,bkhd->bqhd', p, v).reshape(b, s, d)
            return o @ wo + bo

        def _moe_ffn(x, wr, w1, b1, w2, b2):
            T, D = x.shape
            C = int(np.ceil(CAP_FRAC * T))
            logits = x @ wr
            probs = jax.nn.softmax(logits, axis=-1)
            top1 = jnp.argmax(probs, axis=-1)
            m1 = jax.nn.one_hot(top1, N_EXPERTS, dtype=x.dtype)
            top2 = jnp.argmax(jnp.where(m1 > 0, -jnp.inf, logits), axis=-1)
            m2 = jax.nn.one_hot(top2, N_EXPERTS, dtype=x.dtype)
            loc1 = jnp.cumsum(m1, axis=0) - 1.0
            loc2 = jnp.cumsum(m2, axis=0) - 1.0 + m1.sum(0, keepdims=True)
            m1 = m1 * (loc1 < C)
            m2 = m2 * (loc2 < C)
            t1 = (probs * m1).sum(-1)
            t2 = (probs * m2).sum(-1)
            denom = jnp.maximum(t1 + t2, jnp.finfo(x.dtype).eps)
            t1, t2 = (t1 / denom, t2 / denom)
            tok = jnp.arange(T)
            s1 = loc1[tok, top1].astype(jnp.int32)
            s2 = loc2[tok, top2].astype(jnp.int32)
            v1 = m1[tok, top1] > 0
            v2 = m2[tok, top2] > 0
            s1 = jnp.where(v1, s1, C)
            s2 = jnp.where(v2, s2, C)
            buf = jnp.zeros((N_EXPERTS, C, D), x.dtype)
            buf = buf.at[top1, s1].set(x, mode='drop')
            buf = buf.at[top2, s2].set(x, mode='drop')
            h = jax.nn.relu(jnp.einsum('ecd,edf->ecf', buf, w1) + b1[:, None, :])
            y = (jnp.einsum('ecf,efd->ecd', h, w2) + b2[:, None, :]) * (1.0 - MOE_TOKEN_DROPOUT)
            y1 = y[top1, jnp.minimum(s1, C - 1)]
            y2 = y[top2, jnp.minimum(s2, C - 1)]
            g1 = t1 * v1
            g2 = t2 * v2
            return g1[:, None] * y1 + g2[:, None] * y2
        h = _layer_norm(x, ln1_g, ln1_b)
        h = _self_attention(h, wq, bq, wk, bk, wv, bv, wo, bo)
        x = x + h
        h = _layer_norm(x, ln2_g, ln2_b)
        b, s, d = h.shape
        moe = _moe_ffn(h.reshape(b * s, d), wr, w1, b1, w2, b2).reshape(b, s, d)
        return x + moe
    x = x + jnp.tanh(g_xattn[0]) * _L0_xattn_ref(_layernorm(x, axis=-1), ctx_1024, ctx_1024, L0_xattn_Wq, L0_xattn_bq, L0_xattn_Wk, L0_xattn_bk, L0_xattn_Wv, L0_xattn_bv, L0_xattn_Wo, L0_xattn_bo)
    x = x + jnp.tanh(g_ffn[0]) * _L0_ffn_ref(_layernorm(x, axis=-1), L0_ffn_wf, L0_ffn_uf, L0_ffn_bf, L0_ffn_wi, L0_ffn_ui, L0_ffn_bi, L0_ffn_wc, L0_ffn_uc, L0_ffn_bc, L0_ffn_wo, L0_ffn_uo, L0_ffn_bo, L0_ffn_in_c)
    x = x + jnp.tanh(g_xattn[1]) * _L1_xattn_ref(ctx_1024, ctx_1024, _layernorm(x, axis=-1), L1_xattn_Wk, L1_xattn_bk, L1_xattn_Wv, L1_xattn_bv, L1_xattn_Wq, L1_xattn_bq, L1_xattn_Wo, L1_xattn_bo)
    x = x + jnp.tanh(g_ffn[1]) * _L1_ffn_ref(_layernorm(x, axis=-1), L1_ffn_wq, L1_ffn_bq, L1_ffn_wk, L1_ffn_bk, L1_ffn_wv, L1_ffn_bv, L1_ffn_wo, L1_ffn_bo, L1_ffn_ln1_g, L1_ffn_ln1_b, L1_ffn_ln2_g, L1_ffn_ln2_b, L1_ffn_wr, L1_ffn_w1, L1_ffn_b1, L1_ffn_w2, L1_ffn_b2)
    return x

_drawn_inputs = setup_inputs


def setup_inputs(seed=0):
    import zlib

    import numpy as np

    out = dict(_drawn_inputs(seed))
    spreads = {'g_ffn': (-1.0, 0.2),
     'L0_xattn_bq': (0.0, 0.282),
     'L0_xattn_bk': (0.0, 0.8),
     'L0_xattn_bv': (0.0, 0.1),
     'L0_xattn_bo': (0.0, 0.1),
     'L0_ffn_bf': (0.0, 0.455),
     'L0_ffn_bi': (0.0, 0.42),
     'L0_ffn_bc': (0.0, 0.1),
     'L0_ffn_bo': (0.0, 0.1),
     'L0_ffn_in_c': (0.0, 0.614),
     'L1_xattn_bk': (0.0, 0.8),
     'L1_xattn_bv': (0.0, 0.1),
     'L1_xattn_bq': (0.0, 0.279),
     'L1_xattn_bo': (0.0, 0.1)}
    factors = {'L1_ffn_wq': 8.0,
     'L1_ffn_bq': 8.0,
     'L1_ffn_wk': 8.0,
     'L1_ffn_bk': 8.0,
     'L1_ffn_bv': 2.88,
     'L1_ffn_ln1_g': 6.05,
     'L1_ffn_ln1_b': 6.247,
     'L1_ffn_ln2_g': 2.75,
     'L1_ffn_b1': 5.973,
     'L1_ffn_b2': 2.671}
    for name, (base, spread) in spreads.items():
        noise = np.random.default_rng([zlib.crc32(name.encode()), seed]).standard_normal(out[name].shape)
        drawn = base * np.exp(spread * noise) if base else spread * noise
        out[name] = jnp.asarray(drawn.astype(out[name].dtype))
    for name, factor in factors.items():
        out[name] = (out[name] * factor).astype(out[name].dtype)
    return out
```

```python
from contextlib import ExitStack

import concourse.bass as bass
from concourse import mybir

F32 = mybir.dt.float32
BF16 = mybir.dt.bfloat16
U32 = mybir.dt.uint32
ALU = mybir.AluOpType
ACT = mybir.ActivationFunctionType
AX = mybir.AxisListType

P = 128
B, S, D = 8, 256, 256
H, DK = 16, 16
TT = S // P
KT = D // P
NT = B * TT
E, F, C = 8, 1024, 512
FT = F // P
CT = C // P
EPS_LN = 1e-5
EPS_F32 = 1.1920928955078125e-07
SCALE = 0.25
KEEP = 0.8
SLOTS = 6
Q_PART = (0, 0, 1, 1, 0, 2)
K_PART = (0, 1, 0, 1, 2, 0)
KROWS = SLOTS * DK
MROWS = 2
UNITS = 16
RING = 8

(W_Q0, W_K0, W_V0, W_O0, W_F, W_UF, W_I, W_UI, W_C, W_UC, W_OX, W_UO,
 W_Q1, W_K1, W_V1, W_O1, W_QS, W_KS, W_VS, W_OS) = range(20)
(C_Q0, C_K0, C_F, C_I, C_C, C_IN, C_Q1, C_K1, C_QS, C_KS) = range(10)
(R_V0, R_O0, R_OF, R_V1, R_O1, R_VS, R_OS, R_G1, R_B1, R_G2, R_B2, R_E) = range(12)
WEIGHTS = {"A": (W_Q0, W_K0, W_V0, W_O0), "X": (W_Q1, W_K1, W_V1, W_O1), "S": (W_QS, W_KS, W_VS, W_OS)}
COLS = {"A": (C_Q0, C_K0), "X": (C_Q1, C_K1), "S": (C_QS, C_KS)}
ROWS = {"A": (R_V0, R_O0), "X": (R_V1, R_O1), "S": (R_VS, R_OS)}


class Job:

    def __init__(self, n, kind, b, par):
        self.n, self.kind, self.b, self.par = n, kind, b, par
        self.tail = b if kind == "A" else B + b
        self.load = b if kind == "A" else B + b


def job_a(n, par):
    return Job(n, "A", n, par)


def schedule(eng, steps):
    A = [job_a(n, n % 2) for n in range(B)]
    steps.alone(A[0])
    steps.step(-1, A[1], A[0], None, None)
    steps.step(0, A[2], A[1], A[0], None)
    steps.step(1, A[3], A[2], A[1], A[0])
    with eng.Fori(0, 2) as i:
        k = 2 * i + 2
        steps.enter(k, "A", i)
        steps.step(k, job_a(k + 2, 0), job_a(k + 1, 1), job_a(k, 0), job_a(k - 1, 1))
        k = 2 * i + 3
        steps.step(k, job_a(k + 2, 1), job_a(k + 1, 0), job_a(k, 1), job_a(k - 1, 0))
        steps.leave("A")
    steps.left(6, "A", 2)
    steps.step(6, None, A[7], A[6], A[5])
    steps.step(7, None, None, A[7], A[6])
    steps.after(A[7])
    steps.middle()

    X = [Job(8, "X", 0, 0)] + [Job(7 + 2 * b, "X", b, 1) for b in range(1, B)]
    T = [Job(10 + 2 * b, "S", b, 0) for b in range(B - 1)] + [Job(23, "S", B - 1, 1)]
    steps.alone(X[0])
    steps.step(7, X[1], X[0], None, None)
    steps.step(8, None, X[1], X[0], None)
    steps.alone(T[0])
    steps.step(9, X[2], T[0], X[1], None)
    steps.step(10, T[1], X[2], T[0], None)
    with eng.Fori(0, 5) as i:
        r = i + 2
        k = 2 * i + 11
        steps.enter(k, "B", i)
        steps.step(k, Job(k + 2, "X", r + 1, 1), Job(k + 1, "S", r - 1, 0), Job(k, "X", r, 1),
                   Job(k - 1, "S", r - 2, 0))
        k = 2 * i + 12
        steps.step(k, Job(k + 2, "S", r, 0), Job(k + 1, "X", r + 1, 1), Job(k, "S", r - 1, 0), None)
        steps.leave("B")
    steps.left(21, "B", 5)
    steps.step(21, None, T[6], X[7], T[5])
    steps.alone(T[7])
    steps.step(22, None, T[7], T[6], None)
    steps.step(23, None, None, T[7], T[6])
    steps.after(T[7])


def wait(eng, sem, value):
    if isinstance(value, int) and value <= 0:
        return
    eng.wait_ge(sem, value)


def settle(eng, sem):
    eng.sem_inc(sem, 1)


class Chain:

    def __init__(self, eng, sem, per):
        self.eng, self.sem, self.per = eng, sem, per
        self.base, self.n = 0, 0

    def mark(self, ins):
        ins.then_inc(self.sem, 1)
        self.n += 1

    def wait(self):
        self.eng.wait_ge(self.sem, self.base + self.n)

    def link(self, ins):
        self.mark(ins)
        self.wait()

    def enter(self, name, i):
        self.start = self.base + self.n
        self.base, self.n = self.start + self.per[name] * i, 0

    def leave(self, name):
        assert self.n == self.per[name], (name, self.n)

    def left(self, name, count):
        self.base, self.n = self.start + self.per[name] * count, 0


def flamingo(nc, t):
    ctx = ExitStack()
    with ctx:
        def sb(name, shape, dt=F32):
            return ctx.enter_context(nc.sbuf_tensor("sb_" + name, shape, dt))

        def bank(name):
            return ctx.enter_context(nc.psum_tensor("ps_" + name, [P, 512], F32))

        sems = {}

        def sem(name):
            if name not in sems:
                sems[name] = ctx.enter_context(nc.semaphore(name))
            return sems[name]

        weights = sb("weights", [P, 20, KT, D])
        cols = sb("cols", [P, 10, KT])
        rows = sb("rows", [P, R_E, D])
        b1c = sb("b1c", [P, E, FT])
        wr = sb("wr", [P, KT, E])
        gates_in = sb("gates_in", [P, 4])
        tg = sb("tg", [P, 4])
        x = sb("x", [P, NT, D])
        x4 = sb("x4", [P, NT, D])
        xo = sb("xo", [P, NT, D])
        h2 = xo
        ctxT = sb("ctxT", [P, KT, S])
        hN = sb("hN", [P, TT, D])
        hT = sb("hT", [P, KT, S])
        tN = sb("tN", [P, TT, D])
        tT = sb("tT", [P, KT, S])
        stats = sb("stats", [P, 2, TT, 6])
        mv = sb("mv", [P, 2, TT, 2])
        ve = sb("ve", [P, 3, TT])
        rec = sb("rec", [P, TT])
        rstd = sb("rstd", [P, 3, TT])
        minus_half = sb("minus_half", [P, 2, TT])
        full = sb("full", [P, 2, KT, S])
        parts = sb("parts", [P, 3, 2, KT, S], BF16)
        qs = sb("qs", [P, 2, H, S], BF16)
        ks = sb("ks", [P, 2, H, S], BF16)
        vv = sb("vv", [P, 2, TT, H, 32])
        nmax = sb("nmax", [P, TT, H])
        nmaxb = sb("nmaxb", [P, TT, MROWS, H], BF16)
        nmt = sb("nmt", [32, S], BF16)
        ring = sb("ring", [P, RING, 2, S])
        os_ = sb("os", [P, 4, S])
        rden = sb("rden", [P, TT, H])
        on = sb("on", [P, TT, D])
        ot = sb("ot", [P, KT, S])
        res = sb("res", [P, TT, D])
        cT = sb("cT", [P, KT, S])
        gact = sb("gact", [P, 3, KT, S])
        cu = sb("cu", [P, TT, D])
        xt = sb("xt", [P, TT, D])
        lg = sb("lg", [P, NT, E])
        ident = sb("ident", [P, P])
        identb = sb("identb", [P, P], BF16)

        p1 = [bank("p1a"), bank("p1b")]
        p2 = [bank("p2a"), bank("p2b")]
        po = [bank("poa"), bank("pob")]
        g = [bank("g0"), bank("g1")]

        def bk(t_, a):
            return t_[:, :].rearrange("p (a c) -> p a c", a=a)

        parts_dram = nc.dram_tensor("parts_dram", (3, 2, KT, P, S), BF16, kind="Internal").ap()
        buf_dram = nc.dram_tensor("buf_dram", (E * C, D), F32, kind="Internal").ap()
        y_dram = nc.dram_tensor("y_dram", (E * C, D), F32, kind="Internal").ap()

        w1s = qs[:, :, :, :].rearrange("p a h s -> p (a h s)").bitcast(F32).rearrange(
            "p (a k f) -> p a k f", a=2, k=KT)
        w2s = ks[:, :, :, :].rearrange("p a h s -> p (a h s)").bitcast(F32).rearrange(
            "p (a k f) -> p a k f", a=2, k=FT)
        arena = weights[:, :, :, :].rearrange("p a k n -> p (a k) n")
        br = [arena[:, 4 * i:4 * i + 4, :] for i in range(2)]
        bT = arena[:, 8:12, :].rearrange("p (k a) n -> p k (a n)", k=KT)
        yb = [arena[:, 12 + 4 * i:16 + 4 * i, :] for i in range(2)]
        b2r = arena[:, 32:40, :]
        yg = arena[:, 0:32, :]
        hid = ring[:, :, :, :].rearrange("p a b c -> p a (b c)")
        zero = x4[:, 0:1, :]

        (ld_small, ld_w0, ld_w1, ld_x0, ld_x1) = [sem(s) for s in
                                                  ("ld_small", "ld_w0", "ld_w1", "ld_x0", "ld_x1")]
        NSMALL = 6

        block = ctx.enter_context(nc.Block())

        class SpSteps:
            def __init__(self, sp):
                self.sp = sp

            def enter(self, k, name, i):
                pass

            def leave(self, name):
                pass

            def left(self, k, name, count):
                pass

            def load_context(self, b):
                src = t["ctxT"].rearrange("b (k p) s -> b p k s", p=P)
                self.sp.dma_start(ctxT[:, :, :], src[bass.ds(b, 1)].rearrange("o p k s -> (o p) k s")
                                  ).then_inc(sem("context_in"), 16)

            def parts_out(self, j):
                sp = self.sp
                wait(sp, sem("split"), j.n + 1)
                settle(sp, sem("sp_passed"))
                wait(sp, sem("stacked"), 16 * 2 * SLOTS * j.n)
                settle(sp, sem("sp_passed"))
                sp.dma_start(parts_dram.rearrange("a q m p c -> p (a q m) c"),
                             parts[:, :, :, :, :].rearrange("p a q m c -> p (a q m) c")
                             ).then_inc(sem("parts_out"), 16)

            def stack(self, j):
                sp = self.sp
                wait(sp, sem("parts_out"), 16 * (j.n + 1))
                settle(sp, sem("sp_passed"))
                wait(sp, sem("scores2"), UNITS * (j.n - 1))
                settle(sp, sem("sp_passed"))
                for q, (dst, part) in enumerate(((qs, Q_PART), (ks, K_PART))):
                    for s in range(SLOTS):
                        src = parts_dram[part[s], q].rearrange("m (h d) c -> d (m h) c", d=DK)
                        sp.dma_start(dst[DK * s:DK * (s + 1), j.par, :, :], src).then_inc(sem("stacked"), 16)

            def next_context(self, j):
                if j.kind == "S":
                    return
                wait(self.sp, sem("v_mm"), j.n + 1)
                settle(self.sp, sem("sp_passed"))
                self.load_context(j.b + 1)

            def alone(self, j):
                self.parts_out(j)
                self.stack(j)
                self.next_context(j)

            def step(self, k, front, mid, back, tail):
                sp = self.sp
                if front:
                    self.parts_out(front)
                if mid:
                    wait(sp, sem("nmax_sb"), mid.n + 1)
                    settle(sp, sem("sp_passed"))
                    for r in range(MROWS):
                        sp.dma_start(qs[KROWS + r:KROWS + r + 1, mid.par, :, :], nmt[H * r:H * (r + 1), :]
                                     ).then_inc(sem("nmax_in"), 16)
                if front:
                    self.stack(front)
                    self.next_context(front)

            def after(self, j):
                pass

            def middle(self):
                pass

        @block.sync
        def _(sp):
            sp.dma_start(x[:, 0:TT, :], t["x"][0].rearrange("(t p) d -> p t d", p=P)).then_inc(ld_x0, 16)
            wv = t["weights"].rearrange("w (k p) n -> p w k n", p=P)
            sp.dma_start(weights[:, 0:4, :, :], wv[:, 0:4]).then_inc(ld_w0, 16)
            steps = SpSteps(sp)
            steps.load_context(0)
            sp.dma_start(cols[:, :, :], t["cols"].rearrange("p (a k) -> p a k", k=KT)).then_inc(ld_small, 16)
            rv = t["rows"]
            sp.dma_start(rows[:, :, :].rearrange("p a d -> p (a d)"),
                         bass.AP(rv.tensor, rv.offset, [[0, P], [1, R_E * D]])).then_inc(ld_small, 16)
            gv = t["gates"]
            sp.dma_start(gates_in[:, :], bass.AP(gv.tensor, gv.offset, [[0, P], [1, 4]])).then_inc(ld_small, 16)
            sp.dma_start(b1c[:, :, :], t["b1"].rearrange("p (e f) -> p e f", e=E)).then_inc(ld_small, 16)
            sp.dma_start(wr[:, :, :], t["wr"].rearrange("(k p) e -> p k e", p=P)).then_inc(ld_small, 16)
            sp.dma_start(x[:, TT:NT, :], t["x"][1:B].rearrange("b (t p) d -> p (b t) d", p=P)).then_inc(ld_x1, 16)
            sp.dma_start(weights[:, 4:20, :, :], wv[:, 4:20]).then_inc(ld_w1, 16)
            sp.wait_ge(sem("zero_ready"), 1)
            sp.dma_start(buf_dram.rearrange("(a p) d -> p a d", p=P),
                         zero.to_broadcast([P, E * CT, D])).then_inc(sem("slots_zero"), 16)
            schedule(sp, steps)

            def load_weights(e, par):
                sp.dma_start(w1s[:, par], t["w1"][bass.ds(e, 1)].rearrange("o (k p) f -> p (o k) f", p=P)
                             ).then_inc(sem(f"w1_in{par}"), 16)
                sp.dma_start(w2s[:, par], t["w2"][bass.ds(e, 1)].rearrange("o (k p) f -> p (o k) f", p=P)
                             ).then_inc(sem(f"w2_in{par}"), 16)

            slots = buf_dram.rearrange("(e s p) d -> e p s d", e=E, p=P)
            outs = y_dram.rearrange("(e s p) d -> e p s d", e=E, p=P)

            def load_slots(e, par):
                sp.dma_start(br[par], slots[bass.ds(e, 1)].rearrange("o p s d -> (o p) s d")
                             ).then_inc(sem(f"slots_in{par}"), 16)

            sp.wait_ge(sem("scores2"), UNITS * 3 * B)
            load_weights(0, 0)
            load_weights(1, 1)
            sp.wait_ge(sem("tail_mm"), 2 * B)
            bv = t["b2"]
            sp.dma_start(b2r.rearrange("p e d -> p (e d)"), bass.AP(bv.tensor, bv.offset, [[0, P], [1, E * D]])
                         ).then_inc(sem("b2_in"), 16)
            sp.wait_ge(sem("slots_filled"), 16 * 2 * NT)
            load_slots(0, 0)
            load_slots(1, 1)
            with sp.Fori(0, E // 2 - 1) as i:
                for par in range(2):
                    sp.wait_ge(sem("y_ready"), CT * (2 * i + par + 1))
                    settle(sp, sem("sp_passed"))
                    sp.dma_start(outs[bass.ds(2 * i + par, 1)].rearrange("o p s d -> (o p) s d"), yb[par]
                                 ).then_inc(sem("y_out"), 16)
                    load_weights(2 * i + par + 2, par)
                    load_slots(2 * i + par + 2, par)
            for par in range(2):
                sp.wait_ge(sem("y_ready"), CT * (E - 2 + par + 1))
                sp.dma_start(outs[E - 2 + par], yb[par]).then_inc(sem("y_out"), 16)
            out = t["out"].rearrange("b (t p) d -> p (b t) d", p=P)
            for q in range(4):
                sp.wait_ge(sem("final"), NT // 4 * (q + 1))
                s = slice(NT // 4 * q, NT // 4 * (q + 1))
                sp.dma_start(out[:, s, :], x4[:, s, :]).then_inc(sem("stored"), 16)
            sp.wait_ge(sem("stored"), 64)

        class PoolSteps:
            def __init__(self, pool):
                self.pool = pool
                self.chain = Chain(pool, sem("pool_chain"), {"A": 6, "B": 6})

            def enter(self, k, name, i):
                self.chain.enter(name, i)

            def leave(self, name):
                self.chain.leave(name)

            def left(self, k, name, count):
                self.chain.left(name, count)

            def rstd(self, who, count, kind):
                wait(self.pool, sem(f"{who}_var"), count)
                a, n = (0, 1) if who == "tail" else (1, 2 if kind == "S" else 1)
                self.pool.tensor_tensor(rstd[:, a:a + n, :], ve[:, a:a + n, :], minus_half[:, 0:n, :], ALU.pow
                                        ).then_inc(sem(f"{who}_rstd"), 1)

            def split(self, j):
                pool, link = self.pool, self.chain.link
                wait(pool, sem("qk_full"), 2 * (j.n + 1))
                wait(pool, sem("parts_out"), 16 * j.n)
                settle(pool, sem("pool_passed"))
                link(pool.tensor_copy(parts[:, 0], full[:, :, :, :]))
                link(pool.tensor_tensor(full[:, :, :, :], full[:, :, :, :], parts[:, 0], ALU.subtract))
                settle(pool, sem("pool_passed"))
                link(pool.tensor_copy(parts[:, 1], full[:, :, :, :]))
                pool.tensor_tensor(parts[:, 2], full[:, :, :, :], parts[:, 1], ALU.subtract
                                   ).then_inc(sem("split"), 1)

            def alone(self, j):
                self.rstd("front", j.n + 1, j.kind)
                self.split(j)

            def step(self, k, front, mid, back, tail):
                if tail:
                    self.rstd("tail", tail.tail + 1, tail.kind)
                if front:
                    self.rstd("front", front.n + 1, front.kind)
                if tail and tail.kind == "S":
                    self.keep(tail)
                if front:
                    self.split(front)

            def keep(self, j):
                wait(self.pool, sem("tail_h"), j.tail + 1)
                settle(self.pool, sem("pool_passed"))
                self.pool.tensor_copy(h2[:, bass.ds(TT * j.b, TT), :], tN[:, :, :]).then_inc(sem("kept"), 1)

            def after(self, j):
                self.rstd("tail", j.tail + 1, j.kind)
                if j.kind == "S":
                    self.keep(j)

            def middle(self):
                pass

        top = sb("top", [P, NT, 8])
        topi = sb("topi", [P, NT, 8], U32)
        idxf = sb("idxf", [P, 2, NT])
        iota = sb("iota", [P, E])
        mask = sb("mask", [P, 2, NT, E], BF16)
        tri = sb("tri", [P, P], BF16)
        ones = sb("ones", [P, P], BF16)
        zeros32 = sb("zeros32", [P, 2 * NT])
        ex = sb("ex", [P, NT, 8])
        sums = sb("sums", [P, NT])
        inc = sb("inc", [P, 2 * NT, E])
        loc = sb("loc", [P, 2 * NT, E])
        pos = sb("pos", [P, 2 * NT])
        valid = sb("valid", [P, 2, NT])
        slotf = sb("slotf", [P, 2 * NT])
        slotg = sb("slotg", [P, 2 * NT])
        sidx = sb("sidx", [P, 2 * NT], U32)
        gidx = sb("gidx", [P, 2 * NT], U32)
        prob = sb("prob", [P, 2, NT])
        den = sb("den", [P, NT])
        gate = sb("gate", [P, 2, NT])

        @block.gpsimd
        def _(pool):
            steps = PoolSteps(pool)
            link = steps.chain.link
            pool.memset(minus_half[:, :, :], -0.5).then_inc(sem("pool_const"), 1)
            link(pool.memset(ident[:, :], 0.0))
            pool.affine_select(out=ident[:, :], in_=ident[:, :], compare_op=ALU.not_equal, fill=1.0, base=0,
                               pattern=[[-1, P]], channel_multiplier=1).then_inc(sem("pool_const"), 1)
            link(pool.memset(identb[:, :], 0.0))
            pool.affine_select(out=identb[:, :], in_=identb[:, :], compare_op=ALU.not_equal, fill=1.0, base=0,
                               pattern=[[-1, P]], channel_multiplier=1).then_inc(sem("pool_const"), 1)
            link(pool.memset(vv[:, :, :, :, DK:], 1.0))
            link(pool.memset(ks[KROWS:, :, :, :], 1.0))
            pool.memset(ones[:, :], 1.0).then_inc(sem("pool_const"), 1)
            link(pool.memset(tri[:, :], 1.0))
            pool.affine_select(out=tri[:, :], in_=tri[:, :], compare_op=ALU.is_ge, fill=0.0, base=0,
                               pattern=[[1, P]], channel_multiplier=-1).then_inc(sem("pool_const"), 1)
            pool.iota(iota[:, :], [[1, E]], base=0, channel_multiplier=0,
                      allow_small_or_imprecise_dtypes=True).then_inc(sem("pool_const"), 1)
            pool.wait_ge(sem("pool_const"), 6)
            pool.wait_ge(sem("pool_chain"), 5)
            schedule(pool, steps)
            pool.wait_ge(sem("slots_zero"), 16)
            pool.wait_ge(sem("kept"), B)
            pool.wait_ge(sem("slots_ready"), 1)
            for w in range(2):
                for i in range(NT):
                    j = w * NT + i
                    pool.indirect_dma_start(buf_dram, bass.IndirectOffsetOnAxis(sidx[:, j:j + 1], 0),
                                            h2[:, i, :], None, bounds_check=E * C - 1, oob_is_err=False
                                            ).then_inc(sem("slots_filled"), 16)
            pool.wait_ge(sem("y_out"), 16 * E)
            for i in range(NT):
                for w in range(2):
                    j = w * NT + i
                    pool.indirect_dma_start(yg[:, 2 * i + w, :], None, y_dram,
                                            bass.IndirectOffsetOnAxis(gidx[:, j:j + 1], 0),
                                            bounds_check=E * C - 1, oob_is_err=False
                                            ).then_inc(sem(f"gathered{i}"), 16)

        class ActSteps:
            def __init__(self, act):
                self.act = act

            def enter(self, k, name, i):
                pass

            def leave(self, name):
                pass

            def left(self, k, name, count):
                pass

            def gate_x(self, j):
                wait(self.act, sem("xo_sum"), j.b + 1)
                self.act.activation(xt[:, :, :], xt[:, :, :], ACT.Tanh).then_inc(sem("xo_tanh"), 1)

            def front_T(self, j):
                wait(self.act, sem("front_tr"), j.n + 1)
                wait(self.act, sem("v_mm"), j.n)
                self.act.activation(hT[:, :, :], bk(g[0], KT), ACT.Copy).then_inc(sem("front_hT"), 1)

            def qk(self, j, q):
                wait(self.act, sem("qk_mm"), 2 * j.n + q + 1)
                wait(self.act, sem("split"), j.n)
                for m in range(KT):
                    ins = self.act.activation(full[:, q, m, :], bk(g[1 - q], KT)[:, m, :], ACT.Identity,
                                              bias=cols[:, COLS[j.kind][q], m:m + 1])
                ins.then_inc(sem("qk_full"), 1)

            def nmax_sb(self, j):
                wait(self.act, sem("nmax_tr"), j.n + 1)
                wait(self.act, sem("nmax_in"), 16 * MROWS * j.n)
                self.act.activation(nmt[:, :], g[1][0:32, 0:P].bitcast(BF16), ACT.Copy
                                    ).then_inc(sem("nmax_sb"), 1)

            def exp(self, j, u):
                act = self.act
                wait(act, sem("scores2"), UNITS * j.n + u + 1)
                if u % 4 == 0:
                    wait(act, sem("pv"), 4 * j.n + u // 4 - 1)
                act.activation(ring[:, u % RING], bk(p2[u % 2], 2), ACT.Exp, scale=SCALE
                               ).then_inc(sem("exp"), 1)

            def o_out(self, j, q):
                wait(self.act, sem("pv"), 4 * j.n + q + 1)
                wait(self.act, sem("o_tr"), 2 * j.n)
                self.act.activation(os_[:, q, :], po[q % 2][:, 0:S], ACT.Copy).then_inc(sem("o_sb"), 1)

            def oT(self, j):
                wait(self.act, sem("on_tr"), j.n + 1)
                wait(self.act, sem("proj_mm"), j.n)
                self.act.activation(ot[:, :, :], bk(g[1], KT), ACT.Copy).then_inc(sem("ot_sb"), 1)

            def tail_T(self, j):
                wait(self.act, sem("tail_tr"), j.tail + 1)
                wait(self.act, sem("tail_mm"), j.tail)
                self.act.activation(tT[:, :, :], bk(g[1], KT), ACT.Copy).then_inc(sem("tail_hT"), 1)

            def recur(self, j, q):
                wait(self.act, sem("gates_mm"), 3 * j.b + q + 1)
                wait(self.act, sem("c_new"), j.b + 1)
                for m in range(KT):
                    ins = self.act.activation(gact[:, q, m, :], bk(g[(q + 1) % 2], KT)[:, m, :], ACT.Tanh,
                                              bias=hcols[:, q, m:m + 1], scale=0.5 if q < 2 else 1.0)
                ins.then_inc(sem("gates"), 1)

            def alone(self, j):
                if j.kind == "X":
                    self.gate_x(j)
                self.front_T(j)
                self.qk(j, 0)
                self.qk(j, 1)

            def step(self, k, front, mid, back, tail):
                if front and front.kind == "X":
                    self.gate_x(front)
                for u in range(UNITS):
                    if back:
                        self.exp(back, u)
                    if tail and u == 2:
                        self.tail_T(tail)
                    if front and u == 3:
                        self.front_T(front)
                    if front and u in (5, 6):
                        self.qk(front, u - 5)
                    if tail and tail.kind == "A" and u in (7, 8, 9):
                        self.recur(tail, u - 7)
                    if back and u in (6, 10, 14):
                        self.o_out(back, (u - 6) // 4)
                if back:
                    self.o_out(back, 3)
                if mid:
                    self.nmax_sb(mid)
                if back:
                    self.oT(back)

            def after(self, j):
                self.tail_T(j)
                if j.kind == "A":
                    for q in range(3):
                        self.recur(j, q)

            def middle(self):
                pass

        hcols = sb("hcols", [P, 3, KT])

        @block.scalar
        def _(act):
            act.wait_ge(ld_small, 16 * 5)
            act.activation(tg[:, :], gates_in[:, :], ACT.Tanh).then_inc(sem("tg_ready"), 1)
            act.wait_ge(sem("hcols"), 1)
            schedule(act, ActSteps(act))
            act.wait_ge(sem("router_shift"), 1)
            act.activation(ex[:, :, :], ex[:, :, :], ACT.Exp).then_inc(sem("router_exp"), 1)

            def expert(e, par, prev):
                for h in range(KT):
                    act.wait_ge(sem("slots_tr"), KT * e + h + 1)
                    if prev:
                        act.wait_ge(sem("up_mm"), FT * e)
                    act.activation(bT[:, h, :], g[h][:, :], ACT.Copy).then_inc(sem("slots_T"), 1)
                for f in range(FT):
                    act.wait_ge(sem("up_mm"), FT * e + f + 1)
                    if prev:
                        act.wait_ge(sem("down_mm"), CT * e)
                    act.activation(hid[:, f, :], [p1, p2][f // 2 % 2][f % 2][:, :], ACT.Relu,
                                   bias=b1c[:, bass.ds(e, 1), f:f + 1].rearrange("p e f -> p (e f)")
                                   ).then_inc(sem("hidden"), 1)

            expert(0, 0, False)
            expert(1, 1, True)
            with act.Fori(1, E // 2) as i:
                for par in range(2):
                    expert(2 * i + par, par, True)

        class DveSteps:
            def __init__(self, dve):
                self.dve = dve
                self.chain = Chain(dve, sem("dve_chain"), {"A": 30, "B": 27})

            def enter(self, k, name, i):
                self.chain.enter(name, i)

            def leave(self, name):
                self.chain.leave(name)

            def left(self, k, name, count):
                self.chain.left(name, count)

            def norm_stats(self, w, who, src, b, again=False):
                dve, chain = self.dve, self.chain
                settle(dve, sem("dve_passed"))
                for i in range(TT):
                    chain.mark(dve.bn_stats(stats[:, w, i, :], src[:, bass.ds(TT * b + i, 1), :].rearrange(
                        "p o d -> p (o d)")))
                chain.wait()
                settle(dve, sem("dve_passed"))
                for i in range(TT):
                    chain.mark(dve.bn_aggr(mv[:, w, i, :], stats[:, w, i, :]))
                chain.wait()
                ins = dve.tensor_scalar(ve[:, w, :], mv[:, w, :, 1], EPS_LN, None, ALU.add)
                if again:
                    chain.link(ins)
                    chain.link(dve.reciprocal(rec[:, :], ve[:, w, :]))
                    ins = dve.tensor_scalar(ve[:, 2, :], rec[:, :], -EPS_LN, 1.0 + EPS_LN, ALU.mult, ALU.add)
                ins.then_inc(sem(f"{who}_var"), 1)

            def norm_apply(self, w, src, b, dst, ins_b=0):
                for i in range(TT):
                    ins = self.dve.tensor_scalar(dst[:, bass.ds(TT * ins_b + i, 1), :],
                                                 src[:, bass.ds(TT * b + i, 1), :],
                                                 mv[:, w, i, 0:1], rstd[:, w, i:i + 1], ALU.subtract, ALU.mult)
                return ins

            def add_row(self, dst, r):
                return self.dve.tensor_tensor(dst[:, :, :], dst[:, :, :],
                                              rows[:, r:r + 1, :].to_broadcast([P, TT, D]), ALU.add)

            def front_start(self, j):
                if j.kind == "X":
                    if isinstance(j.b, int) and j.b == 0:
                        self.dve.wait_ge(sem("cu_ready"), 1)
                    self.dve.tensor_tensor(xt[:, :, :], xo[:, bass.ds(TT * j.b, TT), :], cu[:, :, :], ALU.add
                                           ).then_inc(sem("xo_sum"), 1)

            def front_stats(self, j):
                dve = self.dve
                if j.kind == "A":
                    if isinstance(j.n, int) and j.n <= 1:
                        dve.wait_ge((ld_x0, ld_x1)[j.n], 16)
                if j.kind == "X":
                    wait(dve, sem("xo_tanh"), j.b + 1)
                    xs = x[:, bass.ds(TT * j.b, TT), :]
                    self.chain.link(dve.scalar_tensor_tensor(xs, xt[:, :, :], tg[:, 2:3], xs, ALU.mult, ALU.add))
                if j.kind == "S":
                    wait(dve, sem("residual"), j.n - (1 if isinstance(j.n, int) and j.b in (0, B - 1) else 2))
                self.norm_stats(1, "front", x, j.b, j.kind == "S")

            def front_apply(self, j):
                dve, chain = self.dve, self.chain
                wait(dve, sem("front_rstd"), j.n + 1)
                wait(dve, sem("front_tr"), j.n)
                if j.kind != "S":
                    self.norm_apply(1, x, j.b, hN).then_inc(sem("front_h"), 1)
                    return
                chain.link(self.norm_apply(1, x, j.b, x4, j.b))
                for i in range(TT):
                    ins = dve.scalar_tensor_tensor(hN[:, i, :], x4[:, bass.ds(TT * j.b + i, 1), :].rearrange(
                        "p o d -> p (o d)"), rstd[:, 2, i:i + 1], rows[:, R_G1, :], ALU.mult, ALU.mult)
                chain.link(ins)
                self.add_row(hN, R_B1).then_inc(sem("front_h"), 1)

            def tail_src(self, j):
                return x if j.kind == "A" else x4

            def tail_stats(self, j):
                wait(self.dve, sem("residual"), j.n + 1)
                self.norm_stats(0, "tail", self.tail_src(j), j.b)

            def tail_apply(self, j):
                dve, chain = self.dve, self.chain
                wait(dve, sem("tail_rstd"), j.tail + 1)
                wait(dve, sem("tail_tr"), j.tail)
                if j.kind != "S":
                    self.norm_apply(0, x, j.b, tN).then_inc(sem("tail_h"), 1)
                    return
                wait(dve, sem("kept"), j.b)
                chain.link(self.norm_apply(0, x4, j.b, tN))
                chain.link(dve.tensor_tensor(tN[:, :, :], tN[:, :, :],
                                             rows[:, R_G2:R_G2 + 1, :].to_broadcast([P, TT, D]), ALU.mult))
                self.add_row(tN, R_B2).then_inc(sem("tail_h"), 1)

            def maximum(self, j, u):
                dve = self.dve
                hp, q = u // 2, u % 2
                wait(dve, sem("scores1"), UNITS * j.n + u + 1)
                dve.tensor_reduce(nmax[:, q, 2 * hp:2 * hp + 2], bk(p1[u % 2], 2), AX.X, ALU.max, negate=True
                                  ).then_inc(sem("max"), 1)

            def split_max(self, j):
                dve, chain = self.dve, self.chain
                wait(dve, sem("max"), UNITS * (j.n + 1))
                wait(dve, sem("nmax_tr"), j.n)
                chain.link(dve.tensor_copy(nmaxb[:, :, 0, :], nmax[:, :, :]))
                dve.tensor_tensor(nmaxb[:, :, 1, :], nmax[:, :, :], nmaxb[:, :, 0, :], ALU.subtract
                                  ).then_inc(sem("nmaxb"), 1)

            def normalise(self, j):
                dve, chain = self.dve, self.chain
                wait(dve, sem("on_tr"), j.n)
                for q in range(TT):
                    o = g[q][:, :].rearrange("p (h c) -> p h c", h=H)
                    wait(dve, sem("o_tr"), 2 * j.n + q + 1)
                    chain.link(dve.reciprocal(rden[:, q, :], o[:, :, DK]))
                    dve.tensor_tensor(on[:, q, :].rearrange("p (h c) -> p h c", h=H), o[:, :, 0:DK],
                                      rden[:, q, :].rearrange("p (h o) -> p h o", o=1).to_broadcast([P, H, DK]),
                                      ALU.mult).then_inc(sem("on"), 1)

            def v_out(self, j, bank_):
                dve = self.dve
                wait(dve, sem("v_mm"), j.n + 1)
                wait(dve, sem("pv"), 4 * (j.n - 1))
                for q in range(TT):
                    ins = dve.tensor_tensor(
                        vv[:, j.par, q, :, 0:DK], bk(g[bank_], TT)[:, q, :].rearrange("p (h c) -> p h c", h=H),
                        rows[:, ROWS[j.kind][0], :].rearrange("p (h c) -> p h c", h=H), ALU.add)
                ins.then_inc(sem("v_sb"), 1)

            def residual(self, j):
                dve, chain = self.dve, self.chain
                wait(dve, sem("proj_mm"), j.n + 1)
                xs = x[:, bass.ds(TT * j.b, TT), :]
                chain.link(dve.tensor_tensor(res[:, :, :], bk(g[0], TT),
                                             rows[:, ROWS[j.kind][1], :].rearrange("p (o d) -> p o d", o=1
                                                                                   ).to_broadcast([P, TT, D]), ALU.add))
                if j.kind == "S":
                    x4s = x4[:, bass.ds(TT * j.b, TT), :]
                    dve.tensor_tensor(x4s, res[:, :, :], x4s, ALU.add
                                      ).then_inc(sem("residual"), 1)
                else:
                    w = 0 if j.kind == "A" else 1
                    dve.scalar_tensor_tensor(xs, res[:, :, :], tg[:, w:w + 1], xs, ALU.mult, ALU.add
                                             ).then_inc(sem("residual"), 1)

            def recur(self, j):
                dve, chain = self.dve, self.chain
                wait(dve, sem("gates"), 3 * (j.b + 1))
                chain.mark(dve.scalar_tensor_tensor(gact[:, 0], gact[:, 0], 1.0, cT[:, :, :], ALU.add, ALU.mult))
                chain.link(dve.scalar_tensor_tensor(gact[:, 1], gact[:, 1], 1.0, gact[:, 2], ALU.add, ALU.mult))
                chain.link(dve.tensor_tensor(gact[:, 0], gact[:, 0], gact[:, 1], ALU.add))
                dve.tensor_scalar(cT[:, :, :], gact[:, 0], 0.5, None, ALU.mult).then_inc(sem("c_new"), 1)

            def xo_out(self, j):
                wait(self.dve, sem("tail_mm"), j.tail + 1)
                self.dve.tensor_copy(xo[:, bass.ds(TT * j.b, TT), :], bk(g[0], TT)).then_inc(sem("tail_out"), 1)

            def logits(self, j):
                wait(self.dve, sem("tail_mm"), j.tail + 1)
                self.dve.tensor_copy(lg[:, bass.ds(TT * j.b, TT), :],
                                     g[1][:, 0:TT * E].rearrange("p (a e) -> p a e", a=TT)).then_inc(sem("tail_out"), 1)

            def alone(self, j):
                self.front_start(j)
                self.front_stats(j)
                self.front_apply(j)
                self.v_out(j, 1)

            def step(self, k, front, mid, back, tail):
                if front:
                    self.front_start(front)
                for u in range(UNITS):
                    if mid:
                        self.maximum(mid, u)
                    if u == 0:
                        if tail:
                            self.tail_stats(tail)
                        if front:
                            self.front_stats(front)
                    if u == 1:
                        if tail:
                            self.tail_apply(tail)
                        if front:
                            self.front_apply(front)
                    if tail and tail.kind == "A" and u == 9:
                        self.recur(tail)
                    if tail and tail.kind == "A" and u == 11:
                        self.xo_out(tail)
                    if tail and tail.kind == "S" and u == 8:
                        self.logits(tail)
                if mid:
                    self.split_max(mid)
                if back:
                    self.normalise(back)
                if front:
                    self.v_out(front, 0)
                if back:
                    self.residual(back)

            def after(self, j):
                self.tail_stats(j)
                self.tail_apply(j)
                if j.kind == "A":
                    self.recur(j)
                    self.xo_out(j)
                else:
                    self.logits(j)

            def middle(self):
                self.dve.wait_ge(sem("cu_mm"), 1)
                self.dve.tensor_tensor(cu[:, :, :], bk(g[0], TT),
                                       rows[:, R_OF:R_OF + 1, :].to_broadcast([P, TT, D]), ALU.add
                                       ).then_inc(sem("cu_ready"), 1)

        @block.vector
        def _(dve):
            steps = DveSteps(dve)
            chain = steps.chain
            dve.memset(zero, 0.0).then_inc(sem("zero_ready"), 1)
            dve.memset(zeros32[:, :], 0.0)
            dve.wait_ge(ld_small, 16 * 5)
            for q, c in enumerate((C_F, C_I)):
                dve.tensor_scalar(hcols[:, q, :], cols[:, c, :], 0.5, None, ALU.mult)
            dve.tensor_copy(hcols[:, 2, :], cols[:, C_C, :]).then_inc(sem("hcols"), 1)
            dve.tensor_copy(cT[:, :, :], cols[:, C_IN, :].rearrange("p (k o) -> p k o", o=1
                                                                    ).to_broadcast([P, KT, S])).then_inc(sem("c_new"), 1)
            dve.wait_ge(sem("tg_ready"), 1)
            dve.wait_ge(sem("slots_zero"), 16)
            schedule(dve, steps)

            dve.wait_ge(sem("tail_out"), 2 * B)
            for i in range(NT):
                chain.mark(dve.max(top[:, i, :], lg[:, i, :]))
            chain.wait()
            for i in range(NT):
                chain.mark(dve.max_index(topi[:, i, :], top[:, i, :], lg[:, i, :]))
            chain.wait()
            dve.tensor_tensor(ex[:, :, :], top[:, :, :], top[:, :, 0:1].to_broadcast([P, NT, 8]), ALU.subtract
                              ).then_inc(sem("router_shift"), 1)
            chain.link(dve.tensor_copy(idxf[:, :, :], topi[:, :, 0:2].rearrange("p t w -> p w t")))
            dve.wait_ge(sem("pool_const"), 6)
            for w in range(2):
                dve.tensor_tensor(mask[:, w], iota[:, :].rearrange("p (o e) -> p o e", o=1).to_broadcast([P, NT, E]),
                                  idxf[:, w, :].rearrange("p (t o) -> p t o", o=1).to_broadcast([P, NT, E]),
                                  ALU.is_equal).then_inc(sem("masks"), 1)
            dve.wait_ge(sem("counts"), 2)
            tile_counts = g[1][:, 0:2 * NT * E].rearrange("p (j e) -> p j e", e=E)
            before = g[0][:, 0:2 * NT * E].rearrange("p (j e) -> p j e", e=E)
            for e in range(E):
                chain.mark(dve.tensor_tensor_scan(inc[:, :, e], zeros32[:, :], tile_counts[:, :, e], 0.0,
                                                  ALU.add, ALU.add))
            chain.wait()
            chain.link(dve.tensor_tensor(inc[:, :, :], inc[:, :, :], tile_counts, ALU.subtract))
            chain.link(dve.tensor_tensor(loc[:, :, :], inc[:, :, :], before, ALU.add))
            chain.link(dve.scalar_tensor_tensor(loc[:, :, :], loc[:, :, :], -1.0,
                                                mask[:, :, :, :].rearrange("p w t e -> p (w t) e"), ALU.add, ALU.mult))
            chain.link(dve.tensor_reduce(pos[:, :], loc[:, :, :], AX.X, ALU.add))
            iw = idxf[:, :, :].rearrange("p w t -> p (w t)")
            vw = valid[:, :, :].rearrange("p w t -> p (w t)")
            chain.mark(dve.tensor_scalar(vw, pos[:, :], float(C), None, ALU.is_lt))
            chain.link(dve.tensor_scalar(slotf[:, :], pos[:, :], float(C), float(E * C), ALU.is_ge, ALU.mult))
            chain.link(dve.tensor_tensor(slotf[:, :], slotf[:, :], pos[:, :], ALU.add))
            chain.link(dve.scalar_tensor_tensor(slotf[:, :], iw, float(C), slotf[:, :], ALU.mult, ALU.add))
            chain.mark(dve.tensor_copy(sidx[:, :], slotf[:, :]))
            chain.link(dve.tensor_scalar(slotg[:, :], pos[:, :], float(C - 1), None, ALU.min))
            chain.link(dve.scalar_tensor_tensor(slotg[:, :], iw, float(C), slotg[:, :], ALU.mult, ALU.add))
            dve.tensor_copy(gidx[:, :], slotg[:, :]).then_inc(sem("slots_ready"), 1)
            dve.wait_ge(sem("router_exp"), 1)
            chain.link(dve.tensor_reduce(sums[:, :], ex[:, :, :], AX.X, ALU.add))
            chain.link(dve.reciprocal(sums[:, :], sums[:, :]))
            chain.link(dve.tensor_tensor(prob[:, :, :], ex[:, :, 0:2].rearrange("p t w -> p w t"),
                                         sums[:, :].rearrange("p (o t) -> p o t", o=1).to_broadcast([P, 2, NT]), ALU.mult))
            chain.link(dve.tensor_tensor(prob[:, :, :], prob[:, :, :], valid[:, :, :], ALU.mult))
            chain.link(dve.tensor_tensor(den[:, :], prob[:, 0, :], prob[:, 1, :], ALU.add))
            chain.link(dve.tensor_scalar(den[:, :], den[:, :], EPS_F32, None, ALU.max))
            chain.link(dve.reciprocal(den[:, :], den[:, :]))
            chain.link(dve.tensor_tensor(gate[:, :, :], prob[:, :, :],
                                         den[:, :].rearrange("p (o t) -> p o t", o=1).to_broadcast([P, 2, NT]), ALU.mult))
            chain.link(dve.tensor_scalar(gate[:, :, :], gate[:, :, :], KEEP, None, ALU.mult))

            def expert(e, par, prev):
                for s in range(CT):
                    dve.wait_ge(sem("down_mm"), CT * e + s + 1)
                    if prev:
                        dve.wait_ge(sem("y_out"), 16 * (e - 1))
                    dve.tensor_tensor(yb[par][:, s:s + 1, :], po[s % 2][:, 0:D].rearrange("p (o d) -> p o d", o=1),
                                      b2r[:, bass.ds(e, 1), :], ALU.add).then_inc(sem("y_ready"), 1)

            dve.wait_ge(sem("b2_in"), 16)
            expert(0, 0, False)
            expert(1, 1, False)
            with dve.Fori(1, E // 2) as i:
                for par in range(2):
                    expert(2 * i + par, par, True)

            for i in range(NT):
                dve.wait_ge(sem(f"gathered{i}"), 32)
                for w in range(2):
                    chain.link(dve.scalar_tensor_tensor(x4[:, i, :], yg[:, 2 * i + w, :], gate[:, w, i:i + 1],
                                                        x4[:, i, :], ALU.mult, ALU.add))
                dve.scalar_tensor_tensor(x4[:, i, :], x4[:, i, :], tg[:, 3:4], x[:, i, :], ALU.mult, ALU.add
                                         ).then_inc(sem("final"), 1)

        class PeSteps:
            def __init__(self, pe):
                self.pe = pe
                self.read = [None, None]

            def enter(self, k, name, i):
                self.read = [(sem("residual"), k), (sem("ot_sb"), k)]

            def leave(self, name):
                pass

            def left(self, k, name, count):
                self.read = [(sem("residual"), k), (sem("ot_sb"), k)]

            def claim(self, i, reader, value):
                if self.read[i]:
                    wait(self.pe, *self.read[i])
                self.read[i] = (sem(reader), value)
                return g[i]

            def project(self, bank_, w, moving, cols_=None):
                for m in range(KT):
                    for k in range(KT):
                        ins = self.pe.matmul(bk(bank_, KT)[:, m, :], weights[:, w, k, P * m:P * (m + 1)],
                                             moving[:, k, :], start=k == 0, stop=k == KT - 1)
                return ins

            def project_rows(self, bank_, w, still):
                for q in range(TT):
                    for k in range(KT):
                        ins = self.pe.matmul(bk(bank_, TT)[:, q, :], still[:, k, P * q:P * (q + 1)],
                                             weights[:, w, k, :], start=k == 0, stop=k == KT - 1)
                return ins

            def transpose_rows(self, bank_, src):
                for q in range(TT):
                    for k in range(KT):
                        ins = self.pe.transpose(bk(bank_, KT)[:, k, P * q:P * (q + 1)],
                                                src[:, q, P * k:P * (k + 1)], ident[:, :])
                return ins

            def front_T(self, j):
                wait(self.pe, sem("front_h"), j.n + 1)
                self.transpose_rows(self.claim(0, "front_hT", j.n + 1), hN).then_inc(sem("front_tr"), 1)

            def qk(self, j, q):
                pe = self.pe
                if j.kind != "S" and q == 1:
                    wait(pe, sem("context_in"), 16 * (j.load + 1))
                if q == 0:
                    wait(pe, sem("front_hT"), j.n + 1)
                src = hT if q == 0 or j.kind == "S" else ctxT
                b_ = self.claim(1 - q, "qk_full", 2 * j.n + q + 1)
                self.project(b_, WEIGHTS[j.kind][q], src).then_inc(sem("qk_mm"), 1)

            def v(self, j, i):
                b_ = self.claim(i, "v_sb", j.n + 1)
                src = hT if j.kind == "S" else ctxT
                self.project_rows(b_, WEIGHTS[j.kind][2], src).then_inc(sem("v_mm"), 1)

            def scores1(self, j, u):
                pe = self.pe
                if u == 0:
                    wait(pe, sem("stacked"), 16 * 2 * SLOTS * (j.n + 1))
                wait(pe, sem("max"), UNITS * j.n + u - 1)
                hp, q = u // 2, u % 2
                for a in range(2):
                    h = 2 * hp + a
                    ins = pe.matmul(bk(p1[u % 2], 2)[:, a, :], qs[0:KROWS, j.par, h, P * q:P * (q + 1)],
                                    ks[0:KROWS, j.par, h, :], start=True, stop=True)
                ins.then_inc(sem("scores1"), 1)

            def scores2(self, j, u):
                pe = self.pe
                if u == 0:
                    wait(pe, sem("nmax_in"), 16 * MROWS * (j.n + 1))
                wait(pe, sem("exp"), UNITS * j.n + u - 1)
                hp, kt = u // 2, u % 2
                for a in range(2):
                    h = 2 * hp + a
                    ins = pe.matmul(bk(p2[u % 2], 2)[:, a, :], ks[0:KROWS + MROWS, j.par, h, P * kt:P * (kt + 1)],
                                    qs[0:KROWS + MROWS, j.par, h, :], start=True, stop=True)
                ins.then_inc(sem("scores2"), 1)

            def pv(self, j, q):
                pe = self.pe
                if q == 0:
                    wait(pe, sem("v_sb"), j.n + 1)
                wait(pe, sem("exp"), UNITS * j.n + 4 * (q + 1))
                wait(pe, sem("o_sb"), 4 * j.n + q - 1)
                for kt in range(TT):
                    for a in range(4):
                        u = 4 * q + 2 * (a // 2) + kt
                        ins = pe.matmul(po[q % 2][32 * a:32 * a + 32, 0:S], vv[:, j.par, kt, 4 * q + a, :],
                                        ring[:, u % RING, a % 2, :], start=kt == 0, stop=kt == TT - 1,
                                        skip_group_check=True)
                ins.then_inc(sem("pv"), 1)

            def nmax_T(self, j):
                pe = self.pe
                wait(pe, sem("nmaxb"), j.n + 1)
                b_ = self.claim(1, "nmax_sb", j.n + 1)
                for q in range(TT):
                    ins = pe.transpose(b_[0:32, 0:P].bitcast(BF16)[:, P * q:P * (q + 1)],
                                       nmaxb[:, q].rearrange("p r h -> p (r h)"), identb[:, :])
                ins.then_inc(sem("nmax_tr"), 1)

            def o_T(self, j):
                pe = self.pe
                wait(pe, sem("o_sb"), 4 * (j.n + 1))
                for q in range(TT):
                    b_ = self.claim(q, "on", 2 * j.n + q + 1)
                    for a in range(4):
                        ins = pe.transpose(b_[:, P * a:P * (a + 1)], os_[:, a, P * q:P * (q + 1)], ident[:, :])
                    ins.then_inc(sem("o_tr"), 1)

            def on_T(self, j):
                wait(self.pe, sem("on"), 2 * (j.n + 1))
                self.transpose_rows(self.claim(1, "ot_sb", j.n + 1), on).then_inc(sem("on_tr"), 1)

            def out_proj(self, j):
                wait(self.pe, sem("ot_sb"), j.n + 1)
                self.project_rows(self.claim(0, "residual", j.n + 1), WEIGHTS[j.kind][3], ot
                                  ).then_inc(sem("proj_mm"), 1)

            def tail_T(self, j):
                wait(self.pe, sem("tail_h"), j.tail + 1)
                self.transpose_rows(self.claim(1, "tail_hT", j.tail + 1), tN).then_inc(sem("tail_tr"), 1)

            def recur(self, j, q):
                pe = self.pe
                if q == 0:
                    wait(pe, sem("tail_hT"), j.tail + 1)
                    wait(pe, sem("c_new"), j.b + 1)
                b_ = self.claim((q + 1) % 2, "gates", 3 * j.b + q + 1)
                for m in range(KT):
                    for i, (w, src) in enumerate(((W_F + 2 * q, tT), (W_UF + 2 * q, cT))):
                        for k in range(KT):
                            ins = pe.matmul(bk(b_, KT)[:, m, :], weights[:, w, k, P * m:P * (m + 1)],
                                            src[:, k, :], start=i + k == 0, stop=i + k == 2)
                ins.then_inc(sem("gates_mm"), 1)

            def xo(self, j):
                self.project_rows(self.claim(0, "tail_out", j.tail + 1), W_OX, tT).then_inc(sem("tail_mm"), 1)

            def logits(self, j):
                pe = self.pe
                wait(pe, sem("tail_hT"), j.tail + 1)
                b_ = self.claim(1, "tail_out", j.tail + 1)
                for q in range(TT):
                    for k in range(KT):
                        ins = pe.matmul(b_[:, E * q:E * (q + 1)], tT[:, k, P * q:P * (q + 1)], wr[:, k, :],
                                        start=k == 0, stop=k == KT - 1)
                ins.then_inc(sem("tail_mm"), 1)

            def alone(self, j):
                self.front_T(j)
                self.qk(j, 0)
                self.qk(j, 1)
                self.v(j, 1)
                for r in self.read:
                    if r:
                        wait(self.pe, *r)

            def step(self, k, front, mid, back, tail):
                for u in range(UNITS):
                    if mid:
                        self.scores1(mid, u)
                    if back:
                        self.scores2(back, u)
                    if tail and u == 2:
                        self.tail_T(tail)
                    if front and u == 3:
                        self.front_T(front)
                    if front and u in (5, 6):
                        self.qk(front, u - 5)
                    if tail and tail.kind == "A" and u in (7, 8, 9):
                        self.recur(tail, u - 7)
                    if tail and tail.kind == "A" and u == 11:
                        self.xo(tail)
                    if tail and tail.kind == "S" and u == 8:
                        self.logits(tail)
                    if back and u in (6, 10, 14):
                        self.pv(back, (u - 6) // 4)
                if back:
                    self.pv(back, 3)
                if mid:
                    self.nmax_T(mid)
                if back:
                    self.o_T(back)
                if front:
                    self.v(front, 0)
                if back:
                    self.on_T(back)
                    self.out_proj(back)

            def after(self, j):
                self.tail_T(j)
                if j.kind == "A":
                    for q in range(3):
                        self.recur(j, q)
                    self.xo(j)
                else:
                    self.logits(j)

            def middle(self):
                wait(self.pe, sem("c_new"), B + 1)
                self.project_rows(self.claim(0, "cu_ready", 1), W_UO, cT).then_inc(sem("cu_mm"), 1)

        @block.tensor
        def _(pe):
            pe.wait_ge(sem("pool_const"), 6)
            pe.wait_ge(sem("pool_chain"), 5)
            pe.wait_ge(ld_w0, 16)
            pe.wait_ge(ld_w1, 16)
            pe.wait_ge(ld_small, 16 * 5)
            steps = PeSteps(pe)
            schedule(pe, steps)

            pe.wait_ge(sem("masks"), 2)
            mk = mask[:, :, :, :].rearrange("p w t e -> p (w t e)")
            for i, still in enumerate((tri, ones)):
                b_ = steps.claim(i, "slots_ready", 1)
                pe.matmul(b_[:, 0:2 * NT * E], still[:, :], mk, start=True, stop=True).then_inc(sem("counts"), 1)
            pe.wait_ge(sem("slots_ready"), 1)

            def expert(e, par, prev, loads):
                pe.wait_ge(sem(f"slots_in{par}"), 16 * (loads + 1))
                if prev:
                    pe.wait_ge(sem("slots_T"), KT * e)
                for k in range(KT):
                    for s in range(CT):
                        ins = pe.transpose(g[k][:, P * s:P * (s + 1)], br[par][:, s, P * k:P * (k + 1)], ident[:, :])
                    ins.then_inc(sem("slots_tr"), 1)
                pe.wait_ge(sem(f"w1_in{par}"), 16 * (loads + 1))
                pe.wait_ge(sem("slots_T"), KT * (e + 1))
                for f in range(FT):
                    if prev or f >= 4:
                        pe.wait_ge(sem("hidden"), FT * e + f - 3)
                    for k in range(KT):
                        ins = pe.matmul([p1, p2][f // 2 % 2][f % 2][:, :], w1s[:, par, k, P * f:P * (f + 1)],
                                        bT[:, k, :], start=k == 0, stop=k == KT - 1)
                    ins.then_inc(sem("up_mm"), 1)
                pe.wait_ge(sem(f"w2_in{par}"), 16 * (loads + 1))
                pe.wait_ge(sem("hidden"), FT * (e + 1))
                for s in range(CT):
                    if prev or s >= 2:
                        pe.wait_ge(sem("y_ready"), CT * e + s - 1)
                    for f in range(FT):
                        ins = pe.matmul(po[s % 2][:, 0:D], hid[:, f, P * s:P * (s + 1)], w2s[:, par, f, :],
                                        start=f == 0, stop=f == FT - 1)
                    ins.then_inc(sem("down_mm"), 1)

            expert(0, 0, False, 0)
            expert(1, 1, True, 0)
            with pe.Fori(1, E // 2) as i:
                for par in range(2):
                    expert(2 * i + par, par, True, i)


INS = ["x", "ctxT", "weights", "cols", "rows", "gates", "b1", "wr", "w1", "w2", "b2"]


def kernel(x, ctx_1024, g_xattn, g_ffn, **p):
    import numpy as np
    import concourse.bacc as bacc
    from concourse.bass_utils import run_bass_kernel_spmd

    a = {k: np.asarray(v) for k, v in p.items()}
    weights = [a["L0_xattn_Wq"].T, a["L0_xattn_Wk"].T, a["L0_xattn_Wv"].T, a["L0_xattn_Wo"].T]
    for gate in "fic":
        weights += [a[f"L0_ffn_w{gate}"].T, a[f"L0_ffn_u{gate}"].T]
    weights += [a["L0_ffn_wo"].T, a["L0_ffn_uo"].T]
    weights += [a[f"L1_xattn_W{w}"] for w in "qkvo"] + [a[f"L1_ffn_w{w}"] for w in "qkvo"]
    cols = [a[n] for n in ("L0_xattn_bq", "L0_xattn_bk", "L0_ffn_bf", "L0_ffn_bi", "L0_ffn_bc", "L0_ffn_in_c",
                           "L1_xattn_bq", "L1_xattn_bk", "L1_ffn_bq", "L1_ffn_bk")]
    rows = [a[n] for n in ("L0_xattn_bv", "L0_xattn_bo", "L0_ffn_bo", "L1_xattn_bv", "L1_xattn_bo", "L1_ffn_bv",
                           "L1_ffn_bo", "L1_ffn_ln1_g", "L1_ffn_ln1_b", "L1_ffn_ln2_g", "L1_ffn_ln2_b")]
    given = {
        "x": np.asarray(x),
        "ctxT": np.asarray(ctx_1024)[[*range(B), 0]].transpose(0, 2, 1),
        "weights": np.stack(weights),
        "cols": np.stack(cols).reshape(10 * KT, P).T,
        "rows": np.stack(rows),
        "b2": a["L1_ffn_b2"],
        "gates": np.concatenate([np.asarray(g_xattn), np.asarray(g_ffn)]),
        "b1": a["L1_ffn_b1"].reshape(E * FT, P).T,
        "wr": a["L1_ffn_wr"],
        "w1": a["L1_ffn_w1"],
        "w2": a["L1_ffn_w2"],
    }
    nc = bacc.Bacc("TRN2", target_bir_lowering=False, num_devices=1)
    arrays, t = {}, {}
    for name in INS:
        arr = np.ascontiguousarray(given[name])
        arrays[f"in_{name}"] = arr
        t[name] = nc.dram_tensor(f"in_{name}", arr.shape, mybir.dt.from_np(arr.dtype), kind="ExternalInput").ap()
    t["out"] = nc.dram_tensor("out_x", (B, S, D), F32, kind="ExternalOutput").ap()
    flamingo(nc, t)
    return run_bass_kernel_spmd(nc, [arrays], core_ids=[0]).results[0]["out_x"]
```

```python
from contextlib import ExitStack

import concourse.bass as bass
from concourse import mybir

F32 = mybir.dt.float32
BF16 = mybir.dt.bfloat16
U32 = mybir.dt.uint32
ALU = mybir.AluOpType
ACT = mybir.ActivationFunctionType
AX = mybir.AxisListType

P = 128
B, S, D = 8, 256, 256
H, DK = 16, 16
TT = S // P
KT = D // P
NT = B * TT
E, F, C = 8, 1024, 512
FT = F // P
CT = C // P
EPS_LN = 1e-5
EPS_F32 = 1.1920928955078125e-07
SCALE = 0.25
KEEP = 0.8
SLOTS = 6
RUNS = ((0, 3), (3, 2), (5, 1))
KROWS = SLOTS * DK
MROWS = 2
UNITS = 16
RING = 8

(W_Q0, W_K0, W_V0, W_O0, W_F, W_UF, W_I, W_UI, W_C, W_UC, W_OX, W_UO,
 W_Q1, W_K1, W_V1, W_O1, W_QS, W_KS, W_VS, W_OS) = range(20)
(C_Q0, C_K0, C_F, C_I, C_C, C_IN, C_Q1, C_K1, C_QS, C_KS) = range(10)
(R_V0, R_O0, R_OF, R_V1, R_O1, R_VS, R_OS, R_G1, R_B1, R_G2, R_B2, R_E) = range(12)
LAG = 3
SLOTS_OF = UNITS + LAG
AT_QK = (-1, 1)
AT_TAIL_STATS, AT_TAIL_APPLY, AT_LOGITS, AT_GATES, AT_RECUR, AT_XO = 0, 3, 11, (7, 9, 11), 12, 14
AT_TAIL_T = {"A": 6, "S": 8}
AT_MID = (3, 5)
AT_NEXT_SUM, AT_NEXT_STATS, AT_NEXT_VAR, AT_NEXT_APPLY, AT_NEXT_AGAIN = 7, 9, 10, 12, 14
AT_PV = (5, 9, 13, 16)
G_FRONT, G_QK, G_V, G_NMAX, G_ON, G_OUT, G_TAIL, G_GATES, G_XO, G_LOGITS = 1, 1, 0, 1, 0, 0, 0, (1, 0, 1), 0, 0
G_O = (1, 0)
WEIGHTS = {"A": (W_Q0, W_K0, W_V0, W_O0), "X": (W_Q1, W_K1, W_V1, W_O1), "S": (W_QS, W_KS, W_VS, W_OS)}
COLS = {"A": (C_Q0, C_K0), "X": (C_Q1, C_K1), "S": (C_QS, C_KS)}
ROWS = {"A": (R_V0, R_O0), "X": (R_V1, R_O1), "S": (R_VS, R_OS)}


class Job:

    def __init__(self, n, kind, b, par, order=(0, 1)):
        self.n, self.kind, self.b, self.par = n, kind, b, par
        self.order = order
        self.tail = b if kind == "A" else B + b
        self.load = b if kind == "A" else B + b


def job(n, kind, b, order=(0, 1)):
    return Job(n, kind, b, n % 2, order)


def schedule(eng, steps):
    A = [job(n, "A", n) for n in range(B)]
    steps.alone(A[0], A[1])
    steps.step(-1, A[1], A[0], None, None, A[2])
    steps.step(0, A[2], A[1], A[0], None, A[3])
    with eng.Fori(0, 2) as i:
        for half in range(2):
            k = 2 * i + 1 + half
            if half == 0:
                steps.enter(k, "A", i)
            front, mid, back, prev, nxt = (Job(k + d, "A", k + d, (1 + half + d) % 2) for d in (2, 1, 0, -1, 3))
            steps.step(k, front, mid, back, prev, nxt)
        steps.leave("A")
    steps.left(5, "A", 2)
    steps.step(5, A[7], A[6], A[5], A[4], None)
    steps.step(6, None, A[7], A[6], A[5], None)
    X0 = job(B, "X", 0, (1, 0))
    steps.early(X0)
    steps.step(7, None, None, A[7], A[6], None)
    steps.early_end(X0)
    steps.after(A[7])
    steps.middle()

    X = [X0] + [job(B + b if b < 4 else 5 + 2 * b, "X", b) for b in range(1, B)]
    T = [job(12 + 2 * b if b < 5 else 16 + b, "S", b) for b in range(B)]
    steps.alone(X[0], X[1])
    steps.step(7, X[1], X[0], None, None, X[2])
    steps.step(8, X[2], X[1], X[0], None, X[3])
    steps.step(9, X[3], X[2], X[1], X[0], T[0])
    steps.step(10, T[0], X[3], X[2], X[1], X[4])
    steps.step(11, X[4], T[0], X[3], X[2], T[1])
    with eng.Fori(0, 3) as i:
        k = 2 * i + 12
        steps.enter(k, "B", i)
        steps.step(k, Job(k + 2, "S", i + 1, 0), Job(k + 1, "X", i + 4, 1), Job(k, "S", i, 0),
                   Job(k - 1, "X", i + 3, 1), Job(k + 3, "X", i + 5, 1))
        k = 2 * i + 13
        steps.step(k, Job(k + 2, "X", i + 5, 1), Job(k + 1, "S", i + 1, 0), Job(k, "X", i + 4, 1),
                   Job(k - 1, "S", i, 0), Job(k + 3, "S", i + 2, 0))
        steps.leave("B")
    steps.left(18, "B", 3)
    steps.step(18, T[4], X[7], T[3], X[6], T[5])
    steps.step(19, T[5], T[4], X[7], T[3], T[6])
    steps.step(20, T[6], T[5], T[4], X[7], T[7])
    steps.step(21, T[7], T[6], T[5], T[4], None)
    steps.step(22, None, T[7], T[6], T[5], None)
    steps.step(23, None, None, T[7], T[6], None)
    steps.after(T[7])


def wait(eng, sem, value):
    if isinstance(value, int) and value <= 0:
        return
    eng.wait_ge(sem, value)


def settle(eng, sem):
    eng.sem_inc(sem, 1)


class Chain:

    def __init__(self, eng, sem, per):
        self.eng, self.sem, self.per = eng, sem, per
        self.base, self.n = 0, 0

    def mark(self, ins):
        ins.then_inc(self.sem, 1)
        self.n += 1

    def wait(self):
        self.eng.wait_ge(self.sem, self.base + self.n)

    def link(self, ins):
        self.mark(ins)
        self.wait()

    def enter(self, name, i):
        self.start = self.base + self.n
        self.base, self.n = self.start + self.per[name] * i, 0

    def leave(self, name):
        assert self.n == self.per[name], (name, self.n)

    def left(self, name, count):
        self.base, self.n = self.start + self.per[name] * count, 0


def flamingo(nc, t):
    ctx = ExitStack()
    with ctx:
        def sb(name, shape, dt=F32):
            return ctx.enter_context(nc.sbuf_tensor("sb_" + name, shape, dt))

        def bank(name):
            return ctx.enter_context(nc.psum_tensor("ps_" + name, [P, 512], F32))

        sems = {}

        def sem(name):
            if name not in sems:
                sems[name] = ctx.enter_context(nc.semaphore(name))
            return sems[name]

        weights = sb("weights", [P, 20, KT, D])
        cols = sb("cols", [P, 10, KT])
        rows = sb("rows", [P, R_E, D])
        b1c = sb("b1c", [P, E, FT])
        wr = sb("wr", [P, KT, E])
        gates_in = sb("gates_in", [P, 4])
        tg = sb("tg", [P, 4])
        x = sb("x", [P, NT, D])
        x4 = sb("x4", [P, NT, D])
        xo = sb("xo", [P, NT, D])
        h2 = xo
        ctxT = sb("ctxT", [P, KT, S])
        hN = sb("hN", [P, TT, D])
        hT = sb("hT", [P, KT, S])
        tN = sb("tN", [P, TT, D])
        tT = sb("tT", [P, KT, S])
        stats = sb("stats", [P, 2, TT, 6])
        mv = sb("mv", [P, 2, TT, 2])
        ve = sb("ve", [P, 3, TT])
        rec = sb("rec", [P, TT])
        rstd = sb("rstd", [P, 3, TT])
        minus_half = sb("minus_half", [P, 2, TT])
        full = sb("full", [P, 2, KT, S])
        parts = sb("parts", [P, 3, 2, KT, S], BF16)
        qs = sb("qs", [P, 2, H, S], BF16)
        ks = sb("ks", [P, 2, H, S], BF16)
        vv = sb("vv", [P, 2, TT, H, 32])
        nmax = sb("nmax", [P, TT, H])
        nmaxb = sb("nmaxb", [P, TT, MROWS, H], BF16)
        nmt = sb("nmt", [32, S], BF16)
        ring = sb("ring", [P, RING, 2, S])
        os_ = sb("os", [P, 4, S])
        rden = sb("rden", [P, TT, H])
        on = sb("on", [P, TT, D])
        ot = sb("ot", [P, KT, S])
        res = sb("res", [P, TT, D])
        cT = sb("cT", [P, KT, S])
        gact = sb("gact", [P, 3, KT, S])
        tS = gact[:, 0]
        cu = sb("cu", [P, TT, D])
        xt = sb("xt", [P, TT, D])
        lg = sb("lg", [P, NT, E])
        ident = sb("ident", [P, P])
        identb = sb("identb", [P, P], BF16)

        p1 = [bank("p1a"), bank("p1b")]
        p2 = [bank("p2a"), bank("p2b")]
        po = [bank("poa"), bank("pob")]
        g = [bank("g0"), bank("g1")]

        def bk(t_, a):
            return t_[:, :].rearrange("p (a c) -> p a c", a=a)

        parts_dram = nc.dram_tensor("parts_dram", (2, 3 * DK, H * S), BF16, kind="Internal").ap()
        buf_dram = nc.dram_tensor("buf_dram", (E * C, D), F32, kind="Internal").ap()
        y_dram = nc.dram_tensor("y_dram", (E * C, D), F32, kind="Internal").ap()

        w1s = qs[:, :, :, :].rearrange("p a h s -> p (a h s)").bitcast(F32).rearrange(
            "p (a k f) -> p a k f", a=2, k=KT)
        w2s = ks[:, :, :, :].rearrange("p a h s -> p (a h s)").bitcast(F32).rearrange(
            "p (a k f) -> p a k f", a=2, k=FT)
        arena = weights[:, :, :, :].rearrange("p a k n -> p (a k) n")
        br = [arena[:, 4 * i:4 * i + 4, :] for i in range(2)]
        bT = arena[:, 8:12, :].rearrange("p (k a) n -> p k (a n)", k=KT)
        yb = [arena[:, 12 + 4 * i:16 + 4 * i, :] for i in range(2)]
        b2r = arena[:, 32:40, :]
        yg = arena[:, 0:32, :]
        hid = ring[:, :, :, :].rearrange("p a b c -> p a (b c)")
        zero = sb("zero", [P, 1, D])

        (ld_small, ld_w0, ld_w1, ld_x0, ld_x1) = [sem(s) for s in
                                                  ("ld_small", "ld_w0", "ld_w1", "ld_x0", "ld_x1")]
        NSMALL = 6

        block = ctx.enter_context(nc.Block())

        class SpSteps:
            def __init__(self, sp):
                self.sp = sp

            def enter(self, k, name, i):
                pass

            def leave(self, name):
                pass

            def left(self, k, name, count):
                pass

            def load_context(self, b):
                src = t["ctxT"].rearrange("b (k p) s -> b p k s", p=P)
                self.sp.dma_start(ctxT[:, :, :], src[bass.ds(b, 1)].rearrange("o p k s -> (o p) k s")
                                  ).then_inc(sem("context_in"), 16)

            def parts_out(self, j, q):
                sp = self.sp
                wait(sp, sem("split"), 2 * j.n + j.order[q] + 1)
                settle(sp, sem("sp_passed"))
                if j.order[q] == 0:
                    wait(sp, sem("stacked"), 16 * 2 * len(RUNS) * j.n)
                    settle(sp, sem("sp_passed"))
                sp.dma_start(parts_dram[q].rearrange("(a d) (g x) -> (d g) a x", a=3, g=H // KT),
                             parts[:, :, q, :, :].rearrange("p a m c -> p a (m c)")
                             ).then_inc(sem("parts_out"), 16)

            def stack(self, j, qk=(0, 1)):
                sp = self.sp
                wait(sp, sem("parts_out"), 32 * j.n + 16 * (j.order[qk[-1]] + 1))
                settle(sp, sem("sp_passed"))
                wait(sp, sem("scores2"), UNITS * (j.n - 1))
                settle(sp, sem("sp_passed"))
                for r, (s, n) in enumerate(RUNS):
                    for q in qk:
                        src = (parts_dram[0, 0:DK * n] if q == 0 else
                               bass.AP(parts_dram.tensor, parts_dram[1, DK * r:DK * (r + 1)].offset,
                                       [[0, n], [H * S, DK], [1, H * S]]))
                        sp.dma_start((qs, ks)[q][DK * s:DK * (s + n), j.par, :, :].rearrange("p h c -> p (h c)"),
                                     src).then_inc(sem("stacked"), 16)

            def early(self, j):
                pass

            def early_end(self, j):
                self.parts_out(j, 1)
                self.stack(j, (1,))
                self.next_context(j)

            def next_context(self, j):
                if j.kind == "S":
                    return
                wait(self.sp, sem("v_mm"), j.n + 1)
                settle(self.sp, sem("sp_passed"))
                self.load_context(j.b + 1)

            def alone(self, j, nxt):
                self.parts_out(j, 0)
                if j.order[0] == 1:
                    self.stack(j, (0,))
                    return
                self.parts_out(j, 1)
                self.stack(j)
                self.next_context(j)

            def step(self, k, front, mid, back, prev, nxt):
                sp = self.sp
                if front:
                    self.parts_out(front, 0)
                    self.parts_out(front, 1)
                    self.stack(front)
                if mid:
                    wait(sp, sem("nmax_sb"), mid.n + 1)
                    settle(sp, sem("sp_passed"))
                    for r in range(MROWS):
                        sp.dma_start(qs[KROWS + r:KROWS + r + 1, mid.par, :, :], nmt[H * r:H * (r + 1), :]
                                     ).then_inc(sem("nmax_in"), 16)
                if front:
                    self.next_context(front)

            def after(self, j):
                pass

            def middle(self):
                pass

        @block.sync
        def _(sp):
            sp.dma_start(x[:, 0:TT, :], t["x"][0].rearrange("(t p) d -> p t d", p=P)).then_inc(ld_x0, 16)
            wv = t["weights"].rearrange("w (k p) n -> p w k n", p=P)
            sp.dma_start(weights[:, 0:4, :, :], wv[:, 0:4]).then_inc(ld_w0, 16)
            steps = SpSteps(sp)
            steps.load_context(0)
            sp.dma_start(cols[:, :, :], t["cols"].rearrange("p (a k) -> p a k", k=KT)).then_inc(ld_small, 16)
            rv = t["rows"]
            sp.dma_start(rows[:, :, :].rearrange("p a d -> p (a d)"),
                         bass.AP(rv.tensor, rv.offset, [[0, P], [1, R_E * D]])).then_inc(ld_small, 16)
            gv = t["gates"]
            sp.dma_start(gates_in[:, :], bass.AP(gv.tensor, gv.offset, [[0, P], [1, 4]])).then_inc(ld_small, 16)
            sp.dma_start(b1c[:, :, :], t["b1"].rearrange("p (e f) -> p e f", e=E)).then_inc(ld_small, 16)
            sp.dma_start(wr[:, :, :], t["wr"].rearrange("(k p) e -> p k e", p=P)).then_inc(ld_small, 16)
            sp.dma_start(x[:, TT:NT, :], t["x"][1:B].rearrange("b (t p) d -> p (b t) d", p=P)).then_inc(ld_x1, 16)
            sp.dma_start(weights[:, 4:20, :, :], wv[:, 4:20]).then_inc(ld_w1, 16)
            sp.wait_ge(sem("zero_ready"), 1)
            sp.dma_start(buf_dram.rearrange("(a p) d -> p a d", p=P),
                         zero[:, :, :].to_broadcast([P, E * CT, D])).then_inc(sem("slots_zero"), 16)
            schedule(sp, steps)

            def load_weights(e, par):
                sp.dma_start(w1s[:, par], t["w1"][bass.ds(e, 1)].rearrange("o (k p) f -> p (o k) f", p=P)
                             ).then_inc(sem(f"w1_in{par}"), 16)
                sp.dma_start(w2s[:, par], t["w2"][bass.ds(e, 1)].rearrange("o (k p) f -> p (o k) f", p=P)
                             ).then_inc(sem(f"w2_in{par}"), 16)

            slots = buf_dram.rearrange("(e s p) d -> e p s d", e=E, p=P)
            outs = y_dram.rearrange("(e s p) d -> e p s d", e=E, p=P)

            def load_slots(e, par):
                sp.dma_start(br[par], slots[bass.ds(e, 1)].rearrange("o p s d -> (o p) s d")
                             ).then_inc(sem(f"slots_in{par}"), 16)

            sp.wait_ge(sem("scores2"), UNITS * 3 * B)
            load_weights(0, 0)
            load_weights(1, 1)
            sp.wait_ge(sem("tail_mm"), 2 * B)
            bv = t["b2"]
            sp.dma_start(b2r.rearrange("p e d -> p (e d)"), bass.AP(bv.tensor, bv.offset, [[0, P], [1, E * D]])
                         ).then_inc(sem("b2_in"), 16)
            sp.wait_ge(sem("slots_filled"), 16 * 2 * NT)
            load_slots(0, 0)
            load_slots(1, 1)
            with sp.Fori(0, E // 2 - 1) as i:
                for par in range(2):
                    sp.wait_ge(sem("y_ready"), CT * (2 * i + par + 1))
                    settle(sp, sem("sp_passed"))
                    sp.dma_start(outs[bass.ds(2 * i + par, 1)].rearrange("o p s d -> (o p) s d"), yb[par]
                                 ).then_inc(sem("y_out"), 16)
                    load_weights(2 * i + par + 2, par)
                    load_slots(2 * i + par + 2, par)
            for par in range(2):
                sp.wait_ge(sem("y_ready"), CT * (E - 2 + par + 1))
                sp.dma_start(outs[E - 2 + par], yb[par]).then_inc(sem("y_out"), 16)
            out = t["out"].rearrange("b (t p) d -> p (b t) d", p=P)
            for q in range(4):
                sp.wait_ge(sem("final"), NT // 4 * (q + 1))
                s = slice(NT // 4 * q, NT // 4 * (q + 1))
                sp.dma_start(out[:, s, :], x4[:, s, :]).then_inc(sem("stored"), 16)
            sp.wait_ge(sem("stored"), 64)

        class PoolSteps:
            def __init__(self, pool):
                self.pool = pool
                self.chain = Chain(pool, sem("pool_chain"), {"A": 0, "B": 1})

            def enter(self, k, name, i):
                self.chain.enter(name, i)

            def leave(self, name):
                self.chain.leave(name)

            def left(self, k, name, count):
                self.chain.left(name, count)

            def rstd(self, who, count, kind):
                wait(self.pool, sem(f"{who}_var"), count)
                a, n = (0, 1) if who == "tail" else (1, 2 if kind == "S" else 1)
                self.pool.tensor_tensor(rstd[:, a:a + n, :], ve[:, a:a + n, :], minus_half[:, 0:n, :], ALU.pow
                                        ).then_inc(sem(f"{who}_rstd"), 1)

            def rest(self, j, q):
                wait(self.pool, sem("qk_hi"), 2 * j.n + j.order[q] + 1)
                self.pool.tensor_tensor(full[:, q], full[:, q], parts[:, 0, q], ALU.subtract
                                        ).then_inc(sem("qk_rest"), 1)

            def low(self, j, q):
                wait(self.pool, sem("qk_mid"), 2 * j.n + j.order[q] + 1)
                self.pool.tensor_tensor(parts[:, 2, q], full[:, q], parts[:, 1, q], ALU.subtract
                                        ).then_inc(sem("split"), 1)

            def alone(self, j, nxt):
                self.rstd("front", j.n + 1, j.kind)
                if j.kind == "X":
                    self.rstd("front", nxt.n + 1, nxt.kind)
                for q in range(2):
                    if q == 0 or j.order[0] == 0:
                        self.rest(j, q)
                        self.low(j, q)
                if j.kind == "A":
                    self.rstd("front", nxt.n + 1, nxt.kind)

            def early(self, j):
                self.rest(j, 1)

            def early_end(self, j):
                self.low(j, 1)

            def step(self, k, front, mid, back, prev, nxt):
                tail = prev if prev and prev.kind != "X" else None
                if front:
                    self.rest(front, 0)
                if tail:
                    self.rstd("tail", tail.tail + 1, tail.kind)
                if front:
                    self.rest(front, 1)
                if tail and tail.kind == "S":
                    self.keep(tail)
                if front:
                    self.low(front, 0)
                    self.low(front, 1)
                if nxt:
                    self.rstd("front", nxt.n + 1, nxt.kind)
                    self.shift(nxt)

            def keep(self, j):
                pool, chain = self.pool, self.chain
                wait(pool, sem("tail_norm"), j.b + 1)
                settle(pool, sem("pool_passed"))
                chain.link(pool.tensor_tensor(tN[:, :, :], tN[:, :, :],
                                              rows[:, R_G2:R_G2 + 1, :].to_broadcast([P, TT, D]), ALU.mult))
                wait(pool, sem("tail_tr"), j.tail)
                for dst, done in ((tS[:, :, :], "tail_h"), (h2[:, bass.ds(TT * j.b, TT), :], "kept")):
                    pool.tensor_tensor(dst, tN[:, :, :], rows[:, R_B2:R_B2 + 1, :].to_broadcast([P, TT, D]),
                                       ALU.add).then_inc(sem(done), 1)

            def shift(self, j):
                if j.kind == "S":
                    wait(self.pool, sem("front_scaled"), j.b + 1)
                    settle(self.pool, sem("pool_passed"))
                    self.pool.tensor_tensor(hN[:, :, :], hN[:, :, :],
                                            rows[:, R_B1:R_B1 + 1, :].to_broadcast([P, TT, D]), ALU.add
                                            ).then_inc(sem("front_h"), 1)

            def after(self, j):
                self.rstd("tail", j.tail + 1, j.kind)
                if j.kind == "S":
                    self.keep(j)

            def middle(self):
                pass

        top = sb("top", [P, NT, 8])
        topi = sb("topi", [P, NT, 8], U32)
        idxf = sb("idxf", [P, 2, NT])
        iota = sb("iota", [P, E])
        mask = sb("mask", [P, 2, NT, E], BF16)
        tri = sb("tri", [P, P], BF16)
        ones = sb("ones", [P, P], BF16)
        zeros32 = sb("zeros32", [P, 2 * NT])
        ex = sb("ex", [P, NT, 8])
        sums = sb("sums", [P, NT])
        inc = sb("inc", [P, 2 * NT, E])
        loc = sb("loc", [P, 2 * NT, E])
        pos = sb("pos", [P, 2 * NT])
        valid = sb("valid", [P, 2, NT])
        slotf = sb("slotf", [P, 2 * NT])
        slotg = sb("slotg", [P, 2 * NT])
        sidx = sb("sidx", [P, 2 * NT], U32)
        gidx = sb("gidx", [P, 2 * NT], U32)
        prob = sb("prob", [P, 2, NT])
        den = sb("den", [P, NT])
        gate = sb("gate", [P, 2, NT])

        @block.gpsimd
        def _(pool):
            steps = PoolSteps(pool)
            link = steps.chain.link
            pool.memset(minus_half[:, :, :], -0.5).then_inc(sem("pool_const"), 1)
            link(pool.memset(ident[:, :], 0.0))
            pool.affine_select(out=ident[:, :], in_=ident[:, :], compare_op=ALU.not_equal, fill=1.0, base=0,
                               pattern=[[-1, P]], channel_multiplier=1).then_inc(sem("pool_const"), 1)
            link(pool.memset(identb[:, :], 0.0))
            pool.affine_select(out=identb[:, :], in_=identb[:, :], compare_op=ALU.not_equal, fill=1.0, base=0,
                               pattern=[[-1, P]], channel_multiplier=1).then_inc(sem("pool_const"), 1)
            link(pool.memset(vv[:, :, :, :, DK:], 1.0))
            link(pool.memset(ks[KROWS:, :, :, :], 1.0))
            pool.memset(ones[:, :], 1.0).then_inc(sem("pool_const"), 1)
            link(pool.memset(tri[:, :], 1.0))
            pool.affine_select(out=tri[:, :], in_=tri[:, :], compare_op=ALU.is_ge, fill=0.0, base=0,
                               pattern=[[1, P]], channel_multiplier=-1).then_inc(sem("pool_const"), 1)
            pool.iota(iota[:, :], [[1, E]], base=0, channel_multiplier=0,
                      allow_small_or_imprecise_dtypes=True).then_inc(sem("pool_const"), 1)
            pool.wait_ge(sem("pool_const"), 6)
            pool.wait_ge(sem("pool_chain"), 5)
            schedule(pool, steps)
            pool.wait_ge(sem("slots_zero"), 16)
            pool.wait_ge(sem("kept"), B)
            pool.wait_ge(sem("slots_ready"), 1)
            for w in range(2):
                for i in range(NT):
                    j = w * NT + i
                    pool.indirect_dma_start(buf_dram, bass.IndirectOffsetOnAxis(sidx[:, j:j + 1], 0),
                                            h2[:, i, :], None, bounds_check=E * C - 1, oob_is_err=False
                                            ).then_inc(sem("slots_filled"), 16)
            pool.wait_ge(sem("y_out"), 16 * E)
            for i in range(NT):
                for w in range(2):
                    j = w * NT + i
                    pool.indirect_dma_start(yg[:, 2 * i + w, :], None, y_dram,
                                            bass.IndirectOffsetOnAxis(gidx[:, j:j + 1], 0),
                                            bounds_check=E * C - 1, oob_is_err=False
                                            ).then_inc(sem(f"gathered{i}"), 16)

        class ActSteps:
            def __init__(self, act):
                self.act = act

            def enter(self, k, name, i):
                pass

            def leave(self, name):
                pass

            def left(self, k, name, count):
                pass

            def gate_x(self, j):
                wait(self.act, sem("xo_sum"), j.b + 1)
                self.act.activation(xt[:, :, :], xt[:, :, :], ACT.Tanh).then_inc(sem("xo_tanh"), 1)

            def front_T(self, j):
                wait(self.act, sem("front_tr"), j.n + 1)
                wait(self.act, sem("v_mm"), j.n)
                self.act.activation(hT[:, :, :], bk(g[G_FRONT], KT), ACT.Copy).then_inc(sem("front_hT"), 1)

            def qk(self, j, q):
                wait(self.act, sem("qk_mm"), 2 * j.n + j.order[q] + 1)
                wait(self.act, sem("split"), 2 * j.n)
                for m in range(KT):
                    ins = self.act.activation(full[:, q, m, :], bk(g[G_QK], KT)[:, m, :], ACT.Identity,
                                              bias=cols[:, COLS[j.kind][q], m:m + 1])
                ins.then_inc(sem("qk_full"), 1)

            def mid_part(self, j, q):
                wait(self.act, sem("qk_rest"), 2 * j.n + j.order[q] + 1)
                wait(self.act, sem("parts_out"), 32 * j.n)
                self.act.activation(parts[:, 1, q], full[:, q], ACT.Copy).then_inc(sem("qk_mid"), 1)

            def nmax_sb(self, j):
                wait(self.act, sem("nmax_tr"), j.n + 1)
                wait(self.act, sem("nmax_in"), 16 * MROWS * j.n)
                self.act.activation(nmt[:, :], g[G_NMAX][0:32, 0:P].bitcast(BF16), ACT.Copy
                                    ).then_inc(sem("nmax_sb"), 1)

            def exp(self, j, u):
                act = self.act
                wait(act, sem("scores2"), UNITS * j.n + u + 1)
                if u % 4 == 0:
                    wait(act, sem("pv"), 4 * j.n + u // 4 - 1)
                act.activation(ring[:, u % RING], bk(p2[u % 2], 2), ACT.Exp, scale=SCALE
                               ).then_inc(sem("exp"), 1)

            def o_out(self, j, q):
                wait(self.act, sem("pv"), 4 * j.n + q + 1)
                wait(self.act, sem("o_tr"), 2 * j.n)
                self.act.activation(os_[:, q, :], po[q % 2][:, 0:S], ACT.Copy).then_inc(sem("o_sb"), 1)

            def oT(self, j):
                wait(self.act, sem("on_tr"), j.n + 1)
                wait(self.act, sem("proj_mm"), j.n)
                self.act.activation(ot[:, :, :], bk(g[G_ON], KT), ACT.Copy).then_inc(sem("ot_sb"), 1)

            def tail_T(self, j):
                wait(self.act, sem("tail_tr"), j.tail + 1)
                wait(self.act, sem("tail_mm"), j.tail)
                self.act.activation(tT[:, :, :], bk(g[G_TAIL], KT), ACT.Copy).then_inc(sem("tail_hT"), 1)

            def recur(self, j, q):
                wait(self.act, sem("gates_mm"), 3 * j.b + q + 1)
                wait(self.act, sem("c_new"), j.b + 1)
                for m in range(KT):
                    ins = self.act.activation(gact[:, q, m, :], bk(g[G_GATES[q]], KT)[:, m, :], ACT.Tanh,
                                              bias=hcols[:, q, m:m + 1], scale=0.5 if q < 2 else 1.0)
                ins.then_inc(sem("gates"), 1)

            def alone(self, j, nxt):
                if j.kind == "X":
                    self.gate_x(j)
                self.front_T(j)
                if nxt.kind == "X":
                    self.gate_x(nxt)
                for q in range(2):
                    if q == 0 or j.order[0] == 0:
                        self.qk(j, q)
                        self.mid_part(j, q)

            def early(self, j):
                self.qk(j, 1)

            def early_end(self, j):
                self.mid_part(j, 1)

            def step(self, k, front, mid, back, prev, nxt):
                tail = prev if prev and prev.kind != "X" else None
                if front:
                    self.front_T(front)
                if prev:
                    self.oT(prev)
                if front:
                    self.qk(front, 0)
                for u in range(SLOTS_OF):
                    if back and u < UNITS:
                        self.exp(back, u)
                    if front and u == AT_QK[1]:
                        self.qk(front, 1)
                    if front and u in AT_MID:
                        self.mid_part(front, AT_MID.index(u))
                    if tail and u == AT_TAIL_T[tail.kind]:
                        self.tail_T(tail)
                    if tail and tail.kind == "A" and u in AT_GATES:
                        self.recur(tail, AT_GATES.index(u))
                    if nxt and nxt.kind == "X" and u == AT_NEXT_SUM:
                        self.gate_x(nxt)
                    if back and u in AT_PV:
                        self.o_out(back, AT_PV.index(u))
                if mid:
                    self.nmax_sb(mid)

            def after(self, j):
                self.oT(j)
                self.tail_T(j)
                if j.kind == "A":
                    for q in range(3):
                        self.recur(j, q)

            def middle(self):
                pass

        hcols = sb("hcols", [P, 3, KT])

        @block.scalar
        def _(act):
            act.wait_ge(ld_small, 16 * 5)
            act.activation(tg[:, :], gates_in[:, :], ACT.Tanh).then_inc(sem("tg_ready"), 1)
            act.wait_ge(sem("hcols"), 1)
            schedule(act, ActSteps(act))
            act.wait_ge(sem("router_shift"), 1)
            act.activation(ex[:, :, :], ex[:, :, :], ACT.Exp).then_inc(sem("router_exp"), 1)

            def expert(e, par, prev):
                for h in range(KT):
                    act.wait_ge(sem("slots_tr"), KT * e + h + 1)
                    if prev:
                        act.wait_ge(sem("up_mm"), FT * e)
                    act.activation(bT[:, h, :], g[h][:, :], ACT.Copy).then_inc(sem("slots_T"), 1)
                for f in range(FT):
                    act.wait_ge(sem("up_mm"), FT * e + f + 1)
                    if prev:
                        act.wait_ge(sem("down_mm"), CT * e)
                    act.activation(hid[:, f, :], [p1, p2][f // 2 % 2][f % 2][:, :], ACT.Relu,
                                   bias=b1c[:, bass.ds(e, 1), f:f + 1].rearrange("p e f -> p (e f)")
                                   ).then_inc(sem("hidden"), 1)

            expert(0, 0, False)
            expert(1, 1, True)
            with act.Fori(1, E // 2) as i:
                for par in range(2):
                    expert(2 * i + par, par, True)

        class DveSteps:
            def __init__(self, dve):
                self.dve = dve
                self.chain = Chain(dve, sem("dve_chain"), {"A": 30, "B": 24})

            def enter(self, k, name, i):
                self.chain.enter(name, i)

            def leave(self, name):
                self.chain.leave(name)

            def left(self, k, name, count):
                self.chain.left(name, count)

            def norm_stats(self, w, src, b):
                dve, chain = self.dve, self.chain
                settle(dve, sem("dve_passed"))
                for i in range(TT):
                    chain.mark(dve.bn_stats(stats[:, w, i, :], src[:, bass.ds(TT * b + i, 1), :].rearrange(
                        "p o d -> p (o d)")))

            def norm_var(self, w, who, again=False):
                dve, chain = self.dve, self.chain
                chain.wait()
                settle(dve, sem("dve_passed"))
                for i in range(TT):
                    chain.mark(dve.bn_aggr(mv[:, w, i, :], stats[:, w, i, :]))
                chain.wait()
                ins = dve.tensor_scalar(ve[:, w, :], mv[:, w, :, 1], EPS_LN, None, ALU.add)
                if again:
                    chain.link(ins)
                    chain.link(dve.reciprocal(rec[:, :], ve[:, w, :]))
                    ins = dve.tensor_scalar(ve[:, 2, :], rec[:, :], -EPS_LN, 1.0 + EPS_LN, ALU.mult, ALU.add)
                ins.then_inc(sem(f"{who}_var"), 1)

            def norm_apply(self, w, src, b, dst, ins_b=0):
                for i in range(TT):
                    ins = self.dve.tensor_scalar(dst[:, bass.ds(TT * ins_b + i, 1), :],
                                                 src[:, bass.ds(TT * b + i, 1), :],
                                                 mv[:, w, i, 0:1], rstd[:, w, i:i + 1], ALU.subtract, ALU.mult)
                return ins

            def hi_part(self, j, q):
                wait(self.dve, sem("qk_full"), 2 * j.n + j.order[q] + 1)
                wait(self.dve, sem("split"), 2 * j.n)
                wait(self.dve, sem("parts_out"), 32 * j.n)
                self.dve.tensor_copy(parts[:, 0, q], full[:, q]).then_inc(sem("qk_hi"), 1)

            def early(self, j):
                self.hi_part(j, 1)
                self.v_out(j, G_V)

            def early_end(self, j):
                pass

            def front_start(self, j):
                if j.kind == "X":
                    if isinstance(j.b, int) and j.b == 0:
                        self.dve.wait_ge(sem("cu_ready"), 1)
                    self.dve.tensor_tensor(xt[:, :, :], xo[:, bass.ds(TT * j.b, TT), :], cu[:, :, :], ALU.add
                                           ).then_inc(sem("xo_sum"), 1)

            def front_stats(self, j, k=None):
                dve = self.dve
                if j.kind == "A":
                    if isinstance(j.n, int) and j.n <= 1:
                        dve.wait_ge((ld_x0, ld_x1)[j.n], 16)
                if j.kind == "X":
                    wait(dve, sem("xo_tanh"), j.b + 1)
                    xs = x[:, bass.ds(TT * j.b, TT), :]
                    self.chain.link(dve.scalar_tensor_tensor(xs, xt[:, :, :], tg[:, 2:3], xs, ALU.mult, ALU.add))
                if j.kind == "S":
                    wait(dve, sem("residual"), k)
                self.norm_stats(1, x, j.b)

            def front_apply(self, j):
                dve, chain = self.dve, self.chain
                wait(dve, sem("front_rstd"), j.n + 1)
                wait(dve, sem("front_tr"), j.n)
                if j.kind != "S":
                    self.norm_apply(1, x, j.b, hN).then_inc(sem("front_h"), 1)
                    return
                chain.mark(self.norm_apply(1, x, j.b, x4, j.b))

            def front_again(self, j):
                dve, chain = self.dve, self.chain
                if j.kind != "S":
                    return
                chain.wait()
                for i in range(TT):
                    ins = dve.scalar_tensor_tensor(hN[:, i, :], x4[:, bass.ds(TT * j.b + i, 1), :].rearrange(
                        "p o d -> p (o d)"), rstd[:, 2, i:i + 1], rows[:, R_G1, :], ALU.mult, ALU.mult)
                ins.then_inc(sem("front_scaled"), 1)

            def tail_src(self, j):
                return x if j.kind == "A" else x4

            def tail_stats(self, j):
                wait(self.dve, sem("residual"), j.n + 1)
                self.norm_stats(0, self.tail_src(j), j.b)
                self.norm_var(0, "tail")

            def tail_apply(self, j):
                dve, chain = self.dve, self.chain
                wait(dve, sem("tail_rstd"), j.tail + 1)
                wait(dve, sem("tail_tr"), j.tail)
                if j.kind != "S":
                    self.norm_apply(0, x, j.b, tN).then_inc(sem("tail_h"), 1)
                    return
                wait(dve, sem("kept"), j.b)
                self.norm_apply(0, x4, j.b, tN).then_inc(sem("tail_norm"), 1)

            def maximum(self, j, u):
                dve = self.dve
                hp, q = u // 2, u % 2
                wait(dve, sem("scores1"), UNITS * j.n + u + 1)
                dve.tensor_reduce(nmax[:, q, 2 * hp:2 * hp + 2], bk(p1[u % 2], 2), AX.X, ALU.max, negate=True
                                  ).then_inc(sem("max"), 1)

            def split_max(self, j):
                dve, chain = self.dve, self.chain
                wait(dve, sem("max"), UNITS * (j.n + 1))
                wait(dve, sem("nmax_tr"), j.n)
                chain.link(dve.tensor_copy(nmaxb[:, :, 0, :], nmax[:, :, :]))
                dve.tensor_tensor(nmaxb[:, :, 1, :], nmax[:, :, :], nmaxb[:, :, 0, :], ALU.subtract
                                  ).then_inc(sem("nmaxb"), 1)

            def normalise(self, j):
                dve, chain = self.dve, self.chain
                wait(dve, sem("on_tr"), j.n)
                for q in range(TT):
                    o = g[G_O[q]][:, :].rearrange("p (h c) -> p h c", h=H)
                    wait(dve, sem("o_tr"), 2 * j.n + q + 1)
                    chain.link(dve.reciprocal(rden[:, q, :], o[:, :, DK]))
                    dve.tensor_tensor(on[:, q, :].rearrange("p (h c) -> p h c", h=H), o[:, :, 0:DK],
                                      rden[:, q, :].rearrange("p (h o) -> p h o", o=1).to_broadcast([P, H, DK]),
                                      ALU.mult).then_inc(sem("on"), 1)

            def v_out(self, j, bank_):
                dve = self.dve
                wait(dve, sem("v_mm"), j.n + 1)
                wait(dve, sem("pv"), 4 * (j.n - 1))
                for q in range(TT):
                    ins = dve.tensor_tensor(
                        vv[:, j.par, q, :, 0:DK], bk(g[bank_], TT)[:, q, :].rearrange("p (h c) -> p h c", h=H),
                        rows[:, ROWS[j.kind][0], :].rearrange("p (h c) -> p h c", h=H), ALU.add)
                ins.then_inc(sem("v_sb"), 1)

            def residual(self, j):
                dve, chain = self.dve, self.chain
                wait(dve, sem("proj_mm"), j.n + 1)
                xs = x[:, bass.ds(TT * j.b, TT), :]
                chain.link(dve.tensor_tensor(res[:, :, :], bk(g[G_OUT], TT),
                                             rows[:, ROWS[j.kind][1], :].rearrange("p (o d) -> p o d", o=1
                                                                                   ).to_broadcast([P, TT, D]), ALU.add))
                if j.kind == "S":
                    x4s = x4[:, bass.ds(TT * j.b, TT), :]
                    dve.tensor_tensor(x4s, res[:, :, :], x4s, ALU.add
                                      ).then_inc(sem("residual"), 1)
                else:
                    w = 0 if j.kind == "A" else 1
                    dve.scalar_tensor_tensor(xs, res[:, :, :], tg[:, w:w + 1], xs, ALU.mult, ALU.add
                                             ).then_inc(sem("residual"), 1)

            def recur(self, j):
                dve, chain = self.dve, self.chain
                wait(dve, sem("gates"), 3 * (j.b + 1))
                chain.mark(dve.scalar_tensor_tensor(gact[:, 0], gact[:, 0], 1.0, cT[:, :, :], ALU.add, ALU.mult))
                chain.link(dve.scalar_tensor_tensor(gact[:, 1], gact[:, 1], 1.0, gact[:, 2], ALU.add, ALU.mult))
                chain.link(dve.tensor_tensor(gact[:, 0], gact[:, 0], gact[:, 1], ALU.add))
                dve.tensor_scalar(cT[:, :, :], gact[:, 0], 0.5, None, ALU.mult).then_inc(sem("c_new"), 1)

            def xo_out(self, j):
                wait(self.dve, sem("tail_mm"), j.tail + 1)
                self.dve.tensor_copy(xo[:, bass.ds(TT * j.b, TT), :], bk(g[G_XO], TT)).then_inc(sem("tail_out"), 1)

            def logits(self, j):
                wait(self.dve, sem("tail_mm"), j.tail + 1)
                self.dve.tensor_copy(lg[:, bass.ds(TT * j.b, TT), :],
                                     g[G_LOGITS][:, 0:TT * E].rearrange("p (a e) -> p a e", a=TT)).then_inc(sem("tail_out"), 1)

            def alone(self, j, nxt):
                self.front_start(j)
                self.front_stats(j)
                self.norm_var(1, "front")
                self.front_apply(j)
                if j.kind == "X":
                    self.norm(nxt)
                for q in range(2):
                    if q == 0 or j.order[0] == 0:
                        self.hi_part(j, q)
                if j.kind == "A":
                    self.v_out(j, G_V)
                    self.norm(nxt)

            def norm(self, j):
                self.front_start(j)
                self.front_stats(j)
                self.norm_var(1, "front")
                self.front_apply(j)

            def step(self, k, front, mid, back, prev, nxt):
                tail = prev if prev and prev.kind != "X" else None
                if front:
                    self.hi_part(front, 0)
                if prev:
                    self.residual(prev)
                for u in range(SLOTS_OF):
                    if front and u == AT_QK[1] + 1:
                        self.hi_part(front, 1)
                    if mid and u >= LAG:
                        self.maximum(mid, u - LAG)
                    if tail and u == AT_TAIL_STATS:
                        self.tail_stats(tail)
                    if tail and u == AT_TAIL_APPLY:
                        self.tail_apply(tail)
                    if tail and tail.kind == "A" and u == AT_RECUR:
                        self.recur(tail)
                    if tail and tail.kind == "A" and u == AT_XO:
                        self.xo_out(tail)
                    if tail and tail.kind == "S" and u == AT_LOGITS:
                        self.logits(tail)
                    if nxt and u == AT_NEXT_SUM:
                        self.front_start(nxt)
                    if nxt and u == AT_NEXT_STATS:
                        self.front_stats(nxt, k)
                    if nxt and u == AT_NEXT_VAR:
                        self.norm_var(1, "front", nxt.kind == "S")
                    if nxt and u == AT_NEXT_APPLY:
                        self.front_apply(nxt)
                    if nxt and u == AT_NEXT_AGAIN:
                        self.front_again(nxt)
                if mid:
                    self.split_max(mid)
                if front:
                    self.v_out(front, G_V)
                if back:
                    self.normalise(back)

            def after(self, j):
                self.residual(j)
                self.tail_stats(j)
                self.tail_apply(j)
                if j.kind == "A":
                    self.recur(j)
                    self.xo_out(j)
                else:
                    self.logits(j)

            def middle(self):
                self.dve.wait_ge(sem("cu_mm"), 1)
                self.dve.tensor_tensor(cu[:, :, :], bk(g[0], TT),
                                       rows[:, R_OF:R_OF + 1, :].to_broadcast([P, TT, D]), ALU.add
                                       ).then_inc(sem("cu_ready"), 1)

        @block.vector
        def _(dve):
            steps = DveSteps(dve)
            chain = steps.chain
            dve.memset(zero[:, :, :], 0.0).then_inc(sem("zero_ready"), 1)
            dve.memset(zeros32[:, :], 0.0)
            dve.wait_ge(ld_small, 16 * 5)
            for q, c in enumerate((C_F, C_I)):
                dve.tensor_scalar(hcols[:, q, :], cols[:, c, :], 0.5, None, ALU.mult)
            dve.tensor_copy(hcols[:, 2, :], cols[:, C_C, :]).then_inc(sem("hcols"), 1)
            dve.tensor_copy(cT[:, :, :], cols[:, C_IN, :].rearrange("p (k o) -> p k o", o=1
                                                                    ).to_broadcast([P, KT, S])).then_inc(sem("c_new"), 1)
            dve.wait_ge(sem("tg_ready"), 1)
            schedule(dve, steps)

            dve.wait_ge(sem("tail_out"), 2 * B)
            for i in range(NT):
                chain.mark(dve.max(top[:, i, :], lg[:, i, :]))
            chain.wait()
            for i in range(NT):
                chain.mark(dve.max_index(topi[:, i, :], top[:, i, :], lg[:, i, :]))
            chain.wait()
            dve.tensor_tensor(ex[:, :, :], top[:, :, :], top[:, :, 0:1].to_broadcast([P, NT, 8]), ALU.subtract
                              ).then_inc(sem("router_shift"), 1)
            chain.link(dve.tensor_copy(idxf[:, :, :], topi[:, :, 0:2].rearrange("p t w -> p w t")))
            dve.wait_ge(sem("pool_const"), 6)
            for w in range(2):
                dve.tensor_tensor(mask[:, w], iota[:, :].rearrange("p (o e) -> p o e", o=1).to_broadcast([P, NT, E]),
                                  idxf[:, w, :].rearrange("p (t o) -> p t o", o=1).to_broadcast([P, NT, E]),
                                  ALU.is_equal).then_inc(sem("masks"), 1)
            dve.wait_ge(sem("counts"), 2)
            tile_counts = g[1][:, 0:2 * NT * E].rearrange("p (j e) -> p j e", e=E)
            before = g[0][:, 0:2 * NT * E].rearrange("p (j e) -> p j e", e=E)
            for e in range(E):
                chain.mark(dve.tensor_tensor_scan(inc[:, :, e], zeros32[:, :], tile_counts[:, :, e], 0.0,
                                                  ALU.add, ALU.add))
            chain.wait()
            chain.link(dve.tensor_tensor(inc[:, :, :], inc[:, :, :], tile_counts, ALU.subtract))
            chain.link(dve.tensor_tensor(loc[:, :, :], inc[:, :, :], before, ALU.add))
            chain.link(dve.scalar_tensor_tensor(loc[:, :, :], loc[:, :, :], -1.0,
                                                mask[:, :, :, :].rearrange("p w t e -> p (w t) e"), ALU.add, ALU.mult))
            chain.link(dve.tensor_reduce(pos[:, :], loc[:, :, :], AX.X, ALU.add))
            iw = idxf[:, :, :].rearrange("p w t -> p (w t)")
            vw = valid[:, :, :].rearrange("p w t -> p (w t)")
            chain.mark(dve.tensor_scalar(vw, pos[:, :], float(C), None, ALU.is_lt))
            chain.link(dve.tensor_scalar(slotf[:, :], pos[:, :], float(C), float(E * C), ALU.is_ge, ALU.mult))
            chain.link(dve.tensor_tensor(slotf[:, :], slotf[:, :], pos[:, :], ALU.add))
            chain.link(dve.scalar_tensor_tensor(slotf[:, :], iw, float(C), slotf[:, :], ALU.mult, ALU.add))
            chain.mark(dve.tensor_copy(sidx[:, :], slotf[:, :]))
            chain.link(dve.tensor_scalar(slotg[:, :], pos[:, :], float(C - 1), None, ALU.min))
            chain.link(dve.scalar_tensor_tensor(slotg[:, :], iw, float(C), slotg[:, :], ALU.mult, ALU.add))
            dve.tensor_copy(gidx[:, :], slotg[:, :]).then_inc(sem("slots_ready"), 1)
            dve.wait_ge(sem("router_exp"), 1)
            chain.link(dve.tensor_reduce(sums[:, :], ex[:, :, :], AX.X, ALU.add))
            chain.link(dve.reciprocal(sums[:, :], sums[:, :]))
            chain.link(dve.tensor_tensor(prob[:, :, :], ex[:, :, 0:2].rearrange("p t w -> p w t"),
                                         sums[:, :].rearrange("p (o t) -> p o t", o=1).to_broadcast([P, 2, NT]), ALU.mult))
            chain.link(dve.tensor_tensor(prob[:, :, :], prob[:, :, :], valid[:, :, :], ALU.mult))
            chain.link(dve.tensor_tensor(den[:, :], prob[:, 0, :], prob[:, 1, :], ALU.add))
            chain.link(dve.tensor_scalar(den[:, :], den[:, :], EPS_F32, None, ALU.max))
            chain.link(dve.reciprocal(den[:, :], den[:, :]))
            chain.link(dve.tensor_tensor(gate[:, :, :], prob[:, :, :],
                                         den[:, :].rearrange("p (o t) -> p o t", o=1).to_broadcast([P, 2, NT]), ALU.mult))
            chain.link(dve.tensor_scalar(gate[:, :, :], gate[:, :, :], KEEP, None, ALU.mult))

            def expert(e, par, prev):
                for s in range(CT):
                    dve.wait_ge(sem("down_mm"), CT * e + s + 1)
                    if prev:
                        dve.wait_ge(sem("y_out"), 16 * (e - 1))
                    dve.tensor_tensor(yb[par][:, s:s + 1, :], po[s % 2][:, 0:D].rearrange("p (o d) -> p o d", o=1),
                                      b2r[:, bass.ds(e, 1), :], ALU.add).then_inc(sem("y_ready"), 1)

            dve.wait_ge(sem("b2_in"), 16)
            expert(0, 0, False)
            expert(1, 1, False)
            with dve.Fori(1, E // 2) as i:
                for par in range(2):
                    expert(2 * i + par, par, True)

            for i in range(NT):
                dve.wait_ge(sem(f"gathered{i}"), 32)
                for w in range(2):
                    chain.link(dve.scalar_tensor_tensor(x4[:, i, :], yg[:, 2 * i + w, :], gate[:, w, i:i + 1],
                                                        x4[:, i, :], ALU.mult, ALU.add))
                dve.scalar_tensor_tensor(x4[:, i, :], x4[:, i, :], tg[:, 3:4], x[:, i, :], ALU.mult, ALU.add
                                         ).then_inc(sem("final"), 1)

        class PeSteps:
            def __init__(self, pe):
                self.pe = pe
                self.read = [None, None]

            def enter(self, k, name, i):
                self.read = [(sem("on"), 2 * k), (sem("on"), 2 * k - 1)]

            def leave(self, name):
                pass

            def left(self, k, name, count):
                self.read = [(sem("on"), 2 * k), (sem("on"), 2 * k - 1)]

            def claim(self, i, reader, value):
                if self.read[i]:
                    wait(self.pe, *self.read[i])
                self.read[i] = (sem(reader), value)
                return g[i]

            def project(self, bank_, w, moving, cols_=None):
                for m in range(KT):
                    for k in range(KT):
                        ins = self.pe.matmul(bk(bank_, KT)[:, m, :], weights[:, w, k, P * m:P * (m + 1)],
                                             moving[:, k, :], start=k == 0, stop=k == KT - 1)
                return ins

            def project_rows(self, bank_, w, still):
                for q in range(TT):
                    for k in range(KT):
                        ins = self.pe.matmul(bk(bank_, TT)[:, q, :], still[:, k, P * q:P * (q + 1)],
                                             weights[:, w, k, :], start=k == 0, stop=k == KT - 1)
                return ins

            def transpose_rows(self, bank_, src):
                for q in range(TT):
                    for k in range(KT):
                        ins = self.pe.transpose(bk(bank_, KT)[:, k, P * q:P * (q + 1)],
                                                src[:, q, P * k:P * (k + 1)], ident[:, :])
                return ins

            def front_T(self, j):
                wait(self.pe, sem("front_h"), j.n + 1)
                self.transpose_rows(self.claim(G_FRONT, "front_hT", j.n + 1), hN).then_inc(sem("front_tr"), 1)

            def qk(self, j, q):
                pe = self.pe
                if j.kind != "S" and q == 1:
                    wait(pe, sem("context_in"), 16 * (j.load + 1))
                if q == 0:
                    wait(pe, sem("front_hT"), j.n + 1)
                src = hT if q == 0 or j.kind == "S" else ctxT
                b_ = self.claim(G_QK, "qk_full", 2 * j.n + j.order[q] + 1)
                self.project(b_, WEIGHTS[j.kind][q], src).then_inc(sem("qk_mm"), 1)

            def v(self, j):
                b_ = self.claim(G_V, "v_sb", j.n + 1)
                src = hT if j.kind == "S" else ctxT
                self.project_rows(b_, WEIGHTS[j.kind][2], src).then_inc(sem("v_mm"), 1)

            def scores1(self, j, u):
                pe = self.pe
                if u == 0:
                    wait(pe, sem("stacked"), 16 * 2 * len(RUNS) * (j.n + 1))
                wait(pe, sem("max"), UNITS * j.n + u - 1)
                hp, q = u // 2, u % 2
                for a in range(2):
                    h = 2 * hp + a
                    ins = pe.matmul(bk(p1[u % 2], 2)[:, a, :], qs[0:KROWS, j.par, h, P * q:P * (q + 1)],
                                    ks[0:KROWS, j.par, h, :], start=True, stop=True)
                ins.then_inc(sem("scores1"), 1)

            def scores2(self, j, u):
                pe = self.pe
                if u == 0:
                    wait(pe, sem("nmax_in"), 16 * MROWS * (j.n + 1))
                wait(pe, sem("exp"), UNITS * j.n + u - 1)
                hp, kt = u // 2, u % 2
                for a in range(2):
                    h = 2 * hp + a
                    ins = pe.matmul(bk(p2[u % 2], 2)[:, a, :], ks[0:KROWS + MROWS, j.par, h, P * kt:P * (kt + 1)],
                                    qs[0:KROWS + MROWS, j.par, h, :], start=True, stop=True)
                ins.then_inc(sem("scores2"), 1)

            def pv(self, j, q):
                pe = self.pe
                if q == 0:
                    wait(pe, sem("v_sb"), j.n + 1)
                wait(pe, sem("exp"), UNITS * j.n + 4 * (q + 1))
                wait(pe, sem("o_sb"), 4 * j.n + q - 1)
                for kt in range(TT):
                    for a in range(4):
                        u = 4 * q + 2 * (a // 2) + kt
                        ins = pe.matmul(po[q % 2][32 * a:32 * a + 32, 0:S], vv[:, j.par, kt, 4 * q + a, :],
                                        ring[:, u % RING, a % 2, :], start=kt == 0, stop=kt == TT - 1,
                                        skip_group_check=True)
                ins.then_inc(sem("pv"), 1)

            def nmax_T(self, j):
                pe = self.pe
                wait(pe, sem("nmaxb"), j.n + 1)
                b_ = self.claim(G_NMAX, "nmax_sb", j.n + 1)
                for q in range(TT):
                    ins = pe.transpose(b_[0:32, 0:P].bitcast(BF16)[:, P * q:P * (q + 1)],
                                       nmaxb[:, q].rearrange("p r h -> p (r h)"), identb[:, :])
                ins.then_inc(sem("nmax_tr"), 1)

            def o_T(self, j):
                pe = self.pe
                wait(pe, sem("o_sb"), 4 * (j.n + 1))
                for q in range(TT):
                    b_ = self.claim(G_O[q], "on", 2 * j.n + q + 1)
                    for a in range(4):
                        ins = pe.transpose(b_[:, P * a:P * (a + 1)], os_[:, a, P * q:P * (q + 1)], ident[:, :])
                    ins.then_inc(sem("o_tr"), 1)

            def on_T(self, j):
                wait(self.pe, sem("on"), 2 * (j.n + 1))
                self.transpose_rows(self.claim(G_ON, "ot_sb", j.n + 1), on).then_inc(sem("on_tr"), 1)

            def out_proj(self, j):
                wait(self.pe, sem("ot_sb"), j.n + 1)
                self.project_rows(self.claim(G_OUT, "residual", j.n + 1), WEIGHTS[j.kind][3], ot
                                  ).then_inc(sem("proj_mm"), 1)

            def tail_T(self, j):
                if isinstance(j.tail, int) and j.tail == 0:
                    self.pe.wait_ge(ld_w1, 16)
                wait(self.pe, sem("tail_h"), j.tail + 1)
                src = tN if j.kind == "A" else tS
                self.transpose_rows(self.claim(G_TAIL, "tail_hT", j.tail + 1), src).then_inc(sem("tail_tr"), 1)

            def recur(self, j, q):
                pe = self.pe
                if q == 0:
                    wait(pe, sem("tail_hT"), j.tail + 1)
                    wait(pe, sem("c_new"), j.b + 1)
                b_ = self.claim(G_GATES[q], "gates", 3 * j.b + q + 1)
                for m in range(KT):
                    for i, (w, src) in enumerate(((W_F + 2 * q, tT), (W_UF + 2 * q, cT))):
                        for k in range(KT):
                            ins = pe.matmul(bk(b_, KT)[:, m, :], weights[:, w, k, P * m:P * (m + 1)],
                                            src[:, k, :], start=i + k == 0, stop=i + k == 2)
                ins.then_inc(sem("gates_mm"), 1)

            def xo(self, j):
                self.project_rows(self.claim(G_XO, "tail_out", j.tail + 1), W_OX, tT).then_inc(sem("tail_mm"), 1)

            def logits(self, j):
                pe = self.pe
                wait(pe, sem("tail_hT"), j.tail + 1)
                b_ = self.claim(G_LOGITS, "tail_out", j.tail + 1)
                for q in range(TT):
                    for k in range(KT):
                        ins = pe.matmul(b_[:, E * q:E * (q + 1)], tT[:, k, P * q:P * (q + 1)], wr[:, k, :],
                                        start=k == 0, stop=k == KT - 1)
                ins.then_inc(sem("tail_mm"), 1)

            def alone(self, j, nxt):
                self.front_T(j)
                self.qk(j, 0)
                if j.order[0] == 0:
                    self.qk(j, 1)
                    self.v(j)

            def early(self, j):
                self.qk(j, 1)
                self.v(j)

            def early_end(self, j):
                pass

            def step(self, k, front, mid, back, prev, nxt):
                tail = prev if prev and prev.kind != "X" else None
                if front:
                    self.front_T(front)
                if prev:
                    self.on_T(prev)
                if front:
                    self.qk(front, 0)
                if prev:
                    self.out_proj(prev)
                for u in range(SLOTS_OF):
                    if back and u < UNITS:
                        self.scores2(back, u)
                    if mid and u >= LAG:
                        self.scores1(mid, u - LAG)
                    if front and u == AT_QK[1]:
                        self.qk(front, 1)
                    if tail and u == AT_TAIL_T[tail.kind]:
                        self.tail_T(tail)
                    if tail and tail.kind == "A" and u in AT_GATES:
                        self.recur(tail, AT_GATES.index(u))
                    if tail and tail.kind == "A" and u == AT_XO:
                        self.xo(tail)
                    if tail and tail.kind == "S" and u == AT_LOGITS:
                        self.logits(tail)
                    if back and u in AT_PV:
                        self.pv(back, AT_PV.index(u))
                if front:
                    self.v(front)
                if mid:
                    self.nmax_T(mid)
                if back:
                    self.o_T(back)

            def after(self, j):
                self.on_T(j)
                self.out_proj(j)
                self.tail_T(j)
                if j.kind == "A":
                    for q in range(3):
                        self.recur(j, q)
                    self.xo(j)
                else:
                    self.logits(j)

            def middle(self):
                wait(self.pe, sem("c_new"), B + 1)
                self.project_rows(self.claim(0, "cu_ready", 1), W_UO, cT).then_inc(sem("cu_mm"), 1)

        @block.tensor
        def _(pe):
            pe.wait_ge(sem("pool_const"), 6)
            pe.wait_ge(sem("pool_chain"), 5)
            pe.wait_ge(ld_w0, 16)
            pe.wait_ge(ld_small, 16 * 5)
            steps = PeSteps(pe)
            schedule(pe, steps)

            pe.wait_ge(sem("masks"), 2)
            mk = mask[:, :, :, :].rearrange("p w t e -> p (w t e)")
            for i, still in enumerate((tri, ones)):
                b_ = steps.claim(i, "slots_ready", 1)
                pe.matmul(b_[:, 0:2 * NT * E], still[:, :], mk, start=True, stop=True).then_inc(sem("counts"), 1)
            pe.wait_ge(sem("slots_ready"), 1)

            def expert(e, par, prev, loads):
                pe.wait_ge(sem(f"slots_in{par}"), 16 * (loads + 1))
                if prev:
                    pe.wait_ge(sem("slots_T"), KT * e)
                for k in range(KT):
                    for s in range(CT):
                        ins = pe.transpose(g[k][:, P * s:P * (s + 1)], br[par][:, s, P * k:P * (k + 1)], ident[:, :])
                    ins.then_inc(sem("slots_tr"), 1)
                pe.wait_ge(sem(f"w1_in{par}"), 16 * (loads + 1))
                pe.wait_ge(sem("slots_T"), KT * (e + 1))
                for f in range(FT):
                    if prev or f >= 4:
                        pe.wait_ge(sem("hidden"), FT * e + f - 3)
                    for k in range(KT):
                        ins = pe.matmul([p1, p2][f // 2 % 2][f % 2][:, :], w1s[:, par, k, P * f:P * (f + 1)],
                                        bT[:, k, :], start=k == 0, stop=k == KT - 1)
                    ins.then_inc(sem("up_mm"), 1)
                pe.wait_ge(sem(f"w2_in{par}"), 16 * (loads + 1))
                pe.wait_ge(sem("hidden"), FT * (e + 1))
                for s in range(CT):
                    if prev or s >= 2:
                        pe.wait_ge(sem("y_ready"), CT * e + s - 1)
                    for f in range(FT):
                        ins = pe.matmul(po[s % 2][:, 0:D], hid[:, f, P * s:P * (s + 1)], w2s[:, par, f, :],
                                        start=f == 0, stop=f == FT - 1)
                    ins.then_inc(sem("down_mm"), 1)

            expert(0, 0, False, 0)
            expert(1, 1, True, 0)
            with pe.Fori(1, E // 2) as i:
                for par in range(2):
                    expert(2 * i + par, par, True, i)


INS = ["x", "ctxT", "weights", "cols", "rows", "gates", "b1", "wr", "w1", "w2", "b2"]


def kernel(x, ctx_1024, g_xattn, g_ffn, **p):
    import numpy as np
    import concourse.bacc as bacc
    from concourse.bass_utils import run_bass_kernel_spmd

    a = {k: np.asarray(v) for k, v in p.items()}
    weights = [a["L0_xattn_Wq"].T, a["L0_xattn_Wk"].T, a["L0_xattn_Wv"].T, a["L0_xattn_Wo"].T]
    for gate in "fic":
        weights += [a[f"L0_ffn_w{gate}"].T, a[f"L0_ffn_u{gate}"].T]
    weights += [a["L0_ffn_wo"].T, a["L0_ffn_uo"].T]
    weights += [a[f"L1_xattn_W{w}"] for w in "qkvo"] + [a[f"L1_ffn_w{w}"] for w in "qkvo"]
    order = np.arange(D).reshape(H // KT, KT, DK).transpose(1, 2, 0).ravel()
    for w in (W_Q0, W_K0, W_Q1, W_K1, W_QS, W_KS):
        weights[w] = weights[w][:, order]
    cols = [a[n] for n in ("L0_xattn_bq", "L0_xattn_bk", "L0_ffn_bf", "L0_ffn_bi", "L0_ffn_bc", "L0_ffn_in_c",
                           "L1_xattn_bq", "L1_xattn_bk", "L1_ffn_bq", "L1_ffn_bk")]
    for c in (C_Q0, C_K0, C_Q1, C_K1, C_QS, C_KS):
        cols[c] = cols[c][order]
    rows = [a[n] for n in ("L0_xattn_bv", "L0_xattn_bo", "L0_ffn_bo", "L1_xattn_bv", "L1_xattn_bo", "L1_ffn_bv",
                           "L1_ffn_bo", "L1_ffn_ln1_g", "L1_ffn_ln1_b", "L1_ffn_ln2_g", "L1_ffn_ln2_b")]
    given = {
        "x": np.asarray(x),
        "ctxT": np.asarray(ctx_1024)[[*range(B), 0]].transpose(0, 2, 1),
        "weights": np.stack(weights),
        "cols": np.stack(cols).reshape(10 * KT, P).T,
        "rows": np.stack(rows),
        "b2": a["L1_ffn_b2"],
        "gates": np.concatenate([np.asarray(g_xattn), np.asarray(g_ffn)]),
        "b1": a["L1_ffn_b1"].reshape(E * FT, P).T,
        "wr": a["L1_ffn_wr"],
        "w1": a["L1_ffn_w1"],
        "w2": a["L1_ffn_w2"],
    }
    nc = bacc.Bacc("TRN2", target_bir_lowering=False, num_devices=1)
    arrays, t = {}, {}
    for name in INS:
        arr = np.ascontiguousarray(given[name])
        arrays[f"in_{name}"] = arr
        t[name] = nc.dram_tensor(f"in_{name}", arr.shape, mybir.dt.from_np(arr.dtype), kind="ExternalInput").ap()
    t["out"] = nc.dram_tensor("out_x", (B, S, D), F32, kind="ExternalOutput").ap()
    flamingo(nc, t)
    return run_bass_kernel_spmd(nc, [arrays], core_ids=[0]).results[0]["out_x"]
```

```python
from contextlib import ExitStack

import concourse.bass as bass
from concourse import mybir

F32 = mybir.dt.float32
BF16 = mybir.dt.bfloat16
F32R = mybir.dt.float32r
U32 = mybir.dt.uint32
ALU = mybir.AluOpType
ACT = mybir.ActivationFunctionType
AX = mybir.AxisListType

P = 128
B, S, D = 8, 256, 256
H, DK = 16, 16
TT = S // P
KT = D // P
NT = B * TT
E, F, C = 8, 1024, 512
FT = F // P
CT = C // P
EPS_LN = 1e-5
EPS_F32 = 1.1920928955078125e-07
SCALE = 0.25
KEEP = 0.8
SLOTS = 6
RUNS = ((0, 3), (3, 2), (5, 1))
KROWS = SLOTS * DK
MROWS = 2
UNITS = 16
RING = 8

(W_Q0, W_K0, W_V0, W_O0, W_F, W_UF, W_I, W_UI, W_C, W_UC, W_OX, W_UO,
 W_Q1, W_K1, W_V1, W_O1, W_QS, W_KS, W_VS, W_OS) = range(20)
(C_Q0, C_K0, C_F, C_I, C_C, C_IN, C_Q1, C_K1, C_QS, C_KS) = range(10)
(R_V0, R_O0, R_OF, R_V1, R_O1, R_VS, R_OS, R_G1, R_B1, R_G2, R_B2, R_E) = range(12)
LAG = 3
SLOTS_OF = UNITS + LAG
AT_QK = (-1, 1)
AT_TAIL_STATS, AT_TAIL_APPLY, AT_LOGITS, AT_GATES, AT_RECUR, AT_XO = 0, 3, 11, (8, 10, 12), 13, 15
AT_TAIL_T = {"A": 6, "S": 10}
AT_MID = (3, 5)
AT_NEXT_SUM, AT_NEXT_STATS, AT_NEXT_VAR, AT_NEXT_APPLY, AT_NEXT_AGAIN = 7, 9, 11, 13, 15
AT_PV = (5, 9, 13, 16)
G_FRONT, G_QK, G_V, G_OUT, G_TAIL, G_GATES, G_XO, G_LOGITS = 1, 0, 0, 1, 1, (0, 1, 0), 1, 1
WEIGHTS = {"A": (W_Q0, W_K0, W_V0, W_O0), "X": (W_Q1, W_K1, W_V1, W_O1), "S": (W_QS, W_KS, W_VS, W_OS)}
COLS = {"A": (C_Q0, C_K0), "X": (C_Q1, C_K1), "S": (C_QS, C_KS)}
ROWS = {"A": (R_V0, R_O0), "X": (R_V1, R_O1), "S": (R_VS, R_OS)}


class Job:

    def __init__(self, n, kind, b, par, order=(0, 1)):
        self.n, self.kind, self.b, self.par = n, kind, b, par
        self.order = order
        self.tail = b if kind == "A" else B + b
        self.load = b if kind == "A" else B + b


def job(n, kind, b, order=(0, 1)):
    return Job(n, kind, b, n % 2, order)


def schedule(eng, steps):
    A = [job(n, "A", n) for n in range(B)]
    steps.alone(A[0], A[1])
    steps.step(-1, A[1], A[0], None, None, A[2])
    steps.step(0, A[2], A[1], A[0], None, A[3])
    with eng.Fori(0, 2) as i:
        for half in range(2):
            k = 2 * i + 1 + half
            if half == 0:
                steps.enter(k, "A", i)
            front, mid, back, prev, nxt = (Job(k + d, "A", k + d, (1 + half + d) % 2) for d in (2, 1, 0, -1, 3))
            steps.step(k, front, mid, back, prev, nxt)
        steps.leave("A")
    steps.left(5, "A", 2)
    steps.step(5, A[7], A[6], A[5], A[4], None)
    steps.step(6, None, A[7], A[6], A[5], None)
    X0 = job(B, "X", 0, (1, 0))
    steps.early(X0)
    steps.step(7, None, None, A[7], A[6], None)
    steps.early_end(X0)
    steps.after(A[7])
    steps.middle()

    X = [X0] + [job(B + b if b < 4 else 5 + 2 * b, "X", b) for b in range(1, B)]
    T = [job(12 + 2 * b if b < 5 else 16 + b, "S", b) for b in range(B)]
    steps.alone(X[0], X[1])
    steps.step(7, X[1], X[0], None, None, X[2])
    steps.step(8, X[2], X[1], X[0], None, X[3])
    steps.step(9, X[3], X[2], X[1], X[0], T[0])
    steps.step(10, T[0], X[3], X[2], X[1], X[4])
    steps.step(11, X[4], T[0], X[3], X[2], T[1])
    with eng.Fori(0, 3) as i:
        k = 2 * i + 12
        steps.enter(k, "B", i)
        steps.step(k, Job(k + 2, "S", i + 1, 0), Job(k + 1, "X", i + 4, 1), Job(k, "S", i, 0),
                   Job(k - 1, "X", i + 3, 1), Job(k + 3, "X", i + 5, 1))
        k = 2 * i + 13
        steps.step(k, Job(k + 2, "X", i + 5, 1), Job(k + 1, "S", i + 1, 0), Job(k, "X", i + 4, 1),
                   Job(k - 1, "S", i, 0), Job(k + 3, "S", i + 2, 0))
        steps.leave("B")
    steps.left(18, "B", 3)
    steps.step(18, T[4], X[7], T[3], X[6], T[5])
    steps.step(19, T[5], T[4], X[7], T[3], T[6])
    steps.step(20, T[6], T[5], T[4], X[7], T[7])
    steps.step(21, T[7], T[6], T[5], T[4], None)
    steps.step(22, None, T[7], T[6], T[5], None)
    steps.step(23, None, None, T[7], T[6], None)
    steps.after(T[7])


def wait(eng, sem, value):
    if isinstance(value, int) and value <= 0:
        return
    eng.wait_ge(sem, value)


def settle(eng, sem):
    eng.sem_inc(sem, 1)


class Chain:

    def __init__(self, eng, sem, per):
        self.eng, self.sem, self.per = eng, sem, per
        self.base, self.n = 0, 0

    def mark(self, ins):
        ins.then_inc(self.sem, 1)
        self.n += 1

    def wait(self):
        self.eng.wait_ge(self.sem, self.base + self.n)

    def link(self, ins):
        self.mark(ins)
        self.wait()

    def enter(self, name, i):
        self.start = self.base + self.n
        self.base, self.n = self.start + self.per[name] * i, 0

    def leave(self, name):
        assert self.n == self.per[name], (name, self.n)

    def left(self, name, count):
        self.base, self.n = self.start + self.per[name] * count, 0


def flamingo(nc, t):
    ctx = ExitStack()
    with ctx:
        def sb(name, shape, dt=F32):
            return ctx.enter_context(nc.sbuf_tensor("sb_" + name, shape, dt))

        def bank(name):
            return ctx.enter_context(nc.psum_tensor("ps_" + name, [P, 512], F32))

        sems = {}

        def sem(name):
            if name not in sems:
                sems[name] = ctx.enter_context(nc.semaphore(name))
            return sems[name]

        cols = sb("cols", [P, 10, KT])
        rows = sb("rows", [P, R_E, D])
        b1c = sb("b1c", [P, E, FT])
        wr = sb("wr", [P, KT, E])
        gates_in = sb("gates_in", [P, 4])
        tg = sb("tg", [P, 4])
        ctxT = sb("ctxT", [P, KT, S])
        hN = sb("hN", [P, TT, D])
        hT = sb("hT", [P, KT, S])
        tN = sb("tN", [P, TT, D])
        tT = sb("tT", [P, KT, S])
        stats = sb("stats", [P, 2, TT, 6])
        mv = sb("mv", [P, 2, TT, 2])
        ve = sb("ve", [P, 3, TT])
        rec = sb("rec", [P, TT])
        rstd = sb("rstd", [P, 3, TT])
        minus_half = sb("minus_half", [P, 2, TT])
        full = sb("full", [P, 2, KT, S])
        parts = sb("parts", [P, 3, 2, KT, S], BF16)
        vv = sb("vv", [P, 2, TT, H, 32])
        nmax = sb("nmax", [P, TT, H])
        nmaxb = sb("nmaxb", [P, TT, MROWS, H], BF16)
        nmt = sb("nmt", [32, S], BF16)
        os_ = sb("os", [P, 4, S])
        rden = sb("rden", [P, TT, H])
        on = sb("on", [P, TT, D])
        ot = sb("ot", [P, KT, S])
        res = sb("res", [P, TT, D])
        cT = sb("cT", [P, KT, S])
        gact = sb("gact", [P, 3, KT, S])
        tS = gact[:, 0]
        cu = sb("cu", [P, TT, D])
        xt = sb("xt", [P, TT, D])
        lg = sb("lg", [P, NT, E])
        ident = sb("ident", [P, P])
        identb = sb("identb", [P, P], BF16)
        top = sb("top", [P, NT, 8])
        topi = sb("topi", [P, NT, 8], U32)
        idxf = sb("idxf", [P, 2, NT])
        iota = sb("iota", [P, E])
        mask = sb("mask", [P, 2, NT, E], BF16)
        tri = sb("tri", [P, P], BF16)
        ones = sb("ones", [P, P], BF16)
        zeros32 = sb("zeros32", [P, 2 * NT])
        ex = sb("ex", [P, NT, 8])
        sums = sb("sums", [P, NT])
        inc, loc = (gact[:, 1].rearrange("p k (j e) -> p k j e", e=E)[:, i] for i in range(2))
        meta = sb("meta", [P, 2 * NT, 2])
        meta_none = sb("meta_none", [P, E * CT, 2])
        pos = sb("pos", [P, 2 * NT])
        valid = sb("valid", [P, 2, NT])
        slotf = sb("slotf", [P, 2 * NT])
        sidx = sb("sidx", [P, 2 * NT], U32)
        prob = sb("prob", [P, 2, NT])
        den = sb("den", [P, NT])
        gate = sb("gate", [P, 2, NT])
        hcols = sb("hcols", [P, 3, KT])
        zero = sb("zero", [P, 1, D])
        meta_sb = sb("meta_sb", [P, E * CT, 2])

        with ExitStack() as attentions:
            def sa(name, shape, dt=F32):
                return attentions.enter_context(nc.sbuf_tensor("sb_" + name, shape, dt))

            weights = sa("weights", [P, 20, KT, D])
            qs = sa("qs", [P, 2, H, S], BF16)
            ks = sa("ks", [P, 2, H, S], BF16)
            ring = sa("ring", [P, RING, 2, S])
            x = sa("x", [P, NT, D])
            x4 = sa("x4", [P, NT, D])
            xo = sa("xo", [P, NT, D])
            h2 = xo
        w1f = sb("w1f", [P, KT, F])[:, :, :]
        br = [sb(f"br{i}", [P, CT, D])[:, :, :] for i in range(2)]
        bT = sb("bT", [P, 2, KT, C], F32R)
        yb = [sb(f"yb{i}", [P, CT, D])[:, :, :] for i in range(2)]
        b2r = sb("b2r", [P, E, D])[:, :, :]
        w1s = sb("w1s", [P, 2, KT, F], F32R)
        w2s = sb("w2s", [P, 2, FT, D], F32R)
        hidden_hi = sb("hidden_hi", [P, FT, C], F32R)
        hidden_lo = sb("hidden_lo", [P, FT, C], F32R)
        w2f = sb("w2f", [P, FT, D])[:, :, :]
        sb("rest_of_x4", [P, FT, D])
        hidden_f = sb("hidden_f", [P, FT, C])

        p1 = [bank("p1a"), bank("p1b")]
        p2 = [bank("p2a"), bank("p2b")]
        po = [bank("poa"), bank("pob")]
        g = [bank("g0"), bank("g1")]

        def bk(t_, a):
            return t_[:, :].rearrange("p (a c) -> p a c", a=a)

        parts_dram = nc.dram_tensor("parts_dram", (2, 3 * DK, H * S), BF16, kind="Internal").ap()
        buf_dram = nc.dram_tensor("buf_dram", (E * C, D), F32, kind="Internal").ap()
        meta_dram = nc.dram_tensor("meta_dram", (E * C, 2), F32, kind="Internal").ap()

        ld_x = [sem(f"ld_x{i}") for i in range(3)]
        (ld_cols, ld_qk, ld_vo, ld_rows, ld_gates, ld_late) = [sem(s) for s in (
            "ld_cols", "ld_qk", "ld_vo", "ld_rows", "ld_gates", "ld_late")]

        block = ctx.enter_context(nc.Block())

        class SpSteps:
            def __init__(self, sp):
                self.sp = sp

            def enter(self, k, name, i):
                pass

            def leave(self, name):
                pass

            def left(self, k, name, count):
                pass

            def load_square(self, w0, w1, done):
                wv = t["weights"].rearrange("w (k p) n -> p w k n", p=P)
                self.sp.dma_start(weights[:, w0:w1, :, :], wv[:, w0:w1]).then_inc(done, 16)

            def load_more(self, k):
                sp = self.sp
                if k == -1:
                    sp.dma_start(x[:, 2 * TT:NT, :], t["x"][2:B].rearrange("b (t p) d -> p (b t) d", p=P)
                                 ).then_inc(ld_x[2], 16)
                if k == 0:
                    self.load_square(W_F, W_Q1, ld_gates)
                if k == 5:
                    self.load_square(W_Q1, W_OS + 1, ld_late)
                    sp.dma_start(b1c[:, :, :], t["b1"].rearrange("p (e f) -> p e f", e=E)).then_inc(ld_late, 16)
                    sp.dma_start(wr[:, :, :], t["wr"].rearrange("(k p) e -> p k e", p=P)).then_inc(ld_late, 16)
                if k == 6:
                    sp.wait_ge(sem("zero_ready"), 1)
                    sp.dma_start(buf_dram.rearrange("(a p) d -> p a d", p=P),
                                 zero[:, :, :].to_broadcast([P, E * CT, D])).then_inc(sem("slots_zero"), 16)
                    sp.wait_ge(sem("meta_none"), 1)
                    sp.dma_start(meta_dram.rearrange("(a p) c -> p a c", p=P), meta_none[:, :, :]
                                 ).then_inc(sem("slots_zero"), 16)

            def load_context(self, b):
                src = t["ctxT"].rearrange("b (k p) s -> b p k s", p=P)
                self.sp.dma_start(ctxT[:, :, :], src[bass.ds(b, 1)].rearrange("o p k s -> (o p) k s")
                                  ).then_inc(sem("context_in"), 16)

            def parts_out(self, j, q):
                sp = self.sp
                wait(sp, sem("split"), 2 * j.n + j.order[q] + 1)
                settle(sp, sem("sp_passed"))
                if j.order[q] == 0:
                    wait(sp, sem("stacked"), 16 * 2 * len(RUNS) * j.n)
                    settle(sp, sem("sp_passed"))
                sp.dma_start(parts_dram[q].rearrange("(a d) (g x) -> (d g) a x", a=3, g=H // KT),
                             parts[:, :, q, :, :].rearrange("p a m c -> p a (m c)")
                             ).then_inc(sem("parts_out"), 16)

            def stack(self, j, qk=(0, 1)):
                sp = self.sp
                wait(sp, sem("parts_out"), 32 * j.n + 16 * (j.order[qk[-1]] + 1))
                settle(sp, sem("sp_passed"))
                wait(sp, sem("scores2"), UNITS * (j.n - 1))
                settle(sp, sem("sp_passed"))
                for r, (s, n) in enumerate(RUNS):
                    for q in qk:
                        src = (parts_dram[0, 0:DK * n] if q == 0 else
                               bass.AP(parts_dram.tensor, parts_dram[1, DK * r:DK * (r + 1)].offset,
                                       [[0, n], [H * S, DK], [1, H * S]]))
                        sp.dma_start((qs, ks)[q][DK * s:DK * (s + n), j.par, :, :].rearrange("p h c -> p (h c)"),
                                     src).then_inc(sem("stacked"), 16)

            def early(self, j):
                pass

            def early_end(self, j):
                self.parts_out(j, 1)
                self.stack(j, (1,))
                self.next_context(j)

            def next_context(self, j):
                if j.kind == "S":
                    return
                wait(self.sp, sem("v_mm"), j.n + 1)
                settle(self.sp, sem("sp_passed"))
                self.load_context(j.b + 1)

            def alone(self, j, nxt):
                self.parts_out(j, 0)
                if j.order[0] == 1:
                    self.stack(j, (0,))
                    return
                self.parts_out(j, 1)
                self.stack(j)
                self.next_context(j)

            def step(self, k, front, mid, back, prev, nxt):
                sp = self.sp
                if isinstance(k, int) and (front is None or front.kind == "A"):
                    self.load_more(k)
                if front:
                    self.parts_out(front, 0)
                    self.parts_out(front, 1)
                    self.stack(front)
                if mid:
                    wait(sp, sem("nmax_sb"), mid.n + 1)
                    settle(sp, sem("sp_passed"))
                    for r in range(MROWS):
                        sp.dma_start(qs[KROWS + r:KROWS + r + 1, mid.par, :, :], nmt[H * r:H * (r + 1), :]
                                     ).then_inc(sem("nmax_in"), 16)
                if front:
                    self.next_context(front)

            def after(self, j):
                pass

            def middle(self):
                pass

        @block.sync
        def _(sp):
            steps = SpSteps(sp)
            sp.dma_start(x[:, 0:TT, :], t["x"][0].rearrange("(t p) d -> p t d", p=P)).then_inc(ld_x[0], 16)
            sp.dma_start(cols[:, :, :], t["cols"].rearrange("p (a k) -> p a k", k=KT)).then_inc(ld_cols, 16)
            gv = t["gates"]
            sp.dma_start(gates_in[:, :], bass.AP(gv.tensor, gv.offset, [[0, P], [1, 4]])).then_inc(ld_cols, 16)
            steps.load_square(W_Q0, W_V0, ld_qk)
            steps.load_context(0)
            steps.load_square(W_V0, W_F, ld_vo)
            sp.dma_start(x[:, TT:2 * TT, :], t["x"][1].rearrange("(t p) d -> p t d", p=P)).then_inc(ld_x[1], 16)
            rv = t["rows"]
            sp.dma_start(rows[:, :, :].rearrange("p a d -> p (a d)"),
                         bass.AP(rv.tensor, rv.offset, [[0, P], [1, R_E * D]])).then_inc(ld_rows, 16)
            schedule(sp, steps)

            def load_w1(e):
                sp.dma_start(w1f, t["w1"][bass.ds(e, 1)].rearrange("o (k p) f -> p (o k) f", p=P)
                             ).then_inc(sem("w1_in"), 16)

            def load_w2(e):
                sp.dma_start(w2f, t["w2"][bass.ds(e, 1)].rearrange("o (k p) f -> p (o k) f", p=P)
                             ).then_inc(sem("w2_in"), 16)

            slots = buf_dram.rearrange("(e s p) d -> e p s d", e=E, p=P)

            def load_slots(e, par):
                sp.dma_start(br[par], slots[bass.ds(e, 1)].rearrange("o p s d -> (o p) s d")
                             ).then_inc(sem(f"slots_in{par}"), 16)

            sp.wait_ge(sem("tail_mm"), 2 * B)
            load_w1(0)
            bv = t["b2"]
            sp.dma_start(b2r.rearrange("p e d -> p (e d)"), bass.AP(bv.tensor, bv.offset, [[0, P], [1, E * D]])
                         ).then_inc(sem("b2_in"), 16)
            out = t["out"].rearrange("(a p) d -> p a d", p=P)
            sp.dma_start(out[:, NT:, :], zero[:, :, :].to_broadcast([P, CT, D])).then_inc(sem("base_out"), 16)
            for q in range(4):
                sp.wait_ge(sem("base"), q + 1)
                s = slice(NT // 4 * q, NT // 4 * (q + 1))
                sp.dma_start(out[:, s, :], x4[:, s, :]).then_inc(sem("base_out"), 16)
            sp.wait_ge(sem("base_out"), 16 * 5)
            load_w2(0)
            sp.wait_ge(sem("slots_filled"), 16 * 2 * NT)
            load_slots(0, 0)
            load_slots(1, 1)

            def ahead(e, par, more):
                sp.wait_ge(sem("w1_split"), e + 1)
                settle(sp, sem("sp_passed"))
                load_w1(e + 1)
                sp.wait_ge(sem("w2_split"), e + 1)
                settle(sp, sem("sp_passed"))
                load_w2(e + 1)
                if more:
                    sp.wait_ge(sem("slots_tr"), KT * (e + 1))
                    settle(sp, sem("sp_passed"))
                    load_slots(e + 2, par)

            ahead(0, 0, True)
            sp.wait_ge(sem("meta_filled"), 16 * 2 * NT)
            sp.dma_start(meta_sb[:, :, :], meta_dram.rearrange("(a p) c -> p a c", p=P)
                         ).then_inc(sem("meta_in"), 16)
            with sp.Fori(0, E // 2 - 2) as i:
                for half in range(2):
                    ahead(2 * i + 1 + half, 1 - half, True)
            ahead(E - 3, 1, True)
            ahead(E - 2, 0, False)
            sp.wait_ge(sem("y_out"), 16 * CT * E)

        class PoolSteps:
            def __init__(self, pool):
                self.pool = pool
                self.chain = Chain(pool, sem("pool_chain"), {"A": 0, "B": 1})

            def enter(self, k, name, i):
                self.chain.enter(name, i)

            def leave(self, name):
                self.chain.leave(name)

            def left(self, k, name, count):
                self.chain.left(name, count)

            def late_constants(self):
                pool, link = self.pool, self.chain.link
                link(pool.memset(identb[:, :], 0.0))
                pool.affine_select(out=identb[:, :], in_=identb[:, :], compare_op=ALU.not_equal, fill=1.0, base=0,
                                   pattern=[[-1, P]], channel_multiplier=1).then_inc(sem("pool_const"), 1)
                pool.wait_ge(sem("pool_const"), 3)
                pool.memset(ks[KROWS:, :, :, :], 1.0).then_inc(sem("pool_const"), 1)
                pool.wait_ge(sem("pool_const"), 4)
                pool.memset(ones[:, :], 1.0).then_inc(sem("pool_const"), 1)
                link(pool.memset(tri[:, :], 1.0))
                pool.affine_select(out=tri[:, :], in_=tri[:, :], compare_op=ALU.is_ge, fill=0.0, base=0,
                                   pattern=[[1, P]], channel_multiplier=-1).then_inc(sem("pool_const"), 1)
                pool.iota(iota[:, :], [[1, E]], base=0, channel_multiplier=0,
                          allow_small_or_imprecise_dtypes=True).then_inc(sem("pool_const"), 1)
                pool.iota(meta[:, :, 0].bitcast(U32), [[0, 2], [P, NT]], base=0, channel_multiplier=1
                          ).then_inc(sem("pool_const"), 1)
                link(pool.memset(meta_none[:, :, :], 0.0))
                pool.iota(meta_none[:, :, 0].bitcast(U32), [[0, E], [P, CT]], base=NT * P, channel_multiplier=1
                          ).then_inc(sem("meta_none"), 1)

            def rstd(self, who, count, kind):
                wait(self.pool, sem(f"{who}_var"), count)
                a, n = (0, 1) if who == "tail" else (1, 2 if kind == "S" else 1)
                self.pool.tensor_tensor(rstd[:, a:a + n, :], ve[:, a:a + n, :], minus_half[:, 0:n, :], ALU.pow
                                        ).then_inc(sem(f"{who}_rstd"), 1)

            def rest(self, j, q):
                wait(self.pool, sem("qk_hi"), 2 * j.n + j.order[q] + 1)
                self.pool.tensor_tensor(full[:, q], full[:, q], parts[:, 0, q], ALU.subtract
                                        ).then_inc(sem("qk_rest"), 1)

            def low(self, j, q):
                wait(self.pool, sem("qk_mid"), 2 * j.n + j.order[q] + 1)
                self.pool.tensor_tensor(parts[:, 2, q], full[:, q], parts[:, 1, q], ALU.subtract
                                        ).then_inc(sem("split"), 1)

            def alone(self, j, nxt):
                self.rstd("front", j.n + 1, j.kind)
                if j.kind == "X":
                    self.rstd("front", nxt.n + 1, nxt.kind)
                for q in range(2):
                    if q == 0 or j.order[0] == 0:
                        self.rest(j, q)
                        self.low(j, q)
                if j.kind == "A":
                    self.rstd("front", nxt.n + 1, nxt.kind)
                    self.late_constants()

            def early(self, j):
                self.rest(j, 1)

            def early_end(self, j):
                self.low(j, 1)

            def step(self, k, front, mid, back, prev, nxt):
                tail = prev if prev and prev.kind != "X" else None
                if front:
                    self.rest(front, 0)
                if tail:
                    self.rstd("tail", tail.tail + 1, tail.kind)
                if front:
                    self.rest(front, 1)
                if tail and tail.kind == "S":
                    self.keep(tail)
                if front:
                    self.low(front, 0)
                    self.low(front, 1)
                if nxt:
                    self.rstd("front", nxt.n + 1, nxt.kind)
                    self.shift(nxt)

            def keep(self, j):
                pool, chain = self.pool, self.chain
                wait(pool, sem("tail_norm"), j.b + 1)
                settle(pool, sem("pool_passed"))
                chain.link(pool.tensor_tensor(tN[:, :, :], tN[:, :, :],
                                              rows[:, R_G2:R_G2 + 1, :].to_broadcast([P, TT, D]), ALU.mult))
                wait(pool, sem("tail_tr"), j.tail)
                for dst, done in ((tS[:, :, :], "tail_h"), (h2[:, bass.ds(TT * j.b, TT), :], "kept")):
                    pool.tensor_tensor(dst, tN[:, :, :], rows[:, R_B2:R_B2 + 1, :].to_broadcast([P, TT, D]),
                                       ALU.add).then_inc(sem(done), 1)

            def shift(self, j):
                if j.kind == "S":
                    wait(self.pool, sem("front_scaled"), j.b + 1)
                    settle(self.pool, sem("pool_passed"))
                    self.pool.tensor_tensor(hN[:, :, :], hN[:, :, :],
                                            rows[:, R_B1:R_B1 + 1, :].to_broadcast([P, TT, D]), ALU.add
                                            ).then_inc(sem("front_h"), 1)

            def after(self, j):
                self.rstd("tail", j.tail + 1, j.kind)
                if j.kind == "S":
                    self.keep(j)

            def middle(self):
                pass

        @block.gpsimd
        def _(pool):
            steps = PoolSteps(pool)
            link = steps.chain.link
            pool.memset(minus_half[:, :, :], -0.5).then_inc(sem("pool_const"), 1)
            link(pool.memset(ident[:, :], 0.0))
            pool.affine_select(out=ident[:, :], in_=ident[:, :], compare_op=ALU.not_equal, fill=1.0, base=0,
                               pattern=[[-1, P]], channel_multiplier=1).then_inc(sem("pool_const"), 1)
            schedule(pool, steps)
            pool.wait_ge(sem("slots_zero"), 32)
            pool.wait_ge(sem("kept"), B)
            pool.wait_ge(sem("slots_ready"), 1)
            for j in range(2 * NT):
                pool.indirect_dma_start(buf_dram, bass.IndirectOffsetOnAxis(sidx[:, j:j + 1], 0),
                                        h2[:, j % NT, :], None, bounds_check=E * C - 1, oob_is_err=False
                                        ).then_inc(sem("slots_filled"), 16)
            pool.wait_ge(sem("gates_ready"), 1)
            for j in range(2 * NT):
                pool.indirect_dma_start(meta_dram, bass.IndirectOffsetOnAxis(sidx[:, j:j + 1], 0),
                                        meta[:, j, :], None, bounds_check=E * C - 1, oob_is_err=False
                                        ).then_inc(sem("meta_filled"), 16)
            pool.wait_ge(sem("base_out"), 16 * 5)
            pool.wait_ge(sem("meta_in"), 16)
            for e in range(E):
                if 0 < e < E - 1:
                    pool.wait_ge(sem("w1_hi"), e + 2)
                    pool.tensor_tensor(w1s[:, 1], w1f, w1s[:, 0].bitcast(F32), ALU.subtract
                                       ).then_inc(sem("w1_split"), 1)
                if e > 0:
                    pool.wait_ge(sem("y_out"), 16 * CT * e)
                for s in range(CT):
                    pool.wait_ge(sem("y_ready"), CT * e + s + 1)
                    pool.indirect_dma_start(
                        t["out"], bass.IndirectOffsetOnAxis(meta_sb[:, CT * e + s, 0:1].bitcast(U32), 0),
                        yb[e % 2][:, s, :], None, compute_op=ALU.add).then_inc(sem("y_out"), 16)
                if e + 1 < E:
                    pool.wait_ge(sem("w2_hi"), e + 2)
                    pool.tensor_tensor(w2s[:, 1], w2f, w2s[:, 0].bitcast(F32), ALU.subtract
                                       ).then_inc(sem("w2_split"), 1)

        class ActSteps:
            def __init__(self, act):
                self.act = act

            def enter(self, k, name, i):
                pass

            def leave(self, name):
                pass

            def left(self, k, name, count):
                pass

            def gate_x(self, j):
                wait(self.act, sem("xo_sum"), j.b + 1)
                self.act.activation(xt[:, :, :], xt[:, :, :], ACT.Tanh).then_inc(sem("xo_tanh"), 1)

            def front_T(self, j):
                wait(self.act, sem("front_tr"), j.n + 1)
                wait(self.act, sem("v_mm"), j.n)
                self.act.activation(hT[:, :, :], bk(g[G_FRONT], KT), ACT.Copy).then_inc(sem("front_hT"), 1)

            def qk(self, j, q):
                wait(self.act, sem("qk_mm"), 2 * j.n + j.order[q] + 1)
                wait(self.act, sem("split"), 2 * j.n)
                for m in range(KT):
                    ins = self.act.activation(full[:, q, m, :], bk(g[G_QK], KT)[:, m, :], ACT.Identity,
                                              bias=cols[:, COLS[j.kind][q], m:m + 1])
                ins.then_inc(sem("qk_full"), 1)

            def mid_part(self, j, q):
                wait(self.act, sem("qk_rest"), 2 * j.n + j.order[q] + 1)
                wait(self.act, sem("parts_out"), 32 * j.n)
                self.act.activation(parts[:, 1, q], full[:, q], ACT.Copy).then_inc(sem("qk_mid"), 1)

            def nmax_sb(self, j):
                wait(self.act, sem("nmax_tr"), j.n + 1)
                wait(self.act, sem("nmax_in"), 16 * MROWS * j.n)
                self.act.activation(nmt[:, :], p1[0][0:32, 0:P].bitcast(BF16), ACT.Copy
                                    ).then_inc(sem("nmax_sb"), 1)

            def exp(self, j, u):
                act = self.act
                wait(act, sem("scores2"), UNITS * j.n + u + 1)
                if u % 4 == 0:
                    wait(act, sem("pv"), 4 * j.n + u // 4 - 1)
                act.activation(ring[:, u % RING], bk(p2[u % 2], 2), ACT.Exp, scale=SCALE
                               ).then_inc(sem("exp"), 1)

            def o_out(self, j, q):
                wait(self.act, sem("pv"), 4 * j.n + q + 1)
                wait(self.act, sem("o_tr"), 2 * j.n)
                self.act.activation(os_[:, q, :], po[q % 2][:, 0:S], ACT.Copy).then_inc(sem("o_sb"), 1)

            def oT(self, j):
                wait(self.act, sem("on_tr"), j.n + 1)
                wait(self.act, sem("proj_mm"), j.n)
                self.act.activation(ot[:, :, :], bk(p1[1], KT), ACT.Copy).then_inc(sem("ot_sb"), 1)

            def tail_T(self, j):
                wait(self.act, sem("tail_tr"), j.tail + 1)
                wait(self.act, sem("tail_mm"), j.tail)
                self.act.activation(tT[:, :, :], bk(g[G_TAIL], KT), ACT.Copy).then_inc(sem("tail_hT"), 1)

            def recur(self, j, q, b_=None):
                b_ = b_ or g[G_GATES[q]]
                wait(self.act, sem("gates_mm"), 3 * j.b + q + 1)
                wait(self.act, sem("c_new"), j.b + 1)
                for m in range(KT):
                    ins = self.act.activation(gact[:, q, m, :], bk(b_, KT)[:, m, :], ACT.Tanh,
                                              bias=hcols[:, q, m:m + 1], scale=0.5 if q < 2 else 1.0)
                ins.then_inc(sem("gates"), 1)

            def alone(self, j, nxt):
                if j.kind == "X":
                    self.gate_x(j)
                self.front_T(j)
                if nxt.kind == "X":
                    self.gate_x(nxt)
                for q in range(2):
                    if q == 0 or j.order[0] == 0:
                        self.qk(j, q)
                        self.mid_part(j, q)

            def early(self, j):
                self.qk(j, 1)

            def early_end(self, j):
                self.mid_part(j, 1)

            def step(self, k, front, mid, back, prev, nxt):
                tail = prev if prev and prev.kind != "X" else None
                if front:
                    self.front_T(front)
                if prev:
                    self.oT(prev)
                if front:
                    self.qk(front, 0)
                for u in range(SLOTS_OF):
                    if back and u < UNITS:
                        self.exp(back, u)
                    if front and u == AT_QK[1]:
                        self.qk(front, 1)
                    if front and u in AT_MID:
                        self.mid_part(front, AT_MID.index(u))
                    if tail and u == AT_TAIL_T[tail.kind]:
                        self.tail_T(tail)
                    if tail and tail.kind == "A" and u in AT_GATES:
                        self.recur(tail, AT_GATES.index(u))
                    if nxt and nxt.kind == "X" and u == AT_NEXT_SUM:
                        self.gate_x(nxt)
                    if back and u in AT_PV:
                        self.o_out(back, AT_PV.index(u))
                if mid:
                    self.nmax_sb(mid)

            def after(self, j):
                self.oT(j)
                self.tail_T(j)
                if j.kind == "A":
                    for q, b_ in enumerate((g[0], p1[0], p1[1])):
                        self.recur(j, q, b_)

            def middle(self):
                pass


        @block.scalar
        def _(act):
            act.wait_ge(ld_cols, 32)
            act.activation(tg[:, :], gates_in[:, :], ACT.Tanh).then_inc(sem("tg_ready"), 1)
            act.wait_ge(sem("hcols"), 1)
            schedule(act, ActSteps(act))
            act.wait_ge(sem("router_shift"), 1)
            act.activation(ex[:, :, :], ex[:, :, :], ACT.Exp).then_inc(sem("router_exp"), 1)

            def slots_T(e, prev):
                for h in range(KT):
                    act.wait_ge(sem("slots_tr"), KT * e + h + 1)
                    if prev:
                        act.wait_ge(sem("up_mm"), FT * e)
                    act.activation(bT[:, 0, h, :], g[h][:, :], ACT.Copy).then_inc(sem("slots_T"), 1)

            def expert(e, par, prev, more):
                for f in range(FT):
                    act.wait_ge(sem("up_mm"), FT * e + f + 1)
                    if prev:
                        act.wait_ge(sem("down_mm"), CT * e)
                    for dst in (hidden_hi, hidden_f):
                        ins = act.activation(dst[:, f, :], [p1, p2][f // 2 % 2][f % 2][:, :], ACT.Relu,
                                             bias=b1c[:, bass.ds(e, 1), f:f + 1].rearrange("p e f -> p (e f)"))
                    ins.then_inc(sem("hidden"), 1)
                if more:
                    slots_T(e + 1, True)

            act.wait_ge(ld_late, 16 * 3)
            act.wait_ge(sem("base"), 4)
            slots_T(0, False)
            expert(0, 0, False, True)
            expert(1, 1, True, True)
            with act.Fori(1, E // 2 - 1) as i:
                for par in range(2):
                    expert(2 * i + par, par, True, True)
            expert(E - 2, 0, True, True)
            expert(E - 1, 1, True, False)

        class DveSteps:
            def __init__(self, dve):
                self.dve = dve
                self.chain = Chain(dve, sem("dve_chain"), {"A": 30, "B": 24})

            def enter(self, k, name, i):
                self.chain.enter(name, i)

            def leave(self, name):
                self.chain.leave(name)

            def left(self, k, name, count):
                self.chain.left(name, count)

            def norm_stats(self, w, src, b):
                dve, chain = self.dve, self.chain
                settle(dve, sem("dve_passed"))
                for i in range(TT):
                    chain.mark(dve.bn_stats(stats[:, w, i, :], src[:, bass.ds(TT * b + i, 1), :].rearrange(
                        "p o d -> p (o d)")))

            def norm_var(self, w, who, again=False):
                dve, chain = self.dve, self.chain
                chain.wait()
                settle(dve, sem("dve_passed"))
                for i in range(TT):
                    chain.mark(dve.bn_aggr(mv[:, w, i, :], stats[:, w, i, :]))
                chain.wait()
                ins = dve.tensor_scalar(ve[:, w, :], mv[:, w, :, 1], EPS_LN, None, ALU.add)
                if again:
                    chain.link(ins)
                    chain.link(dve.reciprocal(rec[:, :], ve[:, w, :]))
                    ins = dve.tensor_scalar(ve[:, 2, :], rec[:, :], -EPS_LN, 1.0 + EPS_LN, ALU.mult, ALU.add)
                ins.then_inc(sem(f"{who}_var"), 1)

            def norm_apply(self, w, src, b, dst, ins_b=0):
                for i in range(TT):
                    ins = self.dve.tensor_scalar(dst[:, bass.ds(TT * ins_b + i, 1), :],
                                                 src[:, bass.ds(TT * b + i, 1), :],
                                                 mv[:, w, i, 0:1], rstd[:, w, i:i + 1], ALU.subtract, ALU.mult)
                return ins

            def hi_part(self, j, q):
                wait(self.dve, sem("qk_full"), 2 * j.n + j.order[q] + 1)
                wait(self.dve, sem("split"), 2 * j.n)
                wait(self.dve, sem("parts_out"), 32 * j.n)
                self.dve.tensor_copy(parts[:, 0, q], full[:, q]).then_inc(sem("qk_hi"), 1)

            def early(self, j):
                self.hi_part(j, 1)
                self.v_out(j, G_V)

            def early_end(self, j):
                pass

            def front_start(self, j):
                if j.kind == "X":
                    if isinstance(j.b, int) and j.b == 0:
                        self.dve.wait_ge(sem("cu_ready"), 1)
                    self.dve.tensor_tensor(xt[:, :, :], xo[:, bass.ds(TT * j.b, TT), :], cu[:, :, :], ALU.add
                                           ).then_inc(sem("xo_sum"), 1)

            def front_stats(self, j, k=None):
                dve = self.dve
                if j.kind == "A":
                    if isinstance(j.n, int) and j.n <= 2:
                        dve.wait_ge(ld_x[j.n], 16)
                if j.kind == "X":
                    wait(dve, sem("xo_tanh"), j.b + 1)
                    xs = x[:, bass.ds(TT * j.b, TT), :]
                    self.chain.link(dve.scalar_tensor_tensor(xs, xt[:, :, :], tg[:, 2:3], xs, ALU.mult, ALU.add))
                if j.kind == "S":
                    wait(dve, sem("residual"), k)
                self.norm_stats(1, x, j.b)

            def front_apply(self, j):
                dve, chain = self.dve, self.chain
                wait(dve, sem("front_rstd"), j.n + 1)
                wait(dve, sem("front_tr"), j.n)
                if j.kind != "S":
                    self.norm_apply(1, x, j.b, hN).then_inc(sem("front_h"), 1)
                    return
                chain.mark(self.norm_apply(1, x, j.b, x4, j.b))

            def front_again(self, j):
                dve, chain = self.dve, self.chain
                if j.kind != "S":
                    return
                chain.wait()
                for i in range(TT):
                    ins = dve.scalar_tensor_tensor(hN[:, i, :], x4[:, bass.ds(TT * j.b + i, 1), :].rearrange(
                        "p o d -> p (o d)"), rstd[:, 2, i:i + 1], rows[:, R_G1, :], ALU.mult, ALU.mult)
                ins.then_inc(sem("front_scaled"), 1)

            def tail_src(self, j):
                return x if j.kind == "A" else x4

            def tail_stats(self, j):
                wait(self.dve, sem("residual"), j.n + 1)
                self.norm_stats(0, self.tail_src(j), j.b)
                self.norm_var(0, "tail")

            def tail_apply(self, j):
                dve, chain = self.dve, self.chain
                wait(dve, sem("tail_rstd"), j.tail + 1)
                wait(dve, sem("tail_tr"), j.tail)
                if j.kind != "S":
                    self.norm_apply(0, x, j.b, tN).then_inc(sem("tail_h"), 1)
                    return
                wait(dve, sem("kept"), j.b)
                self.norm_apply(0, x4, j.b, tN).then_inc(sem("tail_norm"), 1)

            def maximum(self, j, u):
                dve = self.dve
                hp, q = u // 2, u % 2
                wait(dve, sem("scores1"), UNITS * j.n + u + 1)
                dve.tensor_reduce(nmax[:, q, 2 * hp:2 * hp + 2], bk(p1[u % 2], 2), AX.X, ALU.max, negate=True
                                  ).then_inc(sem("max"), 1)

            def split_max(self, j):
                dve, chain = self.dve, self.chain
                wait(dve, sem("max"), UNITS * (j.n + 1))
                wait(dve, sem("nmax_tr"), j.n)
                chain.link(dve.tensor_copy(nmaxb[:, :, 0, :], nmax[:, :, :]))
                dve.tensor_tensor(nmaxb[:, :, 1, :], nmax[:, :, :], nmaxb[:, :, 0, :], ALU.subtract
                                  ).then_inc(sem("nmaxb"), 1)

            def normalise(self, j):
                dve, chain = self.dve, self.chain
                wait(dve, sem("on_tr"), j.n)
                for q in range(TT):
                    o = p2[q][:, :].rearrange("p (h c) -> p h c", h=H)
                    wait(dve, sem("o_tr"), 2 * j.n + q + 1)
                    chain.link(dve.reciprocal(rden[:, q, :], o[:, :, DK]))
                    dve.tensor_tensor(on[:, q, :].rearrange("p (h c) -> p h c", h=H), o[:, :, 0:DK],
                                      rden[:, q, :].rearrange("p (h o) -> p h o", o=1).to_broadcast([P, H, DK]),
                                      ALU.mult).then_inc(sem("on"), 1)

            def v_out(self, j, bank_):
                dve = self.dve
                if isinstance(j.n, int) and j.n == 0:
                    dve.wait_ge(ld_rows, 16)
                wait(dve, sem("v_mm"), j.n + 1)
                wait(dve, sem("pv"), 4 * (j.n - 1))
                for q in range(TT):
                    ins = dve.tensor_tensor(
                        vv[:, j.par, q, :, 0:DK], bk(g[bank_], TT)[:, q, :].rearrange("p (h c) -> p h c", h=H),
                        rows[:, ROWS[j.kind][0], :].rearrange("p (h c) -> p h c", h=H), ALU.add)
                ins.then_inc(sem("v_sb"), 1)

            def residual(self, j):
                dve, chain = self.dve, self.chain
                wait(dve, sem("proj_mm"), j.n + 1)
                xs = x[:, bass.ds(TT * j.b, TT), :]
                chain.link(dve.tensor_tensor(res[:, :, :], bk(g[G_OUT], TT),
                                             rows[:, ROWS[j.kind][1], :].rearrange("p (o d) -> p o d", o=1
                                                                                   ).to_broadcast([P, TT, D]), ALU.add))
                if j.kind == "S":
                    x4s = x4[:, bass.ds(TT * j.b, TT), :]
                    dve.tensor_tensor(x4s, res[:, :, :], x4s, ALU.add
                                      ).then_inc(sem("residual"), 1)
                else:
                    w = 0 if j.kind == "A" else 1
                    dve.scalar_tensor_tensor(xs, res[:, :, :], tg[:, w:w + 1], xs, ALU.mult, ALU.add
                                             ).then_inc(sem("residual"), 1)

            def recur(self, j):
                dve, chain = self.dve, self.chain
                wait(dve, sem("gates"), 3 * (j.b + 1))
                chain.mark(dve.scalar_tensor_tensor(gact[:, 0], gact[:, 0], 1.0, cT[:, :, :], ALU.add, ALU.mult))
                chain.link(dve.scalar_tensor_tensor(gact[:, 1], gact[:, 1], 1.0, gact[:, 2], ALU.add, ALU.mult))
                chain.link(dve.tensor_tensor(gact[:, 0], gact[:, 0], gact[:, 1], ALU.add))
                dve.tensor_scalar(cT[:, :, :], gact[:, 0], 0.5, None, ALU.mult).then_inc(sem("c_new"), 1)

            def xo_out(self, j):
                wait(self.dve, sem("tail_mm"), j.tail + 1)
                self.dve.tensor_copy(xo[:, bass.ds(TT * j.b, TT), :], bk(g[G_XO], TT)).then_inc(sem("tail_out"), 1)

            def logits(self, j):
                wait(self.dve, sem("tail_mm"), j.tail + 1)
                self.dve.tensor_copy(lg[:, bass.ds(TT * j.b, TT), :],
                                     g[G_LOGITS][:, 0:TT * E].rearrange("p (a e) -> p a e", a=TT)).then_inc(sem("tail_out"), 1)

            def alone(self, j, nxt):
                self.front_start(j)
                self.front_stats(j)
                self.norm_var(1, "front")
                self.front_apply(j)
                if j.kind == "X":
                    self.norm(nxt)
                for q in range(2):
                    if q == 0 or j.order[0] == 0:
                        self.hi_part(j, q)
                if j.kind == "A":
                    self.v_out(j, G_V)
                    self.norm(nxt)

            def norm(self, j):
                self.front_start(j)
                self.front_stats(j)
                self.norm_var(1, "front")
                self.front_apply(j)

            def step(self, k, front, mid, back, prev, nxt):
                tail = prev if prev and prev.kind != "X" else None
                if front:
                    self.hi_part(front, 0)
                if prev:
                    self.residual(prev)
                for u in range(SLOTS_OF):
                    if front and u == AT_QK[1] + 1:
                        self.hi_part(front, 1)
                    if mid and u >= LAG:
                        self.maximum(mid, u - LAG)
                    if tail and u == AT_TAIL_STATS:
                        self.tail_stats(tail)
                    if tail and u == AT_TAIL_APPLY:
                        self.tail_apply(tail)
                    if tail and tail.kind == "A" and u == AT_RECUR:
                        self.recur(tail)
                    if tail and tail.kind == "A" and u == AT_XO:
                        self.xo_out(tail)
                    if tail and tail.kind == "S" and u == AT_LOGITS:
                        self.logits(tail)
                    if nxt and u == AT_NEXT_SUM:
                        self.front_start(nxt)
                    if nxt and u == AT_NEXT_STATS:
                        self.front_stats(nxt, k)
                    if nxt and u == AT_NEXT_VAR:
                        self.norm_var(1, "front", nxt.kind == "S")
                    if nxt and u == AT_NEXT_APPLY:
                        self.front_apply(nxt)
                    if nxt and u == AT_NEXT_AGAIN:
                        self.front_again(nxt)
                if mid:
                    self.split_max(mid)
                if back:
                    self.normalise(back)
                if front:
                    self.v_out(front, G_V)

            def after(self, j):
                self.residual(j)
                self.tail_stats(j)
                self.tail_apply(j)
                if j.kind == "A":
                    self.recur(j)
                    self.xo_out(j)
                else:
                    self.logits(j)

            def middle(self):
                self.dve.wait_ge(sem("cu_mm"), 1)
                self.dve.tensor_tensor(cu[:, :, :], bk(g[0], TT),
                                       rows[:, R_OF:R_OF + 1, :].to_broadcast([P, TT, D]), ALU.add
                                       ).then_inc(sem("cu_ready"), 1)

        @block.vector
        def _(dve):
            steps = DveSteps(dve)
            chain = steps.chain
            dve.memset(zero[:, :, :], 0.0).then_inc(sem("zero_ready"), 1)
            dve.memset(zeros32[:, :], 0.0)
            dve.memset(vv[:, :, :, :, DK:], 1.0).then_inc(sem("vv_ones"), 1)
            dve.wait_ge(ld_cols, 32)
            for q, c in enumerate((C_F, C_I)):
                dve.tensor_scalar(hcols[:, q, :], cols[:, c, :], 0.5, None, ALU.mult)
            dve.tensor_copy(hcols[:, 2, :], cols[:, C_C, :]).then_inc(sem("hcols"), 1)
            dve.tensor_copy(cT[:, :, :], cols[:, C_IN, :].rearrange("p (k o) -> p k o", o=1
                                                                    ).to_broadcast([P, KT, S])).then_inc(sem("c_new"), 1)
            dve.wait_ge(sem("tg_ready"), 1)
            schedule(dve, steps)

            dve.wait_ge(sem("tail_out"), 2 * B)
            for i in range(NT):
                chain.mark(dve.max(top[:, i, :], lg[:, i, :]))
            chain.wait()
            for i in range(NT):
                chain.mark(dve.max_index(topi[:, i, :], top[:, i, :], lg[:, i, :]))
            chain.wait()
            dve.tensor_tensor(ex[:, :, :], top[:, :, :], top[:, :, 0:1].to_broadcast([P, NT, 8]), ALU.subtract
                              ).then_inc(sem("router_shift"), 1)
            chain.link(dve.tensor_copy(idxf[:, :, :], topi[:, :, 0:2].rearrange("p t w -> p w t")))
            dve.wait_ge(sem("pool_const"), 8)
            for w in range(2):
                dve.tensor_tensor(mask[:, w], iota[:, :].rearrange("p (o e) -> p o e", o=1).to_broadcast([P, NT, E]),
                                  idxf[:, w, :].rearrange("p (t o) -> p t o", o=1).to_broadcast([P, NT, E]),
                                  ALU.is_equal).then_inc(sem("masks"), 1)
            dve.wait_ge(sem("counts"), 2)
            tile_counts = g[1][:, 0:2 * NT * E].rearrange("p (j e) -> p j e", e=E)
            before = g[0][:, 0:2 * NT * E].rearrange("p (j e) -> p j e", e=E)
            for e in range(E):
                chain.mark(dve.tensor_tensor_scan(inc[:, :, e], zeros32[:, :], tile_counts[:, :, e], 0.0,
                                                  ALU.add, ALU.add))
            chain.wait()
            chain.link(dve.tensor_tensor(inc[:, :, :], inc[:, :, :], tile_counts, ALU.subtract))
            chain.link(dve.tensor_tensor(loc[:, :, :], inc[:, :, :], before, ALU.add))
            chain.link(dve.scalar_tensor_tensor(loc[:, :, :], loc[:, :, :], -1.0,
                                                mask[:, :, :, :].rearrange("p w t e -> p (w t) e"), ALU.add, ALU.mult))
            chain.link(dve.tensor_reduce(pos[:, :], loc[:, :, :], AX.X, ALU.add))
            iw = idxf[:, :, :].rearrange("p w t -> p (w t)")
            vw = valid[:, :, :].rearrange("p w t -> p (w t)")
            chain.mark(dve.tensor_scalar(vw, pos[:, :], float(C), None, ALU.is_lt))
            chain.link(dve.tensor_scalar(slotf[:, :], pos[:, :], float(C), float(E * C), ALU.is_ge, ALU.mult))
            chain.link(dve.tensor_tensor(slotf[:, :], slotf[:, :], pos[:, :], ALU.add))
            chain.link(dve.scalar_tensor_tensor(slotf[:, :], iw, float(C), slotf[:, :], ALU.mult, ALU.add))
            dve.tensor_copy(sidx[:, :], slotf[:, :]).then_inc(sem("slots_ready"), 1)
            dve.wait_ge(sem("router_exp"), 1)
            chain.link(dve.tensor_reduce(sums[:, :], ex[:, :, :], AX.X, ALU.add))
            chain.link(dve.reciprocal(sums[:, :], sums[:, :]))
            chain.link(dve.tensor_tensor(prob[:, :, :], ex[:, :, 0:2].rearrange("p t w -> p w t"),
                                         sums[:, :].rearrange("p (o t) -> p o t", o=1).to_broadcast([P, 2, NT]), ALU.mult))
            chain.link(dve.tensor_tensor(prob[:, :, :], prob[:, :, :], valid[:, :, :], ALU.mult))
            chain.link(dve.tensor_tensor(den[:, :], prob[:, 0, :], prob[:, 1, :], ALU.add))
            chain.link(dve.tensor_scalar(den[:, :], den[:, :], EPS_F32, None, ALU.max))
            chain.link(dve.reciprocal(den[:, :], den[:, :]))
            chain.link(dve.tensor_tensor(gate[:, :, :], prob[:, :, :],
                                         den[:, :].rearrange("p (o t) -> p o t", o=1).to_broadcast([P, 2, NT]), ALU.mult))
            dve.tensor_scalar(meta[:, :, 1], gate[:, :, :].rearrange("p w t -> p (w t)"), KEEP, tg[:, 3:4],
                              ALU.mult, ALU.mult).then_inc(sem("gates_ready"), 1)
            for q in range(4):
                s = slice(NT // 4 * q, NT // 4 * (q + 1))
                dve.scalar_tensor_tensor(x4[:, s, :], x4[:, s, :], tg[:, 3:4], x[:, s, :], ALU.mult, ALU.add
                                         ).then_inc(sem("base"), 1)

            def add_b2(e, par, s, prev):
                dve.wait_ge(sem("down_mm"), CT * e + s + 1)
                if prev:
                    dve.wait_ge(sem("y_out"), 16 * CT * (e - 1))
                dve.tensor_tensor(yb[par][:, s:s + 1, :], po[s % 2][:, 0:D].rearrange("p (o d) -> p o d", o=1),
                                  b2r[:, bass.ds(e, 1), :], ALU.add).then_inc(sem("y_sum"), 1)

            def gated(e, par, s):
                gate_ = meta_sb[:, bass.ds(CT * e + s, 1), 1:2].rearrange("p o c -> p (o c)")
                dve.tensor_scalar(yb[par][:, s, :], yb[par][:, s, :], gate_, None, ALU.mult
                                  ).then_inc(sem("y_ready"), 1)

            def w1_hi(e):
                dve.wait_ge(sem("w1_in"), 16 * (e + 1))
                dve.tensor_copy(w1s[:, 0], w1f).then_inc(sem("w1_hi"), 1)

            def w1_lo(e):
                dve.wait_ge(sem("w1_hi"), e + 1)
                dve.tensor_tensor(w1s[:, 1], w1f, w1s[:, 0].bitcast(F32), ALU.subtract
                                  ).then_inc(sem("w1_split"), 1)

            def w2_hi(e):
                dve.wait_ge(sem("w2_in"), 16 * (e + 1))
                dve.tensor_copy(w2s[:, 0], w2f).then_inc(sem("w2_hi"), 1)

            def slots_lo(e):
                for k in range(KT):
                    dve.wait_ge(sem("slots_T"), KT * e + k + 1)
                    dve.tensor_tensor(bT[:, 1, k, :], g[k][:, :], bT[:, 0, k, :].bitcast(F32), ALU.subtract
                                      ).then_inc(sem("slots_lo"), 1)

            def expert(e, par, prev, more):
                for f in range(FT):
                    dve.wait_ge(sem("hidden"), FT * e + f + 1)
                    dve.tensor_tensor(hidden_lo[:, f, :], hidden_f[:, f, :], hidden_hi[:, f, :].bitcast(F32),
                                      ALU.subtract).then_inc(sem("hidden_lo"), 1)
                if more:
                    dve.wait_ge(sem("up_mm"), FT * (e + 1))
                    w1_hi(e + 1)
                    if isinstance(e, int) and e == 0:
                        w1_lo(1)
                    slots_lo(e + 1)
                if isinstance(e, int) and e == 0:
                    for s in range(CT):
                        add_b2(0, 0, s, False)
                    dve.wait_ge(sem("y_sum"), CT)
                    dve.wait_ge(sem("meta_in"), 16)
                    for s in range(CT):
                        gated(0, 0, s)
                else:
                    for s in range(CT):
                        add_b2(e, par, s, prev)
                        dve.wait_ge(sem("y_sum"), CT * e + s + 1)
                        gated(e, par, s)
                if more:
                    w2_hi(e + 1)

            dve.wait_ge(sem("scores2"), UNITS * 3 * B)
            w1_hi(0)
            w1_lo(0)
            w2_hi(0)
            dve.wait_ge(sem("w2_hi"), 1)
            dve.tensor_tensor(w2s[:, 1], w2f, w2s[:, 0].bitcast(F32), ALU.subtract).then_inc(sem("w2_split"), 1)
            dve.wait_ge(sem("b2_in"), 16)
            slots_lo(0)
            expert(0, 0, False, True)
            expert(1, 1, False, True)
            with dve.Fori(1, E // 2 - 1) as i:
                for par in range(2):
                    expert(2 * i + par, par, True, True)
            expert(E - 2, 0, True, True)
            expert(E - 1, 1, True, False)

        class PeSteps:
            def __init__(self, pe):
                self.pe = pe
                self.read = [None, None]

            def enter(self, k, name, i):
                self.read = [(sem("v_sb"), k + 2), None]

            def leave(self, name):
                pass

            def left(self, k, name, count):
                self.read = [(sem("v_sb"), k + 2), None]

            def claim(self, i, reader, value):
                if self.read[i]:
                    wait(self.pe, *self.read[i])
                self.read[i] = (sem(reader), value)
                return g[i]

            def project(self, bank_, w, moving, cols_=None):
                for m in range(KT):
                    for k in range(KT):
                        ins = self.pe.matmul(bk(bank_, KT)[:, m, :], weights[:, w, k, P * m:P * (m + 1)],
                                             moving[:, k, :], start=k == 0, stop=k == KT - 1)
                return ins

            def project_rows(self, bank_, w, still):
                for q in range(TT):
                    for k in range(KT):
                        ins = self.pe.matmul(bk(bank_, TT)[:, q, :], still[:, k, P * q:P * (q + 1)],
                                             weights[:, w, k, :], start=k == 0, stop=k == KT - 1)
                return ins

            def transpose_rows(self, bank_, src):
                for q in range(TT):
                    for k in range(KT):
                        ins = self.pe.transpose(bk(bank_, KT)[:, k, P * q:P * (q + 1)],
                                                src[:, q, P * k:P * (k + 1)], ident[:, :])
                return ins

            def front_T(self, j):
                wait(self.pe, sem("front_h"), j.n + 1)
                self.transpose_rows(self.claim(G_FRONT, "front_hT", j.n + 1), hN).then_inc(sem("front_tr"), 1)

            def qk(self, j, q):
                pe = self.pe
                if j.kind != "S" and q == 1:
                    wait(pe, sem("context_in"), 16 * (j.load + 1))
                if q == 0:
                    wait(pe, sem("front_hT"), j.n + 1)
                src = hT if q == 0 or j.kind == "S" else ctxT
                b_ = self.claim(G_QK, "qk_full", 2 * j.n + j.order[q] + 1)
                self.project(b_, WEIGHTS[j.kind][q], src).then_inc(sem("qk_mm"), 1)

            def v(self, j):
                if isinstance(j.n, int) and j.n == 0:
                    self.pe.wait_ge(ld_vo, 16)
                b_ = self.claim(G_V, "v_sb", j.n + 1)
                src = hT if j.kind == "S" else ctxT
                self.project_rows(b_, WEIGHTS[j.kind][2], src).then_inc(sem("v_mm"), 1)

            def scores1(self, j, u):
                pe = self.pe
                if u == 0:
                    wait(pe, sem("stacked"), 16 * 2 * len(RUNS) * (j.n + 1))
                wait(pe, sem("max"), UNITS * j.n + u - 1)
                hp, q = u // 2, u % 2
                for a in range(2):
                    h = 2 * hp + a
                    ins = pe.matmul(bk(p1[u % 2], 2)[:, a, :], qs[0:KROWS, j.par, h, P * q:P * (q + 1)],
                                    ks[0:KROWS, j.par, h, :], start=True, stop=True)
                ins.then_inc(sem("scores1"), 1)

            def scores2(self, j, u):
                pe = self.pe
                if u == 0:
                    wait(pe, sem("nmax_in"), 16 * MROWS * (j.n + 1))
                wait(pe, sem("exp"), UNITS * j.n + u - 1)
                hp, kt = u // 2, u % 2
                for a in range(2):
                    h = 2 * hp + a
                    ins = pe.matmul(bk(p2[u % 2], 2)[:, a, :], ks[0:KROWS + MROWS, j.par, h, P * kt:P * (kt + 1)],
                                    qs[0:KROWS + MROWS, j.par, h, :], start=True, stop=True)
                ins.then_inc(sem("scores2"), 1)

            def pv(self, j, q):
                pe = self.pe
                if q == 0:
                    wait(pe, sem("v_sb"), j.n + 1)
                wait(pe, sem("exp"), UNITS * j.n + 4 * (q + 1))
                wait(pe, sem("o_sb"), 4 * j.n + q - 1)
                for kt in range(TT):
                    for a in range(4):
                        u = 4 * q + 2 * (a // 2) + kt
                        ins = pe.matmul(po[q % 2][32 * a:32 * a + 32, 0:S], vv[:, j.par, kt, 4 * q + a, :],
                                        ring[:, u % RING, a % 2, :], start=kt == 0, stop=kt == TT - 1,
                                        skip_group_check=True)
                ins.then_inc(sem("pv"), 1)

            def nmax_T(self, j):
                pe = self.pe
                if isinstance(j.n, int) and j.n == 0:
                    pe.wait_ge(sem("pool_const"), 8)
                    pe.wait_ge(sem("vv_ones"), 1)
                wait(pe, sem("nmaxb"), j.n + 1)
                b_ = p1[0]
                for q in range(TT):
                    ins = pe.transpose(b_[0:32, 0:P].bitcast(BF16)[:, P * q:P * (q + 1)],
                                       nmaxb[:, q].rearrange("p r h -> p (r h)"), identb[:, :])
                ins.then_inc(sem("nmax_tr"), 1)

            def o_T(self, j):
                pe = self.pe
                wait(pe, sem("o_sb"), 4 * (j.n + 1))
                for q in range(TT):
                    b_ = p2[q]
                    for a in range(4):
                        ins = pe.transpose(b_[:, P * a:P * (a + 1)], os_[:, a, P * q:P * (q + 1)], ident[:, :])
                    ins.then_inc(sem("o_tr"), 1)

            def on_T(self, j):
                wait(self.pe, sem("on"), 2 * (j.n + 1))
                self.transpose_rows(p1[1], on).then_inc(sem("on_tr"), 1)

            def out_proj(self, j):
                wait(self.pe, sem("ot_sb"), j.n + 1)
                self.project_rows(self.claim(G_OUT, "residual", j.n + 1), WEIGHTS[j.kind][3], ot
                                  ).then_inc(sem("proj_mm"), 1)

            def tail_T(self, j):
                if isinstance(j.tail, int) and j.tail == 0:
                    self.pe.wait_ge(ld_gates, 16)
                wait(self.pe, sem("tail_h"), j.tail + 1)
                src = tN if j.kind == "A" else tS
                self.transpose_rows(self.claim(G_TAIL, "tail_hT", j.tail + 1), src).then_inc(sem("tail_tr"), 1)

            def recur(self, j, q):
                pe = self.pe
                if q == 0:
                    wait(pe, sem("tail_hT"), j.tail + 1)
                    wait(pe, sem("c_new"), j.b + 1)
                b_ = self.claim(G_GATES[q], "gates", 3 * j.b + q + 1)
                self.gate_part(b_, W_F + 2 * q, tT, True, False)
                self.gate_part(b_, W_UF + 2 * q, cT, False, True).then_inc(sem("gates_mm"), 1)

            def gate_part(self, b_, w, src, first, last):
                for m in range(KT):
                    for k in range(KT):
                        ins = self.pe.matmul(bk(b_, KT)[:, m, :], weights[:, w, k, P * m:P * (m + 1)], src[:, k, :],
                                             start=first and m + k == 0, stop=last and m + k == 2 * KT - 2,
                                             skip_group_check=True)
                return ins

            def xo(self, j):
                self.project_rows(self.claim(G_XO, "tail_out", j.tail + 1), W_OX, tT).then_inc(sem("tail_mm"), 1)

            def logits(self, j):
                pe = self.pe
                wait(pe, sem("tail_hT"), j.tail + 1)
                b_ = self.claim(G_LOGITS, "tail_out", j.tail + 1)
                for q in range(TT):
                    for k in range(KT):
                        ins = pe.matmul(b_[:, E * q:E * (q + 1)], tT[:, k, P * q:P * (q + 1)], wr[:, k, :],
                                        start=k == 0, stop=k == KT - 1)
                ins.then_inc(sem("tail_mm"), 1)

            def alone(self, j, nxt):
                self.front_T(j)
                self.qk(j, 0)
                if j.order[0] == 0:
                    self.qk(j, 1)
                    self.v(j)

            def early(self, j):
                self.pe.wait_ge(ld_late, 16 * 3)
                self.qk(j, 1)
                self.v(j)

            def early_end(self, j):
                pass

            def step(self, k, front, mid, back, prev, nxt):
                tail = prev if prev and prev.kind != "X" else None
                if front:
                    self.front_T(front)
                if prev:
                    self.on_T(prev)
                if front:
                    self.qk(front, 0)
                if prev:
                    self.out_proj(prev)
                for u in range(SLOTS_OF):
                    if back and u < UNITS:
                        self.scores2(back, u)
                    if mid and u >= LAG:
                        self.scores1(mid, u - LAG)
                    if front and u == AT_QK[1]:
                        self.qk(front, 1)
                    if tail and u == AT_TAIL_T[tail.kind]:
                        self.tail_T(tail)
                    if tail and tail.kind == "A" and u in AT_GATES:
                        self.recur(tail, AT_GATES.index(u))
                    if tail and tail.kind == "A" and u == AT_XO:
                        self.xo(tail)
                    if tail and tail.kind == "S" and u == AT_LOGITS:
                        self.logits(tail)
                    if back and u in AT_PV:
                        self.pv(back, AT_PV.index(u))
                if back:
                    self.o_T(back)
                if front:
                    self.v(front)
                    if self.read[1 - G_V]:
                        wait(self.pe, *self.read[1 - G_V])
                        self.read[1 - G_V] = None
                if mid:
                    self.nmax_T(mid)

            def after(self, j):
                self.on_T(j)
                self.out_proj(j)
                if j.kind == "A":
                    wait(self.pe, sem("c_new"), j.b + 1)
                    banks = (self.claim(0, "gates", 3 * j.b + 1), p1[0], p1[1])
                    for q in range(2):
                        self.gate_part(banks[q], W_UF + 2 * q, cT, True, False)
                    self.tail_T(j)
                    self.gate_part(banks[2], W_UF + 4, cT, True, False)
                    wait(self.pe, sem("tail_hT"), j.tail + 1)
                    for q in range(3):
                        self.gate_part(banks[q], W_F + 2 * q, tT, False, True).then_inc(sem("gates_mm"), 1)
                    self.xo(j)
                else:
                    self.tail_T(j)
                    self.logits(j)

            def middle(self):
                wait(self.pe, sem("c_new"), B + 1)
                self.project_rows(self.claim(0, "cu_ready", 1), W_UO, cT).then_inc(sem("cu_mm"), 1)

        @block.tensor
        def _(pe):
            pe.wait_ge(sem("pool_const"), 2)
            pe.wait_ge(ld_qk, 16)
            steps = PeSteps(pe)
            schedule(pe, steps)

            pe.wait_ge(sem("masks"), 2)
            mk = mask[:, :, :, :].rearrange("p w t e -> p (w t e)")
            for i, still in enumerate((tri, ones)):
                b_ = steps.claim(i, "slots_ready", 1)
                pe.matmul(b_[:, 0:2 * NT * E], still[:, :], mk, start=True, stop=True).then_inc(sem("counts"), 1)
            pe.wait_ge(sem("slots_ready"), 1)

            def slots_T(e, par, prev, loads):
                pe.wait_ge(sem(f"slots_in{par}"), 16 * (loads + 1))
                if prev:
                    pe.wait_ge(sem("slots_lo"), KT * e)
                for k in range(KT):
                    for s in range(CT):
                        ins = pe.transpose(g[k][:, P * s:P * (s + 1)], br[par][:, s, P * k:P * (k + 1)], ident[:, :])
                    ins.then_inc(sem("slots_tr"), 1)

            def expert(e, par, prev, loads, more):
                pe.wait_ge(sem("w1_split"), e + 1)
                pe.wait_ge(sem("slots_lo"), KT * (e + 1))
                passes = ((0, 0), (0, 1), (1, 0))
                for f in range(FT):
                    if prev or f >= 4:
                        pe.wait_ge(sem("hidden"), FT * e + f - 3)
                    for k in range(KT):
                        for i, (a, b) in enumerate(passes):
                            ins = pe.matmul([p1, p2][f // 2 % 2][f % 2][:, :], w1s[:, a, k, P * f:P * (f + 1)],
                                            bT[:, b, k, :], start=k + i == 0, stop=k == KT - 1 and i == 2)
                    ins.then_inc(sem("up_mm"), 1)
                if more:
                    slots_T(e + 1, 1 - par, True, loads + par)
                pe.wait_ge(sem("w2_split"), e + 1)
                for s in range(CT):
                    if prev or s >= 2:
                        pe.wait_ge(sem("y_sum"), CT * e + s - 1)
                    for f in range(FT):
                        if s == 0:
                            pe.wait_ge(sem("hidden_lo"), FT * e + f + 1)
                        for i, (a, b) in enumerate(passes):
                            hidden_ = (hidden_hi, hidden_lo)[a]
                            ins = pe.matmul(po[s % 2][:, 0:D], hidden_[:, f, P * s:P * (s + 1)], w2s[:, b, f, :],
                                            start=f + i == 0, stop=f == FT - 1 and i == 2)
                    ins.then_inc(sem("down_mm"), 1)

            slots_T(0, 0, False, 0)
            expert(0, 0, False, 0, True)
            expert(1, 1, True, 0, True)
            with pe.Fori(1, E // 2 - 1) as i:
                for par in range(2):
                    expert(2 * i + par, par, True, i, True)
            expert(E - 2, 0, True, E // 2 - 1, True)
            expert(E - 1, 1, True, E // 2 - 1, False)


INS = ["x", "ctxT", "weights", "cols", "rows", "gates", "b1", "wr", "w1", "w2", "b2"]


def kernel(x, ctx_1024, g_xattn, g_ffn, **p):
    import numpy as np
    import concourse.bacc as bacc
    from concourse.bass_utils import run_bass_kernel_spmd

    a = {k: np.asarray(v) for k, v in p.items()}
    weights = [a["L0_xattn_Wq"].T, a["L0_xattn_Wk"].T, a["L0_xattn_Wv"].T, a["L0_xattn_Wo"].T]
    for gate in "fic":
        weights += [a[f"L0_ffn_w{gate}"].T, a[f"L0_ffn_u{gate}"].T]
    weights += [a["L0_ffn_wo"].T, a["L0_ffn_uo"].T]
    weights += [a[f"L1_xattn_W{w}"] for w in "qkvo"] + [a[f"L1_ffn_w{w}"] for w in "qkvo"]
    order = np.arange(D).reshape(H // KT, KT, DK).transpose(1, 2, 0).ravel()
    for w in (W_Q0, W_K0, W_Q1, W_K1, W_QS, W_KS):
        weights[w] = weights[w][:, order]
    cols = [a[n] for n in ("L0_xattn_bq", "L0_xattn_bk", "L0_ffn_bf", "L0_ffn_bi", "L0_ffn_bc", "L0_ffn_in_c",
                           "L1_xattn_bq", "L1_xattn_bk", "L1_ffn_bq", "L1_ffn_bk")]
    for c in (C_Q0, C_K0, C_Q1, C_K1, C_QS, C_KS):
        cols[c] = cols[c][order]
    rows = [a[n] for n in ("L0_xattn_bv", "L0_xattn_bo", "L0_ffn_bo", "L1_xattn_bv", "L1_xattn_bo", "L1_ffn_bv",
                           "L1_ffn_bo", "L1_ffn_ln1_g", "L1_ffn_ln1_b", "L1_ffn_ln2_g", "L1_ffn_ln2_b")]
    given = {
        "x": np.asarray(x),
        "ctxT": np.asarray(ctx_1024)[[*range(B), 0]].transpose(0, 2, 1),
        "weights": np.stack(weights),
        "cols": np.stack(cols).reshape(10 * KT, P).T,
        "rows": np.stack(rows),
        "b2": a["L1_ffn_b2"],
        "gates": np.concatenate([np.asarray(g_xattn), np.asarray(g_ffn)]),
        "b1": a["L1_ffn_b1"].reshape(E * FT, P).T,
        "wr": a["L1_ffn_wr"],
        "w1": a["L1_ffn_w1"],
        "w2": a["L1_ffn_w2"],
    }
    nc = bacc.Bacc("TRN2", target_bir_lowering=False, num_devices=1)
    arrays, t = {}, {}
    for name in INS:
        arr = np.ascontiguousarray(given[name])
        arrays[f"in_{name}"] = arr
        t[name] = nc.dram_tensor(f"in_{name}", arr.shape, mybir.dt.from_np(arr.dtype), kind="ExternalInput").ap()
    t["out"] = nc.dram_tensor("out_x", (B * S + C, D), F32, kind="ExternalOutput").ap()
    flamingo(nc, t)
    return run_bass_kernel_spmd(nc, [arrays], core_ids=[0]).results[0]["out_x"][:B * S].reshape(B, S, D)
```
